# Optimizing a Trainium2 kernel written in Bass

```python
import numpy as np
import jax
import jax.numpy as jnp

def _softmax(x, axis=-1):
    return jax.nn.softmax(x, axis=axis)

def _gelu(x):
    return jax.nn.gelu(x, approximate=True)

def _silu(x):
    return jax.nn.silu(x)

def _sigmoid(x):
    return jax.nn.sigmoid(x)

def _layernorm(x, axis=-1, eps=1e-05):
    m = jnp.mean(x, axis=axis, keepdims=True)
    v = jnp.var(x, axis=axis, keepdims=True)
    return (x - m) / jnp.sqrt(v + eps)

def _scatter_add(tgt, idx, src, axis=0):
    return tgt.at[idx].add(src)

def _segment_sum(src, seg, n):
    return jax.ops.segment_sum(src, seg, n)
kernel_name = 'mk_hybrid_d1_jaxref_r8_10a8ef'

def setup_inputs(seed: int=0):
    np.random.seed(seed)
    _w = jnp.asarray

    def _L0_attn_a_setup():
        import jax, jax.numpy as jnp
        import numpy as np
        N_HEAD = 16
        N_LANDMARKS = 64
        N_ITER = 6

        def _landmarks(t, nL):
            B, nh, T, hs = t.shape
            return t.reshape(B, nh, nL, T // nL, hs).mean(axis=3)

        def _iterative_inv(K, n_iter=N_ITER):
            I = jnp.eye(K.shape[-1], dtype=K.dtype)
            denom = jnp.max(jnp.sum(K, axis=-2), axis=-1)[..., None, None]
            V = K.swapaxes(-1, -2) / denom
            for _ in range(n_iter):
                KV = K @ V
                V = 0.25 * V @ (13.0 * I - KV @ (15.0 * I - KV @ (7.0 * I - KV)))
            return V
        key = jax.random.key(seed)
        k1, k2, k3 = jax.random.split(key, 3)
        B, T, C = (4, 512, 128)
        x = jax.random.normal(k1, (B, T, C), dtype=jnp.float32)
        W_attn = jax.random.normal(k2, (C, 3 * C), dtype=jnp.float32) * (1.0 / np.sqrt(C))
        W_proj = jax.random.normal(k3, (C, C), dtype=jnp.float32) * (1.0 / np.sqrt(C))
        return {'x': x, 'W_attn': W_attn, 'W_proj': W_proj}
    _L0_attn_a_in = _L0_attn_a_setup()

    def _L0_attn_b_setup():
        import jax, jax.numpy as jnp
        import numpy as np
        B, T, D = (2, 256, 128)
        H = 8
        KD = 128
        VD = 32
        KEY_DIM = H * KD
        VAL_DIM = H * VD
        KS = 4
        EPS_NORM = 1e-06
        EPS_RMS = 1e-05

        def _xavier(key, shape):
            fan_in, fan_out = (shape[0], shape[1])
            lim = np.sqrt(6.0 / (fan_in + fan_out))
            return jax.random.uniform(key, shape, jnp.float32, -lim, lim)

        def _causal_dw_conv_silu(x, w):
            C = x.shape[-1]
            y = jax.lax.conv_general_dilated(jnp.swapaxes(x, 1, 2), w[:, None, :], window_strides=(1,), padding=[(KS - 1, 0)], feature_group_count=C)
            return jax.nn.silu(jnp.swapaxes(y, 1, 2))

        def _l2norm(x):
            n = jnp.sqrt(jnp.sum(x * x, axis=-1, keepdims=True))
            return x / jnp.maximum(n, EPS_NORM)

        def _gdn_forward(x, Wq, Wk, Wv, Wa, Wb, Wg, Wo, A_log, dt_bias, conv_q, conv_k, conv_v, o_norm_w):
            bsz, seq_len, _ = x.shape
            beta = jax.nn.sigmoid(x @ Wb) * 2.0
            g = -jnp.exp(A_log)[None, None, :] * jax.nn.softplus(x @ Wa + dt_bias[None, None, :])
            alpha = jnp.exp(g)
            q = _causal_dw_conv_silu(x @ Wq, conv_q).reshape(bsz, seq_len, H, KD)
            k = _causal_dw_conv_silu(x @ Wk, conv_k).reshape(bsz, seq_len, H, KD)
            v = _causal_dw_conv_silu(x @ Wv, conv_v).reshape(bsz, seq_len, H, VD)
            q = _l2norm(q)
            k = _l2norm(k)
            qT = jnp.swapaxes(q, 0, 1)
            kT = jnp.swapaxes(k, 0, 1)
            vT = jnp.swapaxes(v, 0, 1)
            aT = jnp.swapaxes(alpha, 0, 1)
            bT = jnp.swapaxes(beta, 0, 1)

            def step(state, inp):
                q_t, k_t, v_t, a_t, b_t = inp
                retained = jnp.einsum('bhvk,bhk->bhv', state, k_t)
                a4 = a_t[..., None, None]
                b4 = b_t[..., None, None]
                rk = retained[..., None] * k_t[:, :, None, :]
                vk = v_t[..., None] * k_t[:, :, None, :]
                state = a4 * (state - b4 * rk) + b4 * vk
                o_t = jnp.einsum('bhvk,bhk->bhv', state, q_t)
                return (state, o_t)
            state0 = jnp.zeros((bsz, H, VD, KD), jnp.float32)
            _, outT = jax.lax.scan(step, state0, (qT, kT, vT, aT, bT))
            out = jnp.swapaxes(outT, 0, 1)
            gate = (x @ Wg).reshape(bsz, seq_len, H, VD)
            rms = jax.lax.rsqrt(jnp.mean(out * out, axis=-1, keepdims=True) + EPS_RMS)
            out = out * rms * o_norm_w * jax.nn.silu(gate)
            out = out.reshape(bsz, seq_len, VAL_DIM)
            return out @ Wo
        key = jax.random.key(seed)
        ks = jax.random.split(key, 16)
        x = jax.random.normal(ks[0], (B, T, D), jnp.float32)
        Wq = _xavier(ks[1], (D, KEY_DIM))
        Wk = _xavier(ks[2], (D, KEY_DIM))
        Wv = _xavier(ks[3], (D, VAL_DIM))
        Wa = _xavier(ks[4], (D, H))
        Wb = _xavier(ks[5], (D, H))
        Wg = _xavier(ks[6], (D, VAL_DIM))
        Wo = _xavier(ks[7], (VAL_DIM, D))
        A_log = jnp.log(jax.random.uniform(ks[8], (H,), jnp.float32, 0.5, 16.0))
        dt = jnp.exp(jax.random.uniform(ks[9], (H,), jnp.float32, np.log(0.001), np.log(0.1)))
        dt = jnp.clip(dt, 0.0001, None)
        dt_bias = dt + jnp.log(-jnp.expm1(-dt))

        def conv_w(k, c):
            lim = np.sqrt(6.0 / (1 + KS))
            return jax.random.uniform(k, (c, KS), jnp.float32, -lim, lim)
        conv_q = conv_w(ks[10], KEY_DIM)
        conv_k = conv_w(ks[11], KEY_DIM)
        conv_v = conv_w(ks[12], VAL_DIM)
        o_norm_w = jnp.ones((VD,), jnp.float32)
        return dict(x=x, Wq=Wq, Wk=Wk, Wv=Wv, Wa=Wa, Wb=Wb, Wg=Wg, Wo=Wo, A_log=A_log, dt_bias=dt_bias, conv_q=conv_q, conv_k=conv_k, conv_v=conv_v, o_norm_w=o_norm_w)
    _L0_attn_b_in = _L0_attn_b_setup()

    def _L0_ffn_setup():
        import jax, jax.numpy as jnp
        import numpy as np
        D_MODEL = 128
        HIDDEN = 512
        NUM_EXPERTS = 8
        TOP_K = 2
        DEPTH = 12
        DEPTH_SCALE = 1.0 / np.sqrt(DEPTH)
        key = jax.random.key(seed)
        k_x, k_r, k_g, k_u, k_d = jax.random.split(key, 5)
        s_in = 1.0 / np.sqrt(D_MODEL)
        s_hid = 1.0 / np.sqrt(HIDDEN)
        return {'x': jax.random.normal(k_x, (2, 256, D_MODEL), dtype=jnp.float32), 'Wr': jax.random.normal(k_r, (D_MODEL, NUM_EXPERTS), dtype=jnp.float32) * s_in, 'Wg': jax.random.normal(k_g, (NUM_EXPERTS, D_MODEL, HIDDEN), dtype=jnp.float32) * s_in, 'Wu': jax.random.normal(k_u, (NUM_EXPERTS, D_MODEL, HIDDEN), dtype=jnp.float32) * s_in, 'Wd': jax.random.normal(k_d, (NUM_EXPERTS, HIDDEN, D_MODEL), dtype=jnp.float32) * s_hid}
    _L0_ffn_in = _L0_ffn_setup()
    _d = {'L0_attn_a_x': _L0_attn_a_in['x'], 'L0_attn_a_W_attn': _L0_attn_a_in['W_attn'], 'L0_attn_a_W_proj': _L0_attn_a_in['W_proj'], 'L0_attn_b_Wq': _L0_attn_b_in['Wq'], 'L0_attn_b_Wk': _L0_attn_b_in['Wk'], 'L0_attn_b_Wv': _L0_attn_b_in['Wv'], 'L0_attn_b_Wa': _L0_attn_b_in['Wa'], 'L0_attn_b_Wb': _L0_attn_b_in['Wb'], 'L0_attn_b_Wg': _L0_attn_b_in['Wg'], 'L0_attn_b_Wo': _L0_attn_b_in['Wo'], 'L0_attn_b_A_log': _L0_attn_b_in['A_log'], 'L0_attn_b_dt_bias': _L0_attn_b_in['dt_bias'], 'L0_attn_b_conv_q': _L0_attn_b_in['conv_q'], 'L0_attn_b_conv_k': _L0_attn_b_in['conv_k'], 'L0_attn_b_conv_v': _L0_attn_b_in['conv_v'], 'L0_attn_b_o_norm_w': _L0_attn_b_in['o_norm_w'], 'L0_ffn_Wr': _L0_ffn_in['Wr'], 'L0_ffn_Wg': _L0_ffn_in['Wg'], 'L0_ffn_Wu': _L0_ffn_in['Wu'], 'L0_ffn_Wd': _L0_ffn_in['Wd']}
    _x0 = _d['L0_attn_a_x']
    _d['L0_attn_a_x'] = jax.random.normal(jax.random.fold_in(jax.random.key(seed), 1), (4, 1024, 128), dtype=_x0.dtype)
    del _x0
    return _d

def reference(L0_attn_a_x, L0_attn_a_W_attn, L0_attn_a_W_proj, L0_attn_b_Wq, L0_attn_b_Wk, L0_attn_b_Wv, L0_attn_b_Wa, L0_attn_b_Wb, L0_attn_b_Wg, L0_attn_b_Wo, L0_attn_b_A_log, L0_attn_b_dt_bias, L0_attn_b_conv_q, L0_attn_b_conv_k, L0_attn_b_conv_v, L0_attn_b_o_norm_w, L0_ffn_Wr, L0_ffn_Wg, L0_ffn_Wu, L0_ffn_Wd):

    def _L0_attn_a_ref(x, W_attn, W_proj):
        import jax, jax.numpy as jnp
        import numpy as np
        N_HEAD = 16
        N_LANDMARKS = 64
        N_ITER = 6

        def _landmarks(t, nL):
            B, nh, T, hs = t.shape
            return t.reshape(B, nh, nL, T // nL, hs).mean(axis=3)

        def _iterative_inv(K, n_iter=N_ITER):
            I = jnp.eye(K.shape[-1], dtype=K.dtype)
            denom = jnp.max(jnp.sum(K, axis=-2), axis=-1)[..., None, None]
            V = K.swapaxes(-1, -2) / denom
            for _ in range(n_iter):
                KV = K @ V
                V = 0.25 * V @ (13.0 * I - KV @ (15.0 * I - KV @ (7.0 * I - KV)))
            return V
        B, T, C = x.shape
        nh, nL = (N_HEAD, N_LANDMARKS)
        hs = C // nh
        qkv = x @ W_attn
        q, k, v = jnp.split(qkv, 3, axis=-1)

        def heads(t):
            return t.reshape(B, T, nh, hs).transpose(0, 2, 1, 3)
        q, k, v = (heads(q), heads(k), heads(v))
        q_l = _landmarks(q, nL)
        k_l = _landmarks(k, nL)
        L = jax.nn.softmax(jnp.einsum('bhtd,bhld->bhtl', q, k_l), axis=-1)
        P = _iterative_inv(jax.nn.softmax(jnp.einsum('bhld,bhmd->bhlm', q_l, k_l), axis=-1))
        N = jax.nn.softmax(jnp.einsum('bhld,bhtd->bhlt', q_l, k), axis=-1)
        y = L @ (P @ (N @ v))
        y = y.transpose(0, 2, 1, 3).reshape(B, T, C)
        return y @ W_proj

    def _L0_attn_b_ref(x, Wq, Wk, Wv, Wa, Wb, Wg, Wo, A_log, dt_bias, conv_q, conv_k, conv_v, o_norm_w):
        import jax, jax.numpy as jnp
        import numpy as np
        B, T, D = (2, 256, 128)
        H = 8
        KD = 128
        VD = 32
        KEY_DIM = H * KD
        VAL_DIM = H * VD
        KS = 4
        EPS_NORM = 1e-06
        EPS_RMS = 1e-05

        def _xavier(key, shape):
            fan_in, fan_out = (shape[0], shape[1])
            lim = np.sqrt(6.0 / (fan_in + fan_out))
            return jax.random.uniform(key, shape, jnp.float32, -lim, lim)

        def _causal_dw_conv_silu(x, w):
            C = x.shape[-1]
            y = jax.lax.conv_general_dilated(jnp.swapaxes(x, 1, 2), w[:, None, :], window_strides=(1,), padding=[(KS - 1, 0)], feature_group_count=C)
            return jax.nn.silu(jnp.swapaxes(y, 1, 2))

        def _l2norm(x):
            n = jnp.sqrt(jnp.sum(x * x, axis=-1, keepdims=True))
            return x / jnp.maximum(n, EPS_NORM)

        def _gdn_forward(x, Wq, Wk, Wv, Wa, Wb, Wg, Wo, A_log, dt_bias, conv_q, conv_k, conv_v, o_norm_w):
            bsz, seq_len, _ = x.shape
            beta = jax.nn.sigmoid(x @ Wb) * 2.0
            g = -jnp.exp(A_log)[None, None, :] * jax.nn.softplus(x @ Wa + dt_bias[None, None, :])
            alpha = jnp.exp(g)
            q = _causal_dw_conv_silu(x @ Wq, conv_q).reshape(bsz, seq_len, H, KD)
            k = _causal_dw_conv_silu(x @ Wk, conv_k).reshape(bsz, seq_len, H, KD)
            v = _causal_dw_conv_silu(x @ Wv, conv_v).reshape(bsz, seq_len, H, VD)
            q = _l2norm(q)
            k = _l2norm(k)
            qT = jnp.swapaxes(q, 0, 1)
            kT = jnp.swapaxes(k, 0, 1)
            vT = jnp.swapaxes(v, 0, 1)
            aT = jnp.swapaxes(alpha, 0, 1)
            bT = jnp.swapaxes(beta, 0, 1)

            def step(state, inp):
                q_t, k_t, v_t, a_t, b_t = inp
                retained = jnp.einsum('bhvk,bhk->bhv', state, k_t)
                a4 = a_t[..., None, None]
                b4 = b_t[..., None, None]
                rk = retained[..., None] * k_t[:, :, None, :]
                vk = v_t[..., None] * k_t[:, :, None, :]
                state = a4 * (state - b4 * rk) + b4 * vk
                o_t = jnp.einsum('bhvk,bhk->bhv', state, q_t)
                return (state, o_t)
            state0 = jnp.zeros((bsz, H, VD, KD), jnp.float32)
            _, outT = jax.lax.scan(step, state0, (qT, kT, vT, aT, bT))
            out = jnp.swapaxes(outT, 0, 1)
            gate = (x @ Wg).reshape(bsz, seq_len, H, VD)
            rms = jax.lax.rsqrt(jnp.mean(out * out, axis=-1, keepdims=True) + EPS_RMS)
            out = out * rms * o_norm_w * jax.nn.silu(gate)
            out = out.reshape(bsz, seq_len, VAL_DIM)
            return out @ Wo
        return _gdn_forward(x, Wq, Wk, Wv, Wa, Wb, Wg, Wo, A_log, dt_bias, conv_q, conv_k, conv_v, o_norm_w)

    def _L0_ffn_ref(x, Wr, Wg, Wu, Wd):
        import jax, jax.numpy as jnp
        import numpy as np
        D_MODEL = 128
        HIDDEN = 512
        NUM_EXPERTS = 8
        TOP_K = 2
        DEPTH = 12
        DEPTH_SCALE = 1.0 / np.sqrt(DEPTH)
        B, T, C = x.shape
        flat_x = x.reshape(-1, C)
        logits = flat_x @ Wr
        top_vals, top_idx = jax.lax.top_k(logits, TOP_K)
        rw = jax.nn.softmax(top_vals.astype(jnp.float32), axis=-1).astype(x.dtype)
        combine = jnp.sum(rw[..., None] * jax.nn.one_hot(top_idx, NUM_EXPERTS, dtype=x.dtype), axis=1)
        g = jnp.einsum('nc,ech->neh', flat_x, Wg)
        u = jnp.einsum('nc,ech->neh', flat_x, Wu)
        h = jax.nn.silu(g) * u
        eo = jnp.einsum('neh,ehc->nec', h, Wd) * DEPTH_SCALE
        out = jnp.einsum('ne,nec->nc', combine, eo)
        return out.reshape(B, T, C)
    x = L0_attn_a_x
    x = x + _L0_attn_a_ref(_layernorm(x, axis=-1), L0_attn_a_W_attn, L0_attn_a_W_proj)
    x = x + _L0_ffn_ref(_layernorm(x, axis=-1), L0_ffn_Wr, L0_ffn_Wg, L0_ffn_Wu, L0_ffn_Wd)
    x = x + _L0_attn_b_ref(_layernorm(x, axis=-1), L0_attn_b_Wq, L0_attn_b_Wk, L0_attn_b_Wv, L0_attn_b_Wa, L0_attn_b_Wb, L0_attn_b_Wg, L0_attn_b_Wo, L0_attn_b_A_log, L0_attn_b_dt_bias, L0_attn_b_conv_q, L0_attn_b_conv_k, L0_attn_b_conv_v, L0_attn_b_o_norm_w)
    x = x + _L0_ffn_ref(_layernorm(x, axis=-1), L0_ffn_Wr, L0_ffn_Wg, L0_ffn_Wu, L0_ffn_Wd)
    return x

_drawn_inputs = setup_inputs


def setup_inputs(seed=0):
    import zlib

    import numpy as np

    out = dict(_drawn_inputs(seed))
    spreads = {'L0_attn_b_o_norm_w': (1.0, 0.2)}
    factors = {}
    for name, (base, spread) in spreads.items():
        noise = np.random.default_rng([zlib.crc32(name.encode()), seed]).standard_normal(out[name].shape)
        drawn = base * np.exp(spread * noise) if base else spread * noise
        out[name] = jnp.asarray(drawn.astype(out[name].dtype))
    for name, factor in factors.items():
        out[name] = (out[name] * factor).astype(out[name].dtype)
    return out
```

```python
import concourse.bass as bass
from concourse import mybir
from contextlib import ExitStack

F32 = mybir.dt.float32
U32 = mybir.dt.uint32
I32 = mybir.dt.int32
ALU = mybir.AluOpType
ACT = mybir.ActivationFunctionType
AX = mybir.AxisListType

P = 128
C = 128
TILES = 32
BATCHES = 4
TPB = TILES // BATCHES
T = TPB * P
EPS_LN = 1e-5


class Signal:

    def __init__(self, sem, per=1):
        self.sem, self.per, self.credit = sem, per, 0

    def with_credit(self, credit=1):
        self.credit = credit
        return self

    def open(self, eng):
        eng.sem_inc(self.sem, self.credit)

    def wait(self, eng, passes, k):
        at = passes * self.per + k
        if not isinstance(at, int):
            assert self.credit or k > 0, self.sem
        if not isinstance(at, int) or at > 0:
            eng.wait_ge(self.sem, at + self.credit)


def wide(ap, axis, shape):
    return ap.unsqueeze(axis).to_broadcast(shape)


def make_constants(nc, ctx):
    def sb(name, shape):
        return ctx.enter_context(nc.sbuf_tensor(name, shape, F32))

    k = {
        "ident": sb("ident", [P, P]),
        "ones": sb("ones", [P, P]),
        "half_ones": sb("half_ones", [P, P]),
        "head_rows": sb("head_rows", [P, 16]),
        "upto": sb("upto", [P, P]),
        "after": sb("after", [P, P]),
        "before": sb("before", [P, P]),
    }
    filled = ctx.enter_context(nc.semaphore("const_filled"))
    shaped = ctx.enter_context(nc.semaphore("const_shaped"))
    with nc.Block() as block:
        @block.gpsimd
        def _(pool):
            for name in ("ones", "half_ones", "head_rows", "upto", "after", "before"):
                pool.memset(k[name][:, :], 1.0).then_inc(filled, 1)
            pool.memset(k["ident"][:, :], 0.0).then_inc(filled, 1)
            pool.wait_ge(filled, 7)

            def select(name, ap, op, fill, base, pattern, step):
                pool.affine_select(out=ap, in_=ap, compare_op=op, fill=fill, base=base,
                                   pattern=pattern, channel_multiplier=step).then_inc(shaped, 1)
            select("ident", k["ident"][:, :], ALU.not_equal, 1.0, 0, [[-1, P]], 1)
            select("upto", k["upto"][:, :], ALU.is_ge, 0.0, 0, [[1, P]], -1)
            select("after", k["after"][:, :], ALU.is_gt, 0.0, 0, [[-1, P]], 1)
            select("before", k["before"][:, :], ALU.is_gt, 0.0, 0, [[1, P]], -1)
            select("half", k["half_ones"][:, 0:64], ALU.is_gt, 0.0, 64, [[0, 64]], -1)
            select("half", k["half_ones"][:, 64:128], ALU.is_ge, 0.0, -64, [[0, 64]], 1)
            select("head", k["head_rows"][:, :], ALU.is_ge, 0.0, 0, [[-8, 16]], 1)
            pool.wait_ge(shaped, 7)
            select("head", k["head_rows"][:, :], ALU.is_ge, 0.0, 7, [[8, 16]], -1)
            pool.wait_ge(shaped, 8)
    return k


def nystrom_attention(nc, k, x_sb, w_attn, w_proj):
    PAIRS, NL, HS, ITERS = 8, 64, 8, 6
    with ExitStack() as ctx:
        def sb(name, *shape):
            return ctx.enter_context(nc.sbuf_tensor("a_" + name, list(shape), F32))

        def psum(name, *shape):
            return ctx.enter_context(nc.psum_tensor("a_" + name, list(shape), F32))

        def signal(name, per=1):
            return Signal(nc.alloc_semaphore("a_" + name), per)

        wa, wp = sb("wa", P, 3 * C), sb("wp", P, C)
        stats, moments, rstd = sb("stats", P, TPB, 6), sb("moments", P, TPB, 2), sb("rstd", P, TPB)
        xn, xT = sb("xn", P, TPB, C), sb("xT", P, T)
        qT, kT, v = sb("qT", P, T), sb("kT", P, T), sb("v", P, TPB, C)
        q_land, k_land = sb("q_land", P, NL), sb("k_land", P, NL)
        q_diag, k_diag = sb("q_diag", P, 16, NL), sb("k_diag", P, 16, NL)
        mid_max, mid_sum, denom = sb("mid_max", P, PAIRS), sb("mid_sum", P, PAIRS), sb("denom", P, PAIRS)
        mid_x, K = sb("mid_x", P, PAIRS, NL), sb("K", P, PAIRS, NL)
        K_diag, KT_diag = sb("K_diag", P, PAIRS, P), sb("KT_diag", P, PAIRS, P)
        M = [sb(f"M{n}", P, PAIRS, NL) for n in range(2)]
        M_diag = [sb(f"Md{n}", P, PAIRS, P) for n in range(ITERS)]
        M2_diag = [sb(f"M2d{n}", P, PAIRS, P) for n in range(ITERS)]
        M2 = sb("M2", P, PAIRS, NL)
        R, S, S1 = sb("R", P, PAIRS, NL), sb("S", P, PAIRS, NL), sb("S1", P, PAIRS, NL)
        far_max, far_sum = sb("far_max", P, PAIRS), sb("far_sum", P, PAIRS)
        far, farT = [sb(f"far{n}", P, T) for n in range(2)], [sb(f"farT{n}", P, TPB, P) for n in range(2)]
        W, Wr, Ws = sb("W", P, PAIRS, HS), sb("Wr", P, PAIRS, HS), sb("Ws", P, PAIRS, HS)
        near_max = sb("near_max", P, 16)
        near, nearT = [sb(f"near{n}", P, 16, NL) for n in range(2)], sb("nearT", P, TPB, PAIRS, P)
        U_diag = sb("U_diag", P, PAIRS, 18)
        y_rs, y, yT = sb("y_rs", P, PAIRS, 2), sb("y", P, PAIRS, 2, HS), sb("yT", P, C)

        sc = [psum(f"sc{n}", P, 1024) for n in range(2)]
        tp = [psum(f"tp{n}", P, 512) for n in range(2)]
        nw, sm = psum("nw", P, 512), psum("sm", P, 512)


        alone, pool_alone = signal("alone"), signal("pool_alone")
        loaded, zeroed = signal("loaded"), signal("zeroed")
        bn_done, aggr_done, rstd_ready, xn_ready = signal("bn_done", 8), signal("aggr_done", 8), signal("rstd_ready"), signal("xn_ready", 8)
        land_sum, land_ready, diag_ready = signal("land_sum", 2), signal("land_ready", 2), signal("diag_ready", 2)
        var_ready, root_ready = signal("var_ready"), signal("root_ready")
        mid_max_ready, mid_sub, mid_exp, mid_sum_ready = (signal(n) for n in ("mid_max_ready", "mid_sub", "mid_exp", "mid_sum_ready"))
        mid_recip, K_ready, K_diag_ready = signal("mid_recip"), signal("K_ready"), signal("K_diag_ready")
        denom_ready, M0_ready, M_ready = signal("denom_ready", 2), signal("M0_ready"), signal("M_ready", 7)
        S1_ready, M_diag_ready, M2_ready, M2_diag_ready = signal("S1_ready", 5), signal("M_diag_ready", 5), signal("M2_ready", 6), signal("M2_diag_ready", 12)
        R_ready, S_ready = signal("R_ready", 5), signal("S_ready", 5)
        far_bias, far_exp, far_recip, W0_ready = signal("far_bias", 8), signal("far_exp", 8), signal("far_recip"), signal("W0_ready", 2)
        Wr_ready, Wa_ready, Ws_ready, W_ready = (signal(n, 6) for n in ("Wr_ready", "Wa_ready", "Ws_ready", "W_ready"))
        U_ready = signal("U_ready", 2)
        near_max_ready, near_sub, near_exp = signal("near_max_ready", 8), signal("near_sub", 8), signal("near_exp", 8)
        y_recip, y_ready, yT_ready, x_done = signal("y_recip", 8), signal("y_ready", 8), signal("yT_ready", 8), signal("x_done", 8)
        tp_read, qkv_read = signal("tp_read", 36), signal("qkv_read", 3)
        tp_full, sc_full = signal("tp_full", 36), signal("sc_full", 20)
        mid_full, colsum_full, m2_full, pm_full = signal("mid_full"), signal("colsum_full"), signal("m2_full", 6), signal("pm_full", 5)
        nv_full, t1_full, t2_full, u_full = signal("nv_full", 8), signal("t1_full", 6), signal("t2_full", 6), signal("u_full")
        y_full, yT_full, o_full = signal("y_full", 8), signal("yT_full", 8), signal("o_full", 8)
        TP_KT, TP_FAR, TP_NEAR = 2, 4, 20
        SC_M0, SC_FAR, SC_NEAR = 3, 4, 12
        HALVES = (slice(0, 64), slice(64, 128))

        def tile(b, j):
            return bass.ds(b * (TPB * C) + j * C, C)

        def flat(ap):
            return ap.rearrange("p a b -> p (a b)")

        x_done.with_credit()
        block = ctx.enter_context(nc.Block())

        @block.sync
        def _(sp):
            sp.dma_start(wa[:, :], w_attn).then_inc(loaded.sem, 16)
            sp.dma_start(wp[:, :], w_proj).then_inc(loaded.sem, 16)

        @block.gpsimd
        def _(pool):
            for t in (*M2_diag, U_diag):
                pool.memset(t[:, :, :], 0.0).then_inc(zeroed.sem, 1)
            pool.wait_ge(zeroed.sem, 7)
            pool.memset(U_diag[0:64, :, 16:17], 1.0).then_inc(zeroed.sem, 1)
            pool.memset(U_diag[64:128, :, 17:18], 1.0).then_inc(zeroed.sem, 1)
            pool.wait_ge(zeroed.sem, 9)
            halves = wide(wide(k["half_ones"][:, ::NL], 1, [P, PAIRS, 2]), 3, [P, PAIRS, 2, NL])

            def by_half(t):
                return t[:, :, :].rearrange("p a (h l) -> p a h l", h=2)

            def wait(signal, b, steps):
                signal.wait(pool, b, steps)
                pool.sem_inc(pool_alone.sem, 1)

            with pool.Fori(0, BATCHES) as b:
                wait(K_ready, b, 1)
                pool.tensor_tensor(by_half(K_diag), wide(K[:, :, :], 2, [P, PAIRS, 2, NL]), halves, ALU.mult).then_inc(K_diag_ready.sem, 1)
                for i in range(ITERS):
                    wait(M_ready, b, 2 + i)
                    if i:
                        pool.tensor_tensor(by_half(M_diag[i]), wide(M[i % 2][:, :, :], 2, [P, PAIRS, 2, NL]), halves,
                                           ALU.mult).then_inc(M_diag_ready.sem, 1)
                    if i < ITERS - 1:
                        if i:
                            wait(S_ready, b, i)
                        pool.tensor_scalar(S1[:, :, :], M[i % 2][:, :, :], 3.25, None, ALU.mult).then_inc(S1_ready.sem, 1)

        @block.scalar
        def _(act):
            act.wait_ge(zeroed.sem, 9)
            with act.Fori(0, BATCHES) as b:
                def from_tp(n, out):
                    tp_full.wait(act, b, n + 1)
                    act.activation(out, tp[n % 2][:, :], ACT.Copy).then_inc(tp_read.sem, 1)

                var_ready.wait(act, b, 1)
                act.activation(rstd[:, :], rstd[:, :], ACT.Sqrt).then_inc(root_ready.sem, 1)
                for g in range(2):
                    from_tp(g, xT[:, 512 * g:512 * g + 512])
                for n, out in enumerate((qT[:, :], kT[:, :], flat(v[:, :, :]))):
                    sc_full.wait(act, b, n + 1)
                    act.activation(out, sc[n % 2][:, :], ACT.Copy).then_inc(qkv_read.sem, 1)
                mid_sub.wait(act, b, 1)
                act.activation(mid_x[:, :, :], mid_x[:, :, :], ACT.Exp).then_inc(mid_exp.sem, 1)
                for g in range(2):
                    from_tp(TP_KT + g, flat(KT_diag[:, 4 * g:4 * g + 4, :]))
                for s in range(PAIRS):
                    far_bias.wait(act, b, s + 1)
                    if s >= 2:
                        tp_full.wait(act, b, TP_FAR + 2 * (s - 1))
                    act.activation(far[s % 2][:, :], sc[(SC_FAR + s) % 2][:, :], ACT.Exp, bias=far_max[:, s:s + 1],
                                   accum_out=far_sum[:, s:s + 1]).then_inc(far_exp.sem, 1)
                    if s < ITERS:
                        m2_full.wait(act, b, s + 1)
                        if s:
                            S_ready.wait(act, b, s)
                        act.activation(flat(M2[:, :, :]), nw[:, :], ACT.Copy).then_inc(M2_ready.sem, 1)
                        M2_ready.wait(act, b, s + 1)
                        for r in HALVES:
                            act.activation(M2_diag[s][r, :, r], M2[r, :, :], ACT.Copy).then_inc(M2_diag_ready.sem, 1)
                    for g in range(2):
                        if s >= 2:
                            nv_full.wait(act, b, s - 1)
                        from_tp(TP_FAR + 2 * s + g, flat(farT[s % 2][:, 4 * g:4 * g + 4, :]))
                for s in range(TPB):
                    near_sub.wait(act, b, s + 1)
                    act.activation(near[s % 2][:, :, :], near[s % 2][:, :, :], ACT.Exp).then_inc(near_exp.sem, 1)
                    for g in range(2):
                        from_tp(TP_NEAR + 2 * s + g, flat(nearT[:, s, 4 * g:4 * g + 4, :]))
                for s in range(TPB):
                    yT_full.wait(act, b, s + 1)
                    if s:
                        o_full.wait(act, b, s)
                    act.activation(yT[:, :], tp[s % 2][:, 0:C], ACT.Copy).then_inc(yT_ready.sem, 1)

        @block.vector
        def _(dve):
            dve.wait_ge(zeroed.sem, 9)
            x_done.open(dve)
            with dve.Fori(0, BATCHES) as b:
                for j in range(TPB):
                    dve.bn_stats(stats[:, j, :], x_sb[:, tile(b, j)]).then_inc(bn_done.sem, 1)
                bn_done.wait(dve, b, 8)
                dve.sem_inc(alone.sem, 1)
                for j in range(TPB):
                    dve.bn_aggr(moments[:, j, :], stats[:, j, :]).then_inc(aggr_done.sem, 1)
                aggr_done.wait(dve, b, 8)
                dve.tensor_scalar(rstd[:, :], moments[:, :, 1], EPS_LN, None, ALU.add).then_inc(var_ready.sem, 1)
                root_ready.wait(dve, b, 1)
                dve.reciprocal(rstd[:, :], rstd[:, :]).then_inc(rstd_ready.sem, 1)
                rstd_ready.wait(dve, b, 1)
                for j in range(TPB):
                    dve.tensor_scalar(xn[:, j, :], x_sb[:, tile(b, j)], moments[:, j, 0:1], rstd[:, j:j + 1],
                                      ALU.subtract, ALU.mult).then_inc(xn_ready.sem, 1)
                for n, (src, land) in enumerate(((qT, q_land), (kT, k_land))):
                    qkv_read.wait(dve, b, n + 1)
                    dve.tensor_reduce(land[:, :], src[:, :].rearrange("p (l t) -> p l t", l=NL), AX.X, ALU.add).then_inc(land_sum.sem, 1)
                land_sum.wait(dve, b, 2)
                for land in (q_land, k_land):
                    dve.tensor_scalar(land[:, :], land[:, :], NL / T, None, ALU.mult).then_inc(land_ready.sem, 1)
                land_ready.wait(dve, b, 2)
                for land, diag in ((q_land, q_diag), (k_land, k_diag)):
                    dve.tensor_tensor(diag[:, :, :], wide(land[:, :], 1, [P, 16, NL]), wide(k["head_rows"][:, :], 2, [P, 16, NL]),
                                      ALU.mult).then_inc(diag_ready.sem, 1)
                mid = nw[:, :].rearrange("p (a b) -> p a b", b=NL)
                mid_full.wait(dve, b, 1)
                dve.tensor_reduce(mid_max[:, :], mid, AX.X, ALU.max).then_inc(mid_max_ready.sem, 1)
                mid_max_ready.wait(dve, b, 1)
                dve.tensor_tensor(mid_x[:, :, :], mid, wide(mid_max[:, :], 2, [P, PAIRS, NL]), ALU.subtract).then_inc(mid_sub.sem, 1)
                mid_exp.wait(dve, b, 1)
                dve.tensor_reduce(mid_sum[:, :], mid_x[:, :, :], AX.X, ALU.add).then_inc(mid_sum_ready.sem, 1)
                mid_sum_ready.wait(dve, b, 1)
                dve.reciprocal(mid_sum[:, :], mid_sum[:, :]).then_inc(mid_recip.sem, 1)
                mid_recip.wait(dve, b, 1)
                dve.tensor_tensor(K[:, :, :], mid_x[:, :, :], wide(mid_sum[:, :], 2, [P, PAIRS, NL]), ALU.mult).then_inc(K_ready.sem, 1)
                colsum_full.wait(dve, b, 1)
                dve.tensor_reduce(denom[:, :], sm[:, :].rearrange("p (a b) -> p a b", b=NL), AX.X, ALU.max).then_inc(denom_ready.sem, 1)
                denom_ready.wait(dve, b, 1)
                dve.reciprocal(denom[:, :], denom[:, :]).then_inc(denom_ready.sem, 1)
                denom_ready.wait(dve, b, 2)
                sc_full.wait(dve, b, SC_M0 + 1)
                dve.tensor_tensor(M_diag[0][:, :, :], sc[SC_M0 % 2][:, :].rearrange("p (a b) -> p a b", b=P),
                                  wide(denom[:, :], 2, [P, PAIRS, P]), ALU.mult).then_inc(M0_ready.sem, 1)
                M0_ready.wait(dve, b, 1)
                for r in HALVES:
                    dve.tensor_copy(M[0][r, :, :], M_diag[0][r, :, r]).then_inc(M_ready.sem, 1)

                def far_maximum(s):
                    sc_full.wait(dve, b, SC_FAR + s + 1)
                    dve.tensor_reduce(far_max[:, s:s + 1], sc[(SC_FAR + s) % 2][:, :], AX.X, ALU.max, negate=True).then_inc(far_bias.sem, 1)

                far_maximum(0)
                for s in range(PAIRS):
                    if s + 1 < PAIRS:
                        far_maximum(s + 1)
                    if s < ITERS - 1:
                        now, new = M[s % 2], M[(s + 1) % 2]
                        M2_ready.wait(dve, b, s + 1)
                        M_ready.wait(dve, b, 2 + s)
                        dve.scalar_tensor_tensor(flat(R[:, :, :]), flat(now[:, :, :]), 7.0, flat(M2[:, :, :]), ALU.mult, ALU.subtract).then_inc(R_ready.sem, 1)
                        S1_ready.wait(dve, b, s + 1)
                        dve.scalar_tensor_tensor(flat(S[:, :, :]), flat(M2[:, :, :]), -3.75, flat(S1[:, :, :]), ALU.mult, ALU.add).then_inc(S_ready.sem, 1)
                        S_ready.wait(dve, b, s + 1)
                        if s:
                            M_diag_ready.wait(dve, b, s)
                        pm_full.wait(dve, b, s + 1)
                        dve.scalar_tensor_tensor(flat(new[:, :, :]), nw[:, :], 0.25, flat(S[:, :, :]), ALU.mult, ALU.add).then_inc(M_ready.sem, 1)
                far_exp.wait(dve, b, 8)
                dve.reciprocal(far_sum[:, :], far_sum[:, :]).then_inc(far_recip.sem, 1)
                far_recip.wait(dve, b, 1)
                nv_full.wait(dve, b, 8)
                nv = sm[:, 0:128].rearrange("p (a b) -> p a b", b=2 * HS)
                for h, r in enumerate(HALVES):
                    dve.tensor_tensor(W[r, :, :], nv[r, :, HS * h:HS * h + HS], wide(far_sum[r, :], 2, [64, PAIRS, HS]),
                                      ALU.mult).then_inc(W0_ready.sem, 1)
                W0_ready.wait(dve, b, 2)

                def near_softmax(s):
                    scores = sc[(SC_NEAR + s) % 2][:, :].rearrange("p (a b) -> p a b", b=NL)
                    sc_full.wait(dve, b, SC_NEAR + s + 1)
                    if s:
                        near_sub.wait(dve, b, s)
                    dve.tensor_reduce(near_max[:, :], scores, AX.X, ALU.max).then_inc(near_max_ready.sem, 1)
                    near_max_ready.wait(dve, b, s + 1)
                    if s >= 2:
                        tp_full.wait(dve, b, TP_NEAR + 2 * (s - 1))
                    dve.tensor_tensor(near[s % 2][:, :, :], scores, wide(near_max[:, :], 2, [P, 16, NL]), ALU.subtract).then_inc(near_sub.sem, 1)

                near_softmax(0)
                for s in range(TPB):
                    if s + 1 < TPB:
                        near_softmax(s + 1)
                    if s < ITERS:
                        mw, m2w = sm[:, 128:192], sm[:, 192:256]
                        t1_full.wait(dve, b, s + 1)
                        dve.scalar_tensor_tensor(flat(Wr[:, :, :]), flat(W[:, :, :]), 7.0, mw, ALU.mult, ALU.subtract).then_inc(Wr_ready.sem, 1)
                        dve.tensor_scalar(flat(Ws[:, :, :]), flat(W[:, :, :]), 3.25, None, ALU.mult).then_inc(Wa_ready.sem, 1)
                        Wa_ready.wait(dve, b, s + 1)
                        dve.scalar_tensor_tensor(flat(Ws[:, :, :]), mw, -3.75, flat(Ws[:, :, :]), ALU.mult, ALU.add).then_inc(Ws_ready.sem, 1)
                        Ws_ready.wait(dve, b, s + 1)
                        t2_full.wait(dve, b, s + 1)
                        dve.scalar_tensor_tensor(flat(W[:, :, :]), m2w, 0.25, flat(Ws[:, :, :]), ALU.mult, ALU.add).then_inc(W_ready.sem, 1)
                        W_ready.wait(dve, b, s + 1)
                u_full.wait(dve, b, 1)
                for h, r in enumerate(HALVES):
                    dve.tensor_tensor(U_diag[r, :, HS * h:HS * h + HS], sm[r, 256:320].rearrange("p (a b) -> p a b", b=HS),
                                      wide(denom[r, :], 2, [64, PAIRS, HS]), ALU.mult).then_inc(U_ready.sem, 1)

                def output(s):
                    got = sc[s % 2][:, 0:144].rearrange("p (a b) -> p a b", b=18)
                    y_full.wait(dve, b, s + 1)
                    if s:
                        y_ready.wait(dve, b, s)
                    dve.reciprocal(y_rs[:, :, :], got[:, :, 16:18]).then_inc(y_recip.sem, 1)
                    y_recip.wait(dve, b, s + 1)
                    if s:
                        yT_full.wait(dve, b, s)
                    dve.tensor_tensor(y[:, :, :, :], got[:, :, 0:16].rearrange("p a (h d) -> p a h d", h=2),
                                      wide(y_rs[:, :, :], 3, [P, PAIRS, 2, HS]), ALU.mult).then_inc(y_ready.sem, 1)

                def residual(s):
                    o_full.wait(dve, b, s + 1)
                    dve.tensor_tensor(x_sb[:, tile(b, s)], x_sb[:, tile(b, s)], sc[s % 2][:, 512:512 + C],
                                      ALU.add).then_inc(x_done.sem, 1)

                output(0)
                for s in range(TPB):
                    if s + 1 < TPB:
                        output(s + 1)
                    residual(s)
                x_done.wait(dve, b, TPB)

        @block.tensor
        def _(pe):
            pe.wait_ge(loaded.sem, 32)
            with pe.Fori(0, BATCHES) as b:
                use = {"tp": 0}

                def transpose4(ins):
                    n = use["tp"]
                    use["tp"] += 1
                    if n >= 2:
                        tp_read.wait(pe, b, n - 1)
                    for g, ap in enumerate(ins):
                        mm = pe.transpose(tp[n % 2][:, P * g:P * g + P], ap, k["ident"][:, :])
                    mm.then_inc(tp_full.sem, 1)

                x_done.wait(pe, b, 0)
                for g in range(2):
                    xn_ready.wait(pe, b, 4 * g + 4)
                    transpose4([xn[:, j, :] for j in range(4 * g, 4 * g + 4)])
                tp_read.wait(pe, b, 2)
                for n in range(2):
                    for g in range(2):
                        mm = pe.matmul(sc[n][:, 512 * g:512 * g + 512], wa[:, C * n:C * n + C], xT[:, 512 * g:512 * g + 512], start=True, stop=True)
                    mm.then_inc(sc_full.sem, 1)
                qkv_read.wait(pe, b, 1)
                for j in range(TPB):
                    mm = pe.matmul(sc[0][:, C * j:C * j + C], xT[:, P * j:P * j + P], wa[:, 2 * C:3 * C], start=True, stop=True)
                mm.then_inc(sc_full.sem, 1)
                diag_ready.wait(pe, b, 2)
                for s in range(PAIRS):
                    mm = pe.matmul(nw[:, NL * s:NL * s + NL], flat(q_diag[:, 2 * s:2 * s + 2, :]), k_land[:, :], start=True, stop=True)
                mm.then_inc(mid_full.sem, 1)
                K_ready.wait(pe, b, 1)
                pe.matmul(sm[:, :], k["half_ones"][:, :], flat(K[:, :, :]), start=True, stop=True).then_inc(colsum_full.sem, 1)
                K_diag_ready.wait(pe, b, 1)
                for g in range(2):
                    transpose4([K_diag[:, s, :] for s in range(4 * g, 4 * g + 4)])
                tp_read.wait(pe, b, TP_KT + 2)
                qkv_read.wait(pe, b, 2)
                for s in range(PAIRS):
                    mm = pe.matmul(sc[SC_M0 % 2][:, P * s:P * s + P], KT_diag[:, s, :], KT_diag[:, s, :], start=True, stop=True)
                mm.then_inc(sc_full.sem, 1)

                def far_scores(s):
                    n = SC_FAR + s
                    if s == 0:
                        qkv_read.wait(pe, b, 3)
                    elif s == 1:
                        M0_ready.wait(pe, b, 1)
                    else:
                        far_exp.wait(pe, b, s - 1)
                    for g in range(2):
                        mm = pe.matmul(sc[n % 2][:, 512 * g:512 * g + 512], flat(q_diag[:, 2 * s:2 * s + 2, :]),
                                       kT[:, 512 * g:512 * g + 512], start=True, stop=True)
                    mm.then_inc(sc_full.sem, 1)

                def far_times_v(s):
                    tp_read.wait(pe, b, TP_FAR + 2 * s + 2)
                    if s == 0:
                        denom_ready.wait(pe, b, 1)
                    for j in range(TPB):
                        mm = pe.matmul(sm[:, 16 * s:16 * s + 16], farT[s % 2][:, j, :], v[:, j, 16 * s:16 * s + 16],
                                       start=(j == 0), stop=(j == TPB - 1))
                    mm.then_inc(nv_full.sem, 1)

                far_scores(0)
                for s in range(PAIRS):
                    if s + 1 < PAIRS:
                        far_scores(s + 1)
                    if s < ITERS:
                        M_ready.wait(pe, b, 2 + s)
                        if s:
                            M_diag_ready.wait(pe, b, s)
                        for a in range(PAIRS):
                            mm = pe.matmul(nw[:, NL * a:NL * a + NL], M_diag[s][:, a, :], M[s % 2][:, a, :], start=True, stop=True)
                        mm.then_inc(m2_full.sem, 1)
                    far_exp.wait(pe, b, s + 1)
                    for g in range(2):
                        transpose4([far[s % 2][:, P * j:P * j + P] for j in range(4 * g, 4 * g + 4)])
                    if s < ITERS - 1:
                        R_ready.wait(pe, b, s + 1)
                        M2_diag_ready.wait(pe, b, 2 * s + 2)
                        for a in range(PAIRS):
                            mm = pe.matmul(nw[:, NL * a:NL * a + NL], M2_diag[s][:, a, :], R[:, a, :], start=True, stop=True)
                        mm.then_inc(pm_full.sem, 1)
                    if s:
                        far_times_v(s - 1)
                far_times_v(PAIRS - 1)
                M2_diag_ready.wait(pe, b, 12)

                def near_scores(s):
                    n = SC_NEAR + s
                    if s < 2:
                        far_exp.wait(pe, b, 7 + s)
                    else:
                        near_sub.wait(pe, b, s - 1)
                    for g in range(2):
                        mm = pe.matmul(sc[n % 2][:, 512 * g:512 * g + 512], qT[:, P * s:P * s + P], flat(k_diag[:, 8 * g:8 * g + 8, :]),
                                       start=True, stop=True)
                    mm.then_inc(sc_full.sem, 1)

                near_scores(0)
                for s in range(TPB):
                    if s + 1 < TPB:
                        near_scores(s + 1)
                    if s < ITERS:
                        if s:
                            W_ready.wait(pe, b, s)
                        else:
                            W0_ready.wait(pe, b, 2)
                        for a in range(PAIRS):
                            mm = pe.matmul(sm[:, 128 + HS * a:128 + HS * a + HS], M_diag[s][:, a, :], W[:, a, :], start=True, stop=True)
                        mm.then_inc(t1_full.sem, 1)
                    elif s == ITERS:
                        W_ready.wait(pe, b, ITERS)
                        for a in range(PAIRS):
                            mm = pe.matmul(sm[:, 256 + HS * a:256 + HS * a + HS], K_diag[:, a, :], W[:, a, :], start=True, stop=True)
                        mm.then_inc(u_full.sem, 1)
                    near_exp.wait(pe, b, s + 1)
                    for g in range(2):
                        transpose4([flat(near[s % 2][:, 2 * a:2 * a + 2, :]) for a in range(4 * g, 4 * g + 4)])
                    if s < ITERS:
                        Wr_ready.wait(pe, b, s + 1)
                        Ws_ready.wait(pe, b, s + 1)
                        for a in range(PAIRS):
                            mm = pe.matmul(sm[:, 192 + HS * a:192 + HS * a + HS], M2_diag[s][:, a, :], Wr[:, a, :], start=True, stop=True)
                        mm.then_inc(t2_full.sem, 1)

                def near_times_U(s):
                    if s >= 2:
                        y_ready.wait(pe, b, s - 1)
                    for a in range(PAIRS):
                        mm = pe.matmul(sc[s % 2][:, 18 * a:18 * a + 18], nearT[:, s, a, :], U_diag[:, a, :], start=True, stop=True)
                    mm.then_inc(y_full.sem, 1)

                tp_read.wait(pe, b, TP_NEAR + 16)
                U_ready.wait(pe, b, 2)
                near_times_U(0)
                for s in range(TPB):
                    if s + 1 < TPB:
                        near_times_U(s + 1)
                    y_ready.wait(pe, b, s + 1)
                    if s >= 2:
                        x_done.wait(pe, b, s - 1)
                    pe.transpose(tp[s % 2][:, 0:C], y[:, :, :, :].rearrange("p a h d -> p (a h d)"), k["ident"][:, :]).then_inc(yT_full.sem, 1)
                    yT_ready.wait(pe, b, s + 1)
                    pe.matmul(sc[s % 2][:, 512:512 + C], yT[:, :], wp[:, :], start=True, stop=True).then_inc(o_full.sem, 1)


TOKENS = TILES * P
EXPERTS, TOP_K, HIDDEN = 8, 2, 512
DEPTH_SCALE = 1.0 / 12 ** 0.5
SLOT_TILES = TOP_K * TILES + EXPERTS
PARTS = HIDDEN // P


def mixture_of_experts(nc, k, x_sb, wr_dram, wg_dram, wu_dram, wd_dram, xn_dram, y_dram, name):
    with ExitStack() as ctx:
        def sb(n, *shape, dt=F32):
            return ctx.enter_context(nc.sbuf_tensor(name + n, list(shape), dt))

        def psum(cx, n, *shape):
            return cx.enter_context(nc.psum_tensor(name + n, list(shape), F32))

        def signal(n, per=1):
            return Signal(nc.alloc_semaphore(name + n), per)

        wr = sb("wr", P, EXPERTS)
        wg, wu, wd = sb("wg", P, EXPERTS * HIDDEN), sb("wu", P, EXPERTS * HIDDEN), sb("wd", P, EXPERTS * HIDDEN)
        top, best = sb("top", P, TILES, 8), sb("best", P, TILES, 8, dt=U32)
        weight = sb("weight", P, TOP_K, TILES)
        token_row, out_row = sb("token_row", P, SLOT_TILES, dt=U32), sb("out_row", P, SLOT_TILES, dt=U32)
        expert_at = sb("expert_at", 1, SLOT_TILES, dt=I32)
        loaded = signal("loaded")
        route(nc, k, x_sb, wr_dram, wg_dram, wu_dram, wd_dram, xn_dram, wr, wg, wu, wd, top, best, loaded, name)
        place(nc, k, top, best, weight, token_row, out_row, expert_at, name)
        run_experts(nc, k, wg, wu, wd, token_row, out_row, expert_at, xn_dram, y_dram, loaded, name)
        combine(nc, x_sb, weight, y_dram, name)


def route(nc, k, x_sb, wr_dram, wg_dram, wu_dram, wd_dram, xn_dram, wr, wg, wu, wd, top, best, loaded, name):
    with ExitStack() as ctx:
        def sb(n, *shape, dt=F32):
            return ctx.enter_context(nc.sbuf_tensor(name + n, list(shape), dt))

        def signal(n, per=1):
            return Signal(nc.alloc_semaphore(name + n), per)

        G = 8
        stats, moments, rstd = sb("stats", P, G, 6), sb("moments", P, G, 2), sb("rstd", P, G)
        xn, xT = [sb(f"xn{n}", P, G, C) for n in range(2)], sb("xT", P, G, P)
        lg, m8, i8 = sb("lg", P, G, 8), sb("m8", P, G, 8), sb("i8", P, G, 8, dt=U32)
        tp = [ctx.enter_context(nc.psum_tensor(f"{name}tp{n}", [P, 512], F32)) for n in range(2)]
        lp = ctx.enter_context(nc.psum_tensor(f"{name}lp", [P, 512], F32))
        alone = signal("r_alone")
        bn_done, aggr_done, var_ready, root_ready, rstd_ready, xn_ready = (
            signal(n, p) for n, p in (("bn", 8), ("aggr", 8), ("var", 1), ("root", 1), ("rstd", 1), ("xn_ready", 8)))
        tp_full, tp_read, lg_full, lg_ready = signal("tp_full", 2), signal("tp_read", 2), signal("lg_full"), signal("lg_ready")
        m8_ready, i8_ready, kept = signal("m8", 8), signal("i8_", 8), signal("kept", 2)
        stored = [signal(f"stored{n}") for n in range(2)]
        xn_rows = xn_dram.rearrange("(n p) c -> p n c", p=P)
        block = ctx.enter_context(nc.Block())

        @block.sync
        def _(sp):
            sp.dma_start(wr[:, :], wr_dram).then_inc(loaded.sem, 16)
            for w, dram in ((wg, wg_dram), (wu, wu_dram)):
                sp.dma_start(w[:, :].rearrange("c (e h) -> c e h", e=EXPERTS), dram.rearrange("e c h -> c e h")).then_inc(loaded.sem, 16)
            sp.dma_start(wd[:, :].rearrange("h (e j c) -> h e j c", e=EXPERTS, j=PARTS),
                         wd_dram.rearrange("e (j h) c -> h e j c", h=P)).then_inc(loaded.sem, 16)
            for g in range(TILES // G):
                sp.wait_ge(xn_ready.sem, 8 * g + 8)
                sp.dma_start(xn_rows[:, G * g:G * g + G, :], xn[g % 2][:, :, :]).then_inc(stored[g % 2].sem, 16)
            for n in range(2):
                sp.wait_ge(stored[n].sem, 8 * (TILES // G))

        @block.vector
        def _(dve):
            def rest(g):
                lg_ready.wait(dve, g, 1)
                if g:
                    kept.wait(dve, g, 0)
                for j in range(G):
                    dve.max(m8[:, j, :], lg[:, j, :]).then_inc(m8_ready.sem, 1)
                m8_ready.wait(dve, g, 8)
                for j in range(G):
                    dve.max_index(i8[:, j, :], m8[:, j, :], lg[:, j, :]).then_inc(i8_ready.sem, 1)
                i8_ready.wait(dve, g, 8)
                dve.tensor_copy(top[:, G * g:G * g + G, :], m8[:, :, :]).then_inc(kept.sem, 1)
                dve.tensor_copy(best[:, G * g:G * g + G, :], i8[:, :, :]).then_inc(kept.sem, 1)

            for g in range(TILES // G):
                if g:
                    xn_ready.wait(dve, g, 0)
                for j in range(G):
                    dve.bn_stats(stats[:, j, :], x_sb[:, (G * g + j) * C:(G * g + j + 1) * C]).then_inc(bn_done.sem, 1)
                bn_done.wait(dve, g, 8)
                for j in range(G):
                    dve.bn_aggr(moments[:, j, :], stats[:, j, :]).then_inc(aggr_done.sem, 1)
                aggr_done.wait(dve, g, 8)
                dve.tensor_scalar(rstd[:, :], moments[:, :, 1], EPS_LN, None, ALU.add).then_inc(var_ready.sem, 1)
                root_ready.wait(dve, g, 1)
                dve.reciprocal(rstd[:, :], rstd[:, :]).then_inc(rstd_ready.sem, 1)
                rstd_ready.wait(dve, g, 1)
                if g >= 2:
                    tp_full.wait(dve, g - 1, 0)
                    dve.wait_ge(stored[g % 2].sem, 16 * (g // 2))
                for j in range(G):
                    dve.tensor_scalar(xn[g % 2][:, j, :], x_sb[:, (G * g + j) * C:(G * g + j + 1) * C], moments[:, j, 0:1],
                                      rstd[:, j:j + 1], ALU.subtract, ALU.mult).then_inc(xn_ready.sem, 1)
                if g:
                    rest(g - 1)
            rest(TILES // G - 1)
            kept.wait(dve, TILES // G, 0)

        @block.scalar
        def _(act):
            for g in range(TILES // G):
                var_ready.wait(act, g, 1)
                act.activation(rstd[:, :], rstd[:, :], ACT.Sqrt).then_inc(root_ready.sem, 1)
                if g:
                    lg_full.wait(act, g, 0)
                for h in range(2):
                    tp_full.wait(act, g, h + 1)
                    act.activation(xT[:, 4 * h:4 * h + 4, :].rearrange("p a b -> p (a b)"), tp[h][:, :], ACT.Copy).then_inc(tp_read.sem, 1)
                lg_full.wait(act, g, 1)
                if g:
                    i8_ready.wait(act, g, 0)
                act.activation(lg[:, :, :].rearrange("p a b -> p (a b)"), lp[:, 0:64], ACT.Copy).then_inc(lg_ready.sem, 1)

        @block.tensor
        def _(pe):
            pe.wait_ge(loaded.sem, 64)
            for g in range(TILES // G):
                for h in range(2):
                    xn_ready.wait(pe, g, 4 * h + 4)
                    if g:
                        tp_read.wait(pe, g - 1, h + 1)
                    for j in range(4):
                        mm = pe.transpose(tp[h][:, P * j:P * j + P], xn[g % 2][:, 4 * h + j, :], k["ident"][:, :])
                    mm.then_inc(tp_full.sem, 1)
                tp_read.wait(pe, g, 2)
                if g:
                    lg_ready.wait(pe, g, 0)
                for j in range(G):
                    mm = pe.matmul(lp[:, 8 * j:8 * j + 8], xT[:, j, :], wr[:, :], start=True, stop=True)
                mm.then_inc(lg_full.sem, 1)


def place(nc, k, top, best, weight, token_row, out_row, expert_at, name):
    with ExitStack() as ctx:
        def sb(n, *shape, dt=F32):
            return ctx.enter_context(nc.sbuf_tensor(name + n, list(shape), dt))

        def signal(n, per=1):
            return Signal(nc.alloc_semaphore(name + n), per)

        ei, ef, idx, oh = sb("ei", P, 8, dt=I32), sb("ef", P, 8), sb("idx", P, 2, TILES), sb("oh", P, 2, 8, TILES)
        tok, tok_f = sb("tok", P, TILES, dt=I32), sb("tok_f", P, TILES)
        col, col_f = sb("col", P, P, dt=I32), sb("col_f", P, P)
        spare, spare_f = sb("spare", P, SLOT_TILES, dt=I32), sb("spare_f", P, SLOT_TILES)
        both, cum, reset = sb("both", P, 8, TILES), sb("cum", P, 8, TILES), sb("reset", P, 8, TILES)
        total, cnt, need, end = sb("total", P, 8), sb("cnt", P, 8), sb("need", P, 8), sb("end", P, 8)
        need_i = sb("need_i", P, 8, dt=I32)
        off = sb("off", P, 8)
        pick, slot = sb("pick", P, 8, TILES), sb("slot", P, 2, TILES)
        slot_i, a_i, p_i = (sb(n, P, 2 * TILES, dt=I32) for n in ("slot_i", "a_i", "p_i"))
        a_f, p_f = sb("a_f", P, 2 * TILES), sb("p_f", P, 2 * TILES)
        gap, e1 = sb("gap", P, TILES), sb("e1", P, TILES)
        B = [sb(f"B{n}", P, P) for n in range(4)]
        A = [sb(f"A{n}", P, SLOT_TILES) for n in range(4)]
        code = [sb(f"code{n}", P, 2 * TILES) for n in range(1)][0]
        got, late, empty = sb("got", P, SLOT_TILES), sb("late", P, SLOT_TILES), sb("empty", P, SLOT_TILES)
        row = sb("row", P, SLOT_TILES)
        passed = sb("passed", 1, SLOT_TILES, 8)
        at_f = sb("at_f", 1, SLOT_TILES)
        cp = ctx.enter_context(nc.psum_tensor(f"{name}cp", [P, 512], F32))
        ip = ctx.enter_context(nc.psum_tensor(f"{name}ip", [P, 512], F32))
        counted, iotas, gap_ready, e1_ready = signal("counted"), signal("iotas"), signal("gap_ready"), signal("e1_ready")
        total_ready, hot, inverted = signal("total_ready"), signal("hot"), signal("inverted")
        step = signal("step")
        block = ctx.enter_context(nc.Block())

        @block.gpsimd
        def _(pool):
            pool.iota(ei[:, :], [[1, 8]], base=0, channel_multiplier=0).then_inc(iotas.sem, 1)
            pool.iota(tok[:, :], [[P, TILES]], base=1, channel_multiplier=1).then_inc(iotas.sem, 1)
            pool.iota(col[:, :], [[1, P]], base=0, channel_multiplier=0).then_inc(iotas.sem, 1)
            pool.iota(spare[:, :], [[P, SLOT_TILES]], base=TOP_K * TOKENS, channel_multiplier=1).then_inc(iotas.sem, 1)

        @block.scalar
        def _(act):
            gap_ready.wait(act, 0, 1)
            act.activation(e1[:, :], gap[:, :], ACT.Exp).then_inc(e1_ready.sem, 1)

        @block.tensor
        def _(pe):
            total_ready.wait(pe, 0, 1)
            pe.matmul(cp[:, 0:8], k["before"][:, :], total[:, :], start=True, stop=True)
            pe.matmul(cp[:, 8:16], k["ones"][:, :], total[:, :], start=True, stop=True).then_inc(counted.sem, 1)
            for n in range(2 * TILES):
                hot.wait(pe, 0, 2 * n + 2)
                pe.matmul(ip[:, 0:SLOT_TILES], B[n % 4][:, :], A[n % 4][:, :], start=(n == 0), stop=(n == 2 * TILES - 1)).then_inc(inverted.sem, 1)

        @block.vector
        def _(dve):
            steps = [0]

            def then(ins):
                steps[0] += 1
                ins.then_inc(step.sem, 1)
                dve.wait_ge(step.sem, steps[0])

            iotas.wait(dve, 0, 4)
            for i, f in ((ei, ef), (tok, tok_f), (col, col_f), (spare, spare_f)):
                then(dve.tensor_copy(f[:, :], i[:, :]))
            dve.tensor_tensor(gap[:, :], top[:, :, 1], top[:, :, 0], ALU.subtract).then_inc(gap_ready.sem, 1)
            then(dve.tensor_copy(idx[:, :, :].rearrange("p a b -> p b a"), best[:, :, 0:2]))
            for n in range(2):
                then(dve.tensor_tensor(oh[:, n, :, :], wide(ef[:, :], 2, [P, 8, TILES]), wide(idx[:, n, :], 1, [P, 8, TILES]), ALU.is_equal))
            then(dve.tensor_tensor(both[:, :, :], oh[:, 0, :, :], oh[:, 1, :, :], ALU.add))
            then(dve.memset(reset[:, :, :], 1.0))
            then(dve.memset(reset[:, :, 0:1], 0.0))
            then(dve.tensor_tensor_scan(cum[:, :, :].rearrange("p a b -> p (a b)"), reset[:, :, :].rearrange("p a b -> p (a b)"),
                                        both[:, :, :].rearrange("p a b -> p (a b)"), 0.0, ALU.mult, ALU.add))
            dve.tensor_copy(total[:, :], cum[:, :, TILES - 1]).then_inc(total_ready.sem, 1)
            e1_ready.wait(dve, 0, 1)
            then(dve.tensor_scalar(gap[:, :], e1[:, :], 1.0, None, ALU.add))
            then(dve.reciprocal(weight[:, 0, :], gap[:, :]))
            then(dve.tensor_tensor(weight[:, 1, :], e1[:, :], weight[:, 0, :], ALU.mult))
            counted.wait(dve, 0, 1)
            then(dve.tensor_copy(off[:, :], cp[:, 0:8]))
            then(dve.tensor_scalar(need_i[:, :], cp[:, 8:16], float(P - 1), None, ALU.add))
            then(dve.tensor_scalar(need_i[:, :], need_i[:, :], 7, None, ALU.logical_shift_right))
            then(dve.tensor_copy(need[:, :], need_i[:, :]))
            then(dve.tensor_tensor_scan(end[:, :], k["ones"][:, 0:8], need[:, :], 0.0, ALU.mult, ALU.add))
            then(dve.tensor_tensor(cnt[:, :], end[:, :], need[:, :], ALU.subtract))
            then(dve.scalar_tensor_tensor(off[:, :], cnt[:, :], float(P), off[:, :], ALU.mult, ALU.add))
            then(dve.tensor_tensor(cum[:, :, :], cum[:, :, :], both[:, :, :], ALU.subtract))
            then(dve.tensor_tensor(cum[:, :, :], cum[:, :, :], wide(off[:, :], 2, [P, 8, TILES]), ALU.add))
            for n in range(2):
                then(dve.tensor_tensor(pick[:, :, :], cum[:, :, :], oh[:, n, :, :], ALU.mult))
                then(dve.tensor_reduce(slot[:, n, :], pick[:, :, :].rearrange("p e t -> p t e"), AX.X, ALU.add))
            then(dve.tensor_copy(slot_i[:, :], slot[:, :, :].rearrange("p a b -> p (a b)")))
            then(dve.tensor_scalar(a_i[:, :], slot_i[:, :], 7, None, ALU.logical_shift_right))
            then(dve.tensor_scalar(p_i[:, :], slot_i[:, :], P - 1, None, ALU.bitwise_and))
            then(dve.tensor_copy(a_f[:, :], a_i[:, :]))
            then(dve.tensor_copy(p_f[:, :], p_i[:, :]))
            then(dve.tensor_copy(code[:, 0:TILES], tok_f[:, :]))
            then(dve.tensor_scalar(code[:, TILES:2 * TILES], tok_f[:, :], float(TOKENS), None, ALU.add))
            for n in range(2 * TILES):
                if n >= 4:
                    inverted.wait(dve, 0, n - 3)
                dve.tensor_scalar(B[n % 4][:, :], col_f[:, :], p_f[:, n:n + 1], None, ALU.is_equal).then_inc(hot.sem, 1)
                dve.tensor_scalar(A[n % 4][:, :], col_f[:, 0:SLOT_TILES], a_f[:, n:n + 1], code[:, n:n + 1], ALU.is_equal, ALU.mult).then_inc(hot.sem, 1)
            then(dve.tensor_tensor(passed[:, :, :], wide(col_f[0:1, 0:SLOT_TILES], 2, [1, SLOT_TILES, 8]), wide(end[0:1, :], 1, [1, SLOT_TILES, 8]), ALU.is_ge))
            then(dve.tensor_reduce(at_f[:, :], passed[:, :, :], AX.X, ALU.add))
            then(dve.tensor_scalar(at_f[:, :], at_f[:, :], float(EXPERTS - 1), float(HIDDEN), ALU.min, ALU.mult))
            then(dve.tensor_copy(expert_at[:, :], at_f[:, :]))
            inverted.wait(dve, 0, 2 * TILES)
            then(dve.tensor_copy(got[:, :], ip[:, 0:SLOT_TILES]))
            then(dve.tensor_scalar(empty[:, :], got[:, :], 0.0, None, ALU.is_equal))
            then(dve.scalar_tensor_tensor(late[:, :], spare_f[:, :], 1.0, empty[:, :], ALU.add, ALU.mult))
            then(dve.scalar_tensor_tensor(row[:, :], got[:, :], -1.0, late[:, :], ALU.add, ALU.add))
            then(dve.tensor_copy(out_row[:, :], row[:, :]))
            then(dve.tensor_scalar(late[:, :], got[:, :], float(TOKENS), float(-TOKENS), ALU.is_gt, ALU.mult))
            then(dve.tensor_tensor(row[:, :], got[:, :], late[:, :], ALU.add))
            then(dve.tensor_scalar(row[:, :], row[:, :], 1.0, -1.0, ALU.max, ALU.add))
            then(dve.tensor_copy(token_row[:, :], row[:, :]))


def run_experts(nc, k, wg, wu, wd, token_row, out_row, expert_at, xn_dram, y_dram, loaded, name):
    with ExitStack() as ctx:
        def sb(n, *shape, dt=F32):
            return ctx.enter_context(nc.sbuf_tensor(name + n, list(shape), dt))

        def psum(n):
            return ctx.enter_context(nc.psum_tensor(name + n, [P, 512], F32))

        def signal(n, per=1):
            return Signal(nc.alloc_semaphore(name + n), per)

        XB = 4
        xg, row_x, row_y = [sb(f"xg{n}", P, C) for n in range(XB)], [sb(f"row_x{n}", P, 1, dt=U32) for n in range(XB)], [sb(f"row_y{n}", P, 1, dt=U32) for n in range(XB)]
        xgT, act_g, h, hT, out = ([sb(f"{m}{n}", P, w) for n in range(2)] for m, w in (("xgT", P), ("sg", 512), ("h", 512), ("hT", 512), ("yo", C)))
        gp, up = [psum(f"gp{n}") for n in range(2)], [psum(f"up{n}") for n in range(2)]
        xp, hp, dp = psum("xp"), psum("hp"), [psum(f"dp{n}") for n in range(2)]
        rows_x, rows_y, gathered = signal("rows_x"), signal("rows_y"), [signal(f"gathered{n}") for n in range(XB)]
        x_full, x_read, gu_full, g_done, h_done = (signal(n) for n in ("x_full", "x_read", "gu_full", "g_done", "h_done"))
        hT_full, hT_read, d_full, d_read = (signal(n) for n in ("hT_full", "hT_read", "d_full", "d_read"))
        scattered = [signal(f"scattered{n}") for n in range(2)]
        alone = signal("e_alone")
        N = SLOT_TILES

        def column(ap, a):
            return ap[:, bass.ds(a, 1)] if not isinstance(a, int) else ap[:, a:a + 1]

        block = ctx.enter_context(nc.Block())

        @block.gpsimd
        def _(pool):
            def gather(a, u, at):
                if at is None or at >= XB:
                    x_full_wait(pool, a - XB + 1)
                pool.tensor_copy(row_x[u][:, :], column(token_row, a)).then_inc(rows_x.sem, 1)
                pool.wait_ge(rows_x.sem, a + 1)
                pool.sem_inc(alone.sem, 1)
                pool.indirect_dma_start(xg[u][:, :], None, xn_dram, bass.IndirectOffsetOnAxis(row_x[u][:, 0:1], 0)).then_inc(gathered[u].sem, 16)

            def x_full_wait(eng, v):
                eng.wait_ge(x_full.sem, v)
                eng.sem_inc(alone.sem, 1)

            def scatter(a, u, w):
                d_read_wait(a + 1)
                pool.tensor_copy(row_y[u][:, :], column(out_row, a)).then_inc(rows_y.sem, 1)
                pool.wait_ge(rows_y.sem, a + 1)
                pool.sem_inc(alone.sem, 1)
                pool.indirect_dma_start(y_dram, bass.IndirectOffsetOnAxis(row_y[u][:, 0:1], 0), out[w][:, :], None).then_inc(scattered[w].sem, 16)

            def d_read_wait(v):
                pool.wait_ge(d_read.sem, v)
                pool.sem_inc(alone.sem, 1)

            for a in range(3):
                gather(a, a, a)

            def step(s, u, at):
                if at is None or at + 3 < N:
                    gather(s + 3, (u + 3) % 4, None if at is None else at + 3)
                if at is None or at >= 2:
                    scatter(s - 2, (u - 2) % 4, u % 2)

            for s in range(4):
                step(s, s, s)
            with pool.Fori(0, N // 4 - 2) as r:
                for u in range(4):
                    step(r * 4 + (4 + u), u, None)
            for s in range(N - 4, N + 2):
                step(s, s % 4, s)
            for w in range(2):
                pool.wait_ge(scattered[w].sem, 16 * (N // 2))

        @block.tensor
        def _(pe):
            loaded.wait(pe, 0, 64)

            def transpose_x(a, u, at):
                if at is None or at >= 1:
                    pe.wait_ge(x_read.sem, a)
                wait_gathered(pe, a, u)
                pe.transpose(xp[:, 0:P], xg[u][:, :], k["ident"][:, :]).then_inc(x_full.sem, 1)

            def wait_gathered(eng, a, u):
                eng.wait_ge(gathered[u].sem, (a - u + 4) * 4)

            def step(s, u, at):
                if at is None or at < N:
                    e_now = pe.value_load(column(expert_at, s), min_val=0, max_val=(EXPERTS - 1) * HIDDEN)
                if at is None or at >= 2:
                    e_down = pe.value_load(column(expert_at, s - 2), min_val=0, max_val=(EXPERTS - 1) * HIDDEN)
                if at is None or at < N:
                    pe.wait_ge(x_read.sem, s + 1)
                    if at is None or at >= 2:
                        pe.wait_ge(h_done.sem, s - 1)
                    pe.matmul(gp[u % 2][:, :], xgT[u % 2][:, :], wg[:, bass.ds(e_now, HIDDEN)], start=True, stop=True)
                    pe.matmul(up[u % 2][:, :], xgT[u % 2][:, :], wu[:, bass.ds(e_now, HIDDEN)], start=True, stop=True).then_inc(gu_full.sem, 1)
                if at is None or at + 1 < N:
                    transpose_x(s + 1, (u + 1) % 4, None if at is None else at + 1)
                if at is None or 1 <= at <= N:
                    if at is None or at >= 2:
                        pe.wait_ge(hT_read.sem, s - 1)
                    pe.wait_ge(h_done.sem, s)
                    for j in range(PARTS):
                        mm = pe.transpose(hp[:, P * j:P * j + P], h[(u - 1) % 2][:, P * j:P * j + P], k["ident"][:, :])
                    mm.then_inc(hT_full.sem, 1)
                if at is None or at >= 2:
                    pe.wait_ge(hT_read.sem, s - 1)
                    if at is None or at >= 4:
                        pe.wait_ge(d_read.sem, s - 3)
                    for j in range(PARTS):
                        mm = pe.matmul(dp[u % 2][:, 0:C], hT[u % 2][:, P * j:P * j + P], wd[:, bass.ds(e_down + j * C, C)],
                                       start=(j == 0), stop=(j == PARTS - 1))
                    mm.then_inc(d_full.sem, 1)

            transpose_x(0, 0, 0)
            for s in range(4):
                step(s, s, s)
            with pe.Fori(0, N // 4 - 2) as r:
                for u in range(4):
                    step(r * 4 + (4 + u), u, None)
            for s in range(N - 4, N + 2):
                step(s, s % 4, s)

        @block.scalar
        def _(act):
            def read_x(a, u, at):
                act.wait_ge(x_full.sem, a + 1)
                if at is None or at >= 2:
                    act.wait_ge(gu_full.sem, a - 1)
                act.activation(xgT[u % 2][:, :], xp[:, 0:P], ACT.Copy).then_inc(x_read.sem, 1)

            def step(s, u, at):
                if at is None or at + 1 < N:
                    read_x(s + 1, u + 1, None if at is None else at + 1)
                if at is None or at < N:
                    act.wait_ge(gu_full.sem, s + 1)
                    if at is None or at >= 2:
                        act.wait_ge(h_done.sem, s - 1)
                    act.activation(act_g[u % 2][:, :], gp[u % 2][:, :], ACT.Silu).then_inc(g_done.sem, 1)
                if at is None or 1 <= at <= N:
                    act.wait_ge(hT_full.sem, s)
                    if at is None or at >= 3:
                        act.wait_ge(d_full.sem, s - 2)
                    act.activation(hT[(u - 1) % 2][:, :], hp[:, :], ACT.Copy).then_inc(hT_read.sem, 1)

            read_x(0, 0, 0)
            for s in range(4):
                step(s, s, s)
            with act.Fori(0, N // 4 - 2) as r:
                for u in range(4):
                    step(r * 4 + (4 + u), u, None)
            for s in range(N - 4, N + 2):
                step(s, s % 4, s)

        @block.vector
        def _(dve):
            def step(s, u, at):
                if at is None or at < N:
                    dve.wait_ge(g_done.sem, s + 1)
                    if at is None or at >= 2:
                        dve.wait_ge(hT_full.sem, s - 1)
                    dve.tensor_tensor(h[u % 2][:, :], act_g[u % 2][:, :], up[u % 2][:, :], ALU.mult).then_inc(h_done.sem, 1)
                if at is None or at >= 2:
                    dve.wait_ge(d_full.sem, s - 1)
                    if at is None or at >= 4:
                        dve.wait_ge(scattered[u % 2].sem, (s - u % 2 - 2) * 8)
                    dve.tensor_scalar(out[u % 2][:, :], dp[u % 2][:, 0:C], DEPTH_SCALE, None, ALU.mult).then_inc(d_read.sem, 1)

            for s in range(4):
                step(s, s, s)
            with dve.Fori(0, N // 4 - 2) as r:
                for u in range(4):
                    step(r * 4 + (4 + u), u, None)
            for s in range(N - 4, N + 2):
                step(s, s % 4, s)


def combine(nc, x_sb, weight, y_dram, name):
    with ExitStack() as ctx:
        G = 4
        y = [[ctx.enter_context(nc.sbuf_tensor(f"{name}y{n}{m}", [P, G, C], F32)) for m in range(2)] for n in range(2)]
        arrived = [nc.alloc_semaphore(f"{name}arrived{n}") for n in range(2)]
        added = nc.alloc_semaphore(f"{name}added")
        rows = y_dram[0:TOP_K * TOKENS, :].rearrange("(m n p) c -> m p n c", m=TOP_K, p=P)
        block = ctx.enter_context(nc.Block())

        @block.sync
        def _(sp):
            for g in range(TILES // G):
                if g >= 2:
                    sp.wait_ge(added, 2 * G * (g - 1))
                for m in range(TOP_K):
                    sp.dma_start(y[g % 2][m][:, :, :], rows[m, :, G * g:G * g + G, :]).then_inc(arrived[g % 2], 16)

        @block.vector
        def _(dve):
            for g in range(TILES // G):
                dve.wait_ge(arrived[g % 2], 32 * (g // 2 + 1))
                for m in range(TOP_K):
                    if m:
                        dve.wait_ge(added, 2 * G * g + G)
                    for j in range(G):
                        t = G * g + j
                        dve.scalar_tensor_tensor(x_sb[:, t * C:t * C + C], y[g % 2][m][:, j, :], weight[:, m, t:t + 1],
                                                 x_sb[:, t * C:t * C + C], ALU.mult, ALU.add).then_inc(added, 1)
            dve.wait_ge(added, 2 * TILES)


HEADS, KD, VD, TAPS = 8, 128, 32, 4
QUADS = 4
BLOCKS = 2 * HEADS + 2
LEVELS = (2, 4, 8, 16, 32, 64)
EPS_NORM, EPS_RMS = 1e-6, 1e-5
G_, BETA, GAMMA, GAMMA_END, DECAY_END = range(5)


def delta_attention(nc, k, x_sb, w, o_dram):
    with ExitStack() as ctx:
        xT = ctx.enter_context(nc.sbuf_tensor("b_xT", [P, BATCHES, TAPS - 1 + T], F32))
        prm = ctx.enter_context(nc.sbuf_tensor("b_prm", [P, TILES, 5, HEADS], F32))
        delta_inputs(nc, k, x_sb, w, xT, prm)
        delta_chunks(nc, k, w, xT, prm, o_dram)
        delta_output(nc, k, x_sb, w, xT, o_dram)


def delta_inputs(nc, k, x_sb, w, xT, prm):
    with ExitStack() as ctx:
        def sb(n, *shape, dt=F32):
            return ctx.enter_context(nc.sbuf_tensor("b0_" + n, list(shape), dt))

        def signal(n, per=1):
            return Signal(nc.alloc_semaphore("b0_" + n), per)

        G = 8
        stats, moments, rstd = sb("stats", P, G, 6), sb("moments", P, G, 2), sb("rstd", P, G)
        xn = sb("xn", P, G, C)
        wab, a_log, dt = sb("wab", P, 2 * HEADS), sb("a_log", P, HEADS), sb("dt", P, HEADS)
        ab = sb("ab", P, TILES, 2 * HEADS)
        z, nz, lz, eb = (sb(n, P, TILES, HEADS) for n in ("z", "nz", "lz", "eb"))
        tp = [ctx.enter_context(nc.psum_tensor(f"b0_tp{n}", [P, 512], F32)) for n in range(2)]
        ap = ctx.enter_context(nc.psum_tensor("b0_ap", [P, 512], F32))
        gp = [ctx.enter_context(nc.psum_tensor(f"b0_gp{n}", [P, 512], F32)) for n in range(3)]
        loaded, zeroed = signal("loaded"), signal("zeroed")
        bn_done, aggr_done, var_ready, root_ready, rstd_ready, xn_ready = (
            signal(n, p) for n, p in (("bn", 8), ("aggr", 8), ("var", 1), ("root", 1), ("rstd", 1), ("xn_ready", 8)))
        tp_full, tp_read, ab_full, ab_read = signal("tp_full", 2), signal("tp_read", 2), signal("ab_full"), signal("ab_read")
        step, nz_ready, exps, a_ready, g_ready, sums_full, decays = (signal(n) for n in ("step", "nz_ready", "exps", "a_ready", "g_ready", "sums_full", "decays"))
        lz_ready = signal("lz_ready")
        block = ctx.enter_context(nc.Block())

        @block.sync
        def _(sp):
            sp.dma_start(wab[:, 0:HEADS], w["Wa"]).then_inc(loaded.sem, 16)
            sp.dma_start(wab[:, HEADS:2 * HEADS], w["Wb"]).then_inc(loaded.sem, 16)
            sp.dma_start(a_log[:, :], w["A_log"].partition_broadcast(P)).then_inc(loaded.sem, 16)
            sp.dma_start(dt[:, :], w["dt_bias"].partition_broadcast(P)).then_inc(loaded.sem, 16)

        @block.gpsimd
        def _(pool):
            pool.memset(xT[:, :, 0:TAPS - 1], 0.0).then_inc(zeroed.sem, 1)

        @block.vector
        def _(dve):
            for g in range(BATCHES):
                if g:
                    xn_ready.wait(dve, g, 0)
                for j in range(G):
                    dve.bn_stats(stats[:, j, :], x_sb[:, (G * g + j) * C:(G * g + j + 1) * C]).then_inc(bn_done.sem, 1)
                bn_done.wait(dve, g, 8)
                for j in range(G):
                    dve.bn_aggr(moments[:, j, :], stats[:, j, :]).then_inc(aggr_done.sem, 1)
                aggr_done.wait(dve, g, 8)
                dve.tensor_scalar(rstd[:, :], moments[:, :, 1], EPS_LN, None, ALU.add).then_inc(var_ready.sem, 1)
                root_ready.wait(dve, g, 1)
                dve.reciprocal(rstd[:, :], rstd[:, :]).then_inc(rstd_ready.sem, 1)
                rstd_ready.wait(dve, g, 1)
                tp_full.wait(dve, g, 0)
                for j in range(G):
                    dve.tensor_scalar(xn[:, j, :], x_sb[:, (G * g + j) * C:(G * g + j + 1) * C], moments[:, j, 0:1],
                                      rstd[:, j:j + 1], ALU.subtract, ALU.mult).then_inc(xn_ready.sem, 1)
            steps = [0]

            def then(ins):
                steps[0] += 1
                ins.then_inc(step.sem, 1)
                dve.wait_ge(step.sem, steps[0])

            loaded.wait(dve, 0, 64)
            ab_read.wait(dve, BATCHES, 0)
            then(dve.tensor_tensor(z[:, :, :], ab[:, :, 0:HEADS], wide(dt[:, :], 1, [P, TILES, HEADS]), ALU.add))
            then(dve.tensor_scalar(nz[:, :, :], z[:, :, :], -1.0, None, ALU.mult))
            dve.tensor_tensor(nz[:, :, :], nz[:, :, :], z[:, :, :], ALU.min).then_inc(nz_ready.sem, 1)
            lz_ready.wait(dve, 0, 1)
            then(dve.tensor_scalar(z[:, :, :], z[:, :, :], 0.0, None, ALU.max))
            then(dve.tensor_tensor(z[:, :, :], z[:, :, :], lz[:, :, :], ALU.add))
            a_ready.wait(dve, 0, 1)
            then(dve.tensor_tensor(z[:, :, :], z[:, :, :], wide(a_log[:, :], 1, [P, TILES, HEADS]), ALU.mult))
            dve.tensor_scalar(prm[:, :, G_, :], z[:, :, :], -1.0, None, ALU.mult).then_inc(g_ready.sem, 1)
            exps.wait(dve, 0, 2)
            then(dve.tensor_scalar(eb[:, :, :], eb[:, :, :], 1.0, None, ALU.add))
            then(dve.reciprocal(eb[:, :, :], eb[:, :, :]))
            then(dve.tensor_scalar(prm[:, :, BETA, :], eb[:, :, :], 2.0, None, ALU.mult))
            decays.wait(dve, 0, 3)
            then(dve.memset(prm[:, :, GAMMA_END:DECAY_END + 1, :].rearrange("p (b c) a h -> p b c a h", c=TPB)[:, :, TPB - 1], 0.0))

        @block.scalar
        def _(act):
            for g in range(BATCHES):
                var_ready.wait(act, g, 1)
                act.activation(rstd[:, :], rstd[:, :], ACT.Sqrt).then_inc(root_ready.sem, 1)
                for h in range(2):
                    tp_full.wait(act, g, h + 1)
                    act.activation(xT[:, g, TAPS - 1 + 512 * h:TAPS - 1 + 512 * h + 512], tp[h][:, :], ACT.Copy).then_inc(tp_read.sem, 1)
                ab_full.wait(act, g, 1)
                act.activation(ab[:, G * g:G * g + G, :].rearrange("p a b -> p (a b)"), ap[:, 0:128], ACT.Copy).then_inc(ab_read.sem, 1)
            loaded.wait(act, 0, 64)
            act.activation(a_log[:, :], a_log[:, :], ACT.Exp).then_inc(a_ready.sem, 1)
            nz_ready.wait(act, 0, 1)
            act.activation(nz[:, :, :], nz[:, :, :], ACT.Exp).then_inc(exps.sem, 1)
            ab_read.wait(act, BATCHES, 0)
            act.activation(eb[:, :, :], ab[:, :, HEADS:2 * HEADS], ACT.Exp, scale=-1.0).then_inc(exps.sem, 1)
            exps.wait(act, 0, 1)
            act.activation(lz[:, :, :], nz[:, :, :], ACT.Ln, bias=1.0).then_inc(lz_ready.sem, 1)
            sums_full.wait(act, 0, 1)
            for n, which in enumerate((GAMMA, GAMMA_END, DECAY_END)):
                act.activation(prm[:, :, which, :], gp[n][:, 0:256].rearrange("p (a b) -> p a b", b=HEADS), ACT.Exp).then_inc(decays.sem, 1)

        @block.tensor
        def _(pe):
            loaded.wait(pe, 0, 64)
            for g in range(BATCHES):
                for h in range(2):
                    xn_ready.wait(pe, g, 4 * h + 4)
                    if g:
                        tp_read.wait(pe, g - 1, h + 1)
                    for j in range(4):
                        mm = pe.transpose(tp[h][:, P * j:P * j + P], xn[:, 4 * h + j, :], k["ident"][:, :])
                    mm.then_inc(tp_full.sem, 1)
                tp_read.wait(pe, g, 2)
                ab_read.wait(pe, g, 0)
                for j in range(G):
                    mm = pe.matmul(ap[:, 16 * j:16 * j + 16], xT[:, g, TAPS - 1 + P * j:TAPS - 1 + P * j + P], wab[:, :], start=True, stop=True)
                mm.then_inc(ab_full.sem, 1)
            g_ready.wait(pe, 0, 1)
            for n, m in enumerate(("upto", "ones", "after")):
                mm = pe.matmul(gp[n][:, 0:256], k[m][:, :], prm[:, :, G_, :], start=True, stop=True)
            mm.then_inc(sums_full.sem, 1)


def delta_chunks(nc, k, w, xT, prm, o_dram):
    with ExitStack() as ctx:
        def sb(n, *shape, dt=F32):
            return ctx.enter_context(nc.sbuf_tensor("b1_" + n, list(shape), dt))

        def psum(n):
            return ctx.enter_context(nc.psum_tensor("b1_" + n, [P, 512], F32))

        def signal(n, per=1):
            return Signal(nc.alloc_semaphore("b1_" + n), per)

        NL_ = len(LEVELS)
        PASSES = TILES // 2
        STATE = 3 * NL_ + 1
        SLOTS = STATE + 6
        PAIRS_, K_T, Q_T, V_T, E_ = BLOCKS // 2, 3, 7, 10, STATE
        ORDER = (0, 2, 1, 3)
        wq, wk, wv = sb("wq", P, HEADS * KD), sb("wk", P, HEADS * KD), sb("wv", P, HEADS * VD)
        taps = sb("taps", P, BLOCKS, TAPS)
        masks = [sb(f"mask{s}", P, 64) for s in LEVELS]
        mask1 = sb("mask1", P, P)
        W_EXT = TAPS - 1 + P
        PRE = 4
        xh, vT = sb("xh", P, 2, W_EXT), sb("vT", P, 2, 2, P)
        cur_ = [sb(f"cur{e}", P, 2, 5, HEADS) for e in range(2)]
        pre = [sb(f"pre{n}", P, 2, P) for n in range(PRE)]
        kq_ = [sb(f"kq{e}", P, 2, HEADS, 2, P) for e in range(2)]
        sq = [sb(f"sq{n}", P, 4, P) for n in range(2)]
        norm_, rnorm_ = ([sb(f"{n}{e}", P, 2, 2, HEADS) for e in range(2)] for n in ("norm", "rnorm"))
        s__ = [sb(f"s_{e}", P, 2, HEADS) for e in range(2)]
        nv_ = [sb(f"nv{e}", P, 2, 2, 4 * VD) for e in range(2)]
        gm = [sb(f"gm{n}", P, 4, P) for n in range(2)]
        kt_, CT_, PT_, XT_ = ([[sb(f"{n}{e}{q}", P, 4, P) for q in range(QUADS)] for e in range(2)] for n in ("kt", "CT", "PT", "XT"))
        D, X = ([sb(f"{n}{q}", P, 4, P) for q in range(QUADS)] for n in ("D", "X"))
        W = [sb(f"W{q}", P, 4, 64) for q in range(QUADS)]
        S = sb("S", P, QUADS, 4 * VD)
        r, z, wd, o1 = ([sb(f"{n}{q}", P, 4, VD) for q in range(QUADS)] for n in ("r", "z", "wd", "o1"))
        ob = sb("ob", P, QUADS, 4 * VD)
        pj, mx, lv = [psum(f"pj{n}") for n in range(2)], [psum(f"mx{n}") for n in range(2)], [psum(f"lv{q}") for q in range(QUADS)]

        loaded, zeroed, masked, reset = signal("loaded"), signal("zeroed"), signal("masked"), signal("reset")
        alone, pe_alone = signal("alone"), signal("pe_alone")
        xh_ready, cur_part, cur_ready = signal("xh_ready"), signal("cur_part"), signal("cur_ready")
        pj_full, tap_done, tap_next, conv_done, silu_done = (
            signal(n, p * BLOCKS) for n, p in (("pj_full", 1), ("tap_done", 1), ("tap_next", 2), ("conv_done", 1), ("silu_done", 1)))
        squared, n2_ready, n_root, n_step = (
            signal(n, p) for n, p in (("squared", 2 * QUADS), ("n2_ready", 2 * QUADS), ("n_root", 1), ("n_step", 4)))
        v_full, nv_ready = signal("v_full"), signal("nv_ready", 2)
        kt_full, kt_ready, qt_full, gm_ready, e_full, d_ready, kq_full, ct_ready, pt_ready, pt_masked, x1_part, x1_ready, x_full, x_ready = (
            signal(n, QUADS) for n in ("kt_full", "kt_ready", "qt_full", "gm_ready", "e_full", "d_ready", "kq_full", "ct_ready", "pt_ready",
                                       "pt_masked", "x1_part", "x1_ready", "x_full", "x_ready"))
        half_ready = signal("half_ready")
        w_full, w_ready, dx_full, dx_added, t_full, xt_ready = (
            signal(n, NL_ * QUADS) for n in ("w_full", "w_ready", "dx_full", "dx_added", "t_full", "xt_ready"))
        s_full, rg_ready, r_ready, qs_ready, z_full, z_ready, wd_ready, sg_ready, pw_full, o_sum, s_done, o_done = (
            signal(n, QUADS) for n in ("s_full", "rg_ready", "r_ready", "qs_ready", "z_full", "z_ready", "wd_ready", "sg_ready", "pw_full",
                                       "o_sum", "s_done", "o_done"))
        stored = signal("stored", 32)

        def flat(ap):
            return ap.rearrange("p a b -> p (a b)")

        def halves(ap, s, which):
            return ap.rearrange("p h (b t s) -> p h b t s", t=2, s=s)[:, :, :, which, :]

        def rows(l):
            return P // 2 if l == NL_ - 1 else P

        def quad(q):
            return q // 2, slice(4 * (q % 2), 4 * (q % 2) + 4)

        def run(eng, front, back):
            def beside(n, e):
                for slot in range(SLOTS):
                    back(n, e, slot)
                    front(n + 1, 1 - e, slot)
            for slot in range(SLOTS):
                front(0, 0, slot)
            beside(0, 0)
            with eng.Fori(0, (PASSES - 2) // 2) as two:
                beside(two * 2 + 1, 1)
                beside(two * 2 + 2, 0)
            for slot in range(SLOTS):
                back(PASSES - 1, 1, slot)

        o_rows = o_dram.rearrange("(b c p) v -> p b c v", p=P, c=TPB)
        block = ctx.enter_context(nc.Block())

        @block.sync
        def _(sp):
            sp.dma_start(wk[:, :], w["Wk"]).then_inc(loaded.sem, 16)
            sp.dma_start(wq[:, :], w["Wq"]).then_inc(loaded.sem, 16)
            sp.dma_start(wv[:, :], w["Wv"]).then_inc(loaded.sem, 16)
            for n, name in ((0, "conv_k"), (HEADS, "conv_q")):
                sp.dma_start(taps[:, n:n + HEADS, :], w[name].rearrange("(h p) t -> p h t", p=P)).then_inc(loaded.sem, 16)
            sp.dma_start(taps[:, 2 * HEADS:, :], w["conv_v"].rearrange("(h p) t -> p h t", p=P)).then_inc(loaded.sem, 16)
            with sp.Fori(0, PASSES // TPB) as pair, sp.Fori(0, TPB) as c:
                o_done.wait(sp, pair * TPB + c, QUADS)
                for i in range(2):
                    sp.dma_start(o_rows[:, bass.ds(pair * 2 + i, 1), bass.ds(c, 1), :].rearrange("p b c v -> p (b c v)"),
                                 flat(ob[:, 2 * i:2 * i + 2, :])).then_inc(stored.sem, 16)
            stored.wait(sp, PASSES, 0)

        @block.gpsimd
        def _(pool):
            for m in masks:
                pool.memset(m[:, :], -1.0).then_inc(zeroed.sem, 1)
            pool.memset(mask1[:, :], 0.0).then_inc(zeroed.sem, 1)
            pool.wait_ge(zeroed.sem, NL_ + 1)
            for l, (s, m) in enumerate(zip(LEVELS, masks)):
                v = m[:, :].rearrange("p (b s) -> p b s", s=s)
                first, apart = (s, 2 * s) if rows(l) == P else (0, s)
                pool.affine_select(out=v, in_=v, compare_op=ALU.is_ge, fill=0.0, base=-first, pattern=[[-apart, 64 // s], [0, s]],
                                   channel_multiplier=1).then_inc(masked.sem, 1)
            v = mask1[:, :].rearrange("p (a t) -> p a t", t=2)[:, :, 1]
            pool.affine_select(out=v, in_=v, compare_op=ALU.not_equal, fill=-1.0, base=0, pattern=[[2, 64]],
                               channel_multiplier=-1).then_inc(masked.sem, 1)
            pool.wait_ge(masked.sem, NL_ + 1)
            for l, (s, m) in enumerate(zip(LEVELS, masks)):
                v = m[:, :].rearrange("p (b s) -> p b s", s=s)
                first, apart = (s, 2 * s) if rows(l) == P else (0, s)
                pool.affine_select(out=v, in_=v, compare_op=ALU.is_ge, fill=0.0, base=first + s - 1, pattern=[[apart, 64 // s], [0, s]],
                                   channel_multiplier=-1).then_inc(masked.sem, 1)

            def front(m, e, slot):
                cur, CT, PT, XT = cur_[e], CT_[e], PT_[e], XT_[e]

                def build(q):
                    i, hs = quad(q)
                    e_full.wait(pool, m - 1 if q < 2 else m, q + 3 if q < 2 else q - 1)
                    pool.tensor_tensor(gm[q % 2][:, :, :], wide(k["upto"][:, :], 1, [P, 4, P]), wide(cur[:, i, G_, hs], 2, [P, 4, P]),
                                       ALU.mult).then_inc(gm_ready.sem, 1)
                if slot == 0:
                    cur_ready.wait(pool, m, 1)
                    build(0)
                    build(1)
                for q in range(QUADS):
                    if slot == E_ + 1 + q:
                        if q + 2 < QUADS:
                            build(q + 2)
                        ct_ready.wait(pool, m, q + 1)
                        z_full.wait(pool, m - 2, QUADS)
                        pool.tensor_tensor(XT[q][:, :, :], CT[q][:, :, :], wide(mask1[:, :], 1, [P, 4, P]), ALU.mult).then_inc(x1_part.sem, 1)
                        x1_part.wait(pool, m, q + 1)
                        pool.tensor_tensor(XT[q][:, :, :], XT[q][:, :, :], wide(k["ident"][:, :], 1, [P, 4, P]), ALU.add).then_inc(x1_ready.sem, 1)
                        pt_ready.wait(pool, m, q + 1)
                        pool.tensor_tensor(PT[q][:, :, :], PT[q][:, :, :], wide(k["upto"][:, :], 1, [P, 4, P]), ALU.mult).then_inc(pt_masked.sem, 1)

            def back(n, e, slot):
                pass
            run(pool, front, back)

        @block.scalar
        def _(act):
            loaded.wait(act, 0, 96)

            def tokens(m):
                pj_full.wait(act, m - 1, BLOCKS)
                act.activation(xh[:, :, :], xT[:, bass.ds((m // TPB) * 2, 2), bass.ds((m % TPB) * P, W_EXT)], ACT.Copy).then_inc(xh_ready.sem, 1)

            def front(m, e, slot):
                kq, norm, kt = kq_[e], norm_[e], kt_[e]

                def silu(b):
                    conv_done.wait(act, m, b + 1)
                    if b == 0:
                        s_full.wait(act, m - 2, QUADS)
                    if b == 2 * HEADS:
                        v_full.wait(act, m - 1, 1)
                    act.activation(kq[:, :, b % HEADS, b // HEADS, :] if b < 2 * HEADS else vT[:, :, b - 2 * HEADS, :],
                                   pre[b % PRE][:, :, :], ACT.Silu).then_inc(silu_done.sem, 1)
                if slot < PAIRS_:
                    for b in (2 * slot, 2 * slot + 1):
                        pj_full.wait(act, m, b + 1)
                        silu_done.wait(act, m - 1 if b < PRE else m, BLOCKS if b < PRE else b - PRE + 1)
                        act.activation(pre[b % PRE][:, :, :], pj[b % 2][:, 0:2 * W_EXT].rearrange("p (i t) -> p i t", i=2)[:, :, 0:P],
                                       ACT.Copy, scale=taps[:, b, 0:1]).then_inc(tap_done.sem, 1)
                if 0 < slot <= PAIRS_:
                    silu(2 * slot - 2)
                    silu(2 * slot - 1)
                def square(u, bank):
                    n2_ready.wait(act, m - 1 if u < 2 else m, 2 * QUADS - 1 + u if u < 2 else u - 1)
                    act.activation(flat(sq[u % 2][:, :, :]), bank[:, :], ACT.Square).then_inc(squared.sem, 1)

                if slot == E_:
                    n2_ready.wait(act, m, 2 * QUADS)
                    act.activation(norm[:, :, :, :], norm[:, :, :, :], ACT.Sqrt).then_inc(n_root.sem, 1)
                for u, q in enumerate(ORDER):
                    if slot == K_T + u:
                        kt_full.wait(act, m, u + 1)
                        pw_full.wait(act, m - 2, QUADS)
                        act.activation(flat(kt[q][:, :, :]), mx[1][:, :], ACT.Copy).then_inc(kt_ready.sem, 1)
                        square(u, mx[1])
                    if slot == Q_T + u:
                        qt_full.wait(act, m, u + 1)
                        square(QUADS + u, mx[0])
                for q in range(QUADS):
                    if slot == E_ + q:
                        e_full.wait(act, m, q + 1)
                        pt_ready.wait(act, m - 1, q + 1)
                        act.activation(flat(D[q][:, :, :]), mx[0][:, :], ACT.Exp).then_inc(d_ready.sem, 1)

            def back(n, e, slot):
                if slot == 0 and not (isinstance(n, int) and n == PASSES - 1):
                    tokens(n + 1)
                for q in range(QUADS):
                    if slot == 0:
                        x_full.wait(act, n, q + 1)
                        act.activation(flat(X[q][:, :, :]), lv[q][:, :], ACT.Copy).then_inc(x_ready.sem, 1)
                    elif slot < STATE and slot % 3 == 0:
                        t_full.wait(act, n, QUADS * (slot // 3 - 1) + q + 1)
                        l = slot // 3
                        part = rows(l) if l < NL_ else P
                        act.activation(flat(XT_[e][q][0:part, :, :]), lv[q][0:part, :], ACT.Copy).then_inc(xt_ready.sem, 1)
            tokens(0)
            run(act, front, back)

        @block.vector
        def _(dve):
            dve.memset(S[:, :, :], 0.0).then_inc(reset.sem, 1)
            reset.wait(dve, 0, 1)
            loaded.wait(dve, 0, 96)
            dve.wait_ge(masked.sem, 2 * NL_ + 1)

            def front(m, e, slot):
                cur, norm, rnorm, s_, nv, CT, PT = cur_[e], norm_[e], rnorm_[e], s__[e], nv_[e], CT_[e], PT_[e]
                if slot == 0:
                    o_done.wait(dve, m - 2, QUADS)
                    s_done.wait(dve, m - 2, QUADS)
                    dve.sem_inc(alone.sem, 1)
                    for i in range(2):
                        dve.tensor_copy(cur[:, i, :, :].rearrange("p a b -> p (a b)"),
                                        prm[:, :, :, :].rearrange("p t a b -> p t (a b)")[:, bass.ds((m // TPB) * (2 * TPB) + m % TPB + i * TPB, 1), :].rearrange("p t a -> p (t a)")).then_inc(
                            cur_part.sem if i == 0 else cur_ready.sem, 1)
                if slot < PAIRS_:
                    for t in range(1, TAPS):
                        for b in (2 * slot, 2 * slot + 1):
                            if t == 1:
                                tap_done.wait(dve, m, b + 1)
                            else:
                                tap_next.wait(dve, m, 4 * slot + 2 * (t - 2) + b % 2 + 1)
                            src = pj[b % 2][:, 0:2 * W_EXT].rearrange("p (i t) -> p i t", i=2)
                            dve.scalar_tensor_tensor(pre[b % PRE][:, :, :], src[:, :, t:t + P], taps[:, b, t:t + 1], pre[b % PRE][:, :, :],
                                                     ALU.mult, ALU.add).then_inc((conv_done if t == TAPS - 1 else tap_next).sem, 1)
                for u, q in enumerate(ORDER * 2):
                    if slot == K_T + 1 + u:
                        i, hs = quad(q)
                        squared.wait(dve, m, u + 1)
                        dve.tensor_reduce(norm[:, u // QUADS, i, hs], sq[u % 2][:, :, :], AX.X, ALU.add).then_inc(n2_ready.sem, 1)
                if slot == E_ + 1:
                    n_root.wait(dve, m, 1)
                    dve.tensor_scalar(norm[:, :, :, :], norm[:, :, :, :], EPS_NORM, None, ALU.max).then_inc(n_step.sem, 1)
                    n_step.wait(dve, m, 1)
                    dve.reciprocal(rnorm[:, :, :, :], norm[:, :, :, :]).then_inc(n_step.sem, 1)
                    v_full.wait(dve, m, 1)
                    for i in range(2):
                        dve.tensor_tensor(nv[:, i, :, :].rearrange("p a (h d) -> p (a h) d", d=VD), mx[1][:, 256 * i:256 * i + 256].rearrange("p (h d) -> p h d", d=VD),
                                          wide(norm[:, 0, i, :], 2, [P, HEADS, VD]), ALU.mult).then_inc(nv_ready.sem, 1)
                    n_step.wait(dve, m, 2)
                    dve.tensor_tensor(s_[:, :, :], rnorm[:, 0, :, :], rnorm[:, 0, :, :], ALU.mult).then_inc(n_step.sem, 1)
                    n_step.wait(dve, m, 3)
                    dve.tensor_tensor(s_[:, :, :], s_[:, :, :], cur[:, :, BETA, :], ALU.mult).then_inc(n_step.sem, 1)
                for q in range(QUADS):
                    i, hs = quad(q)
                    if slot == E_ + 1 + q:
                        n_step.wait(dve, m, 4)
                        d_ready.wait(dve, m, q + 1)
                        kq_full.wait(dve, m, q + 1)
                        both = [pj[g][:, :].rearrange("p (h m t) -> p h m t", h=2, m=2) for g in range(2)]
                        for h in range(4):
                            dve.scalar_tensor_tensor(CT[q][:, h, :], both[h // 2][:, h % 2, 0, :], s_[:, i, hs][:, h:h + 1], D[q][:, h, :],
                                                     ALU.mult, ALU.mult).then_inc((ct_ready if h == 3 else half_ready).sem, 1)
                        for g in range(2):
                            sl = slice(2 * g, 2 * g + 2)
                            dve.tensor_tensor(PT[q][:, sl, :], both[g][:, :, 1, :], D[q][:, sl, :], ALU.mult).then_inc((pt_ready if g else half_ready).sem, 1)

            def back(n, e, slot):
                cur, rnorm, s_, nv = cur_[e], rnorm_[e], s__[e], nv_[e]
                if 0 < slot < STATE and slot % 3 != 0:
                    l = slot // 3
                    s = LEVELS[l]
                    for q in range(QUADS):
                        if slot % 3 == 1:
                            w_full.wait(dve, n, QUADS * l + q + 1)
                            part = rows(l)
                            dve.tensor_tensor(W[q][0:part, :, :], lv[q][0:part, 0:256].rearrange("p (h c) -> p h c", h=4),
                                              wide(masks[l][0:part, :], 1, [part, 4, 64]), ALU.mult).then_inc(w_ready.sem, 1)
                        else:
                            dx_full.wait(dve, n, QUADS * l + q + 1)
                            v = halves(X[q][:, :, :], s, 0)
                            dve.tensor_tensor(v, v, lv[q][:, 256:512].rearrange("p (h b s) -> p h b s", h=4, s=s), ALU.add).then_inc(dx_added.sem, 1)
                if slot == STATE:
                    o_done.wait(dve, n - 1, QUADS)
                    s_done.wait(dve, n - 1, QUADS)
                if slot == STATE + 4:
                    stored.wait(dve, n - 1, 32)
                for q in range(QUADS):
                    i, hs = quad(q)

                    def per_token(ap):
                        return wide(ap, 2, [P, 4, VD])

                    def per_head(ap):
                        return ap.rearrange("p (h d) -> p h d", d=VD)

                    if slot == STATE + q // 2:
                        s_full.wait(dve, n, q + 1)
                        dve.tensor_tensor(r[q][:, :, :], per_head(lv[q][:, 0:P]), per_token(cur[:, i, GAMMA, hs]), ALU.mult).then_inc(rg_ready.sem, 1)
                        dve.tensor_tensor(o1[q][:, :, :], per_head(lv[q][:, P:2 * P]), per_token(cur[:, i, GAMMA, hs]), ALU.mult).then_inc(qs_ready.sem, 1)
                        rg_ready.wait(dve, n, q + 1)
                        dve.tensor_tensor(r[q][:, :, :], per_head(nv[:, i, q % 2, :]), r[q][:, :, :], ALU.subtract).then_inc(r_ready.sem, 1)
                    if slot == STATE + 2 + q // 2:
                        z_full.wait(dve, n, q + 1)
                        dve.tensor_tensor(z[q][:, :, :], per_head(lv[q][:, 0:P]), per_token(s_[:, i, hs]), ALU.mult).then_inc(z_ready.sem, 1)
                        dve.tensor_tensor(per_head(S[:, q, :]), per_head(S[:, q, :]), per_token(cur[:, i, GAMMA_END, hs]), ALU.mult).then_inc(sg_ready.sem, 1)
                        z_ready.wait(dve, n, q + 1)
                        dve.tensor_tensor(wd[q][:, :, :], z[q][:, :, :], per_token(cur[:, i, DECAY_END, hs]), ALU.mult).then_inc(wd_ready.sem, 1)
                    if slot == STATE + 4 + q // 2:
                        pw_full.wait(dve, n, q + 1)
                        sg_ready.wait(dve, n, q + 1)
                        qs_ready.wait(dve, n, q + 1)
                        dve.tensor_tensor(o1[q][:, :, :], o1[q][:, :, :], per_head(lv[q][:, P:2 * P]), ALU.add).then_inc(o_sum.sem, 1)
                        dve.tensor_tensor(S[:, q, :], S[:, q, :], lv[q][:, 2 * P:3 * P], ALU.add).then_inc(s_done.sem, 1)
                        o_sum.wait(dve, n, q + 1)
                        dve.tensor_tensor(per_head(ob[:, q, :]), o1[q][:, :, :], per_token(rnorm[:, 1, i, hs]), ALU.mult).then_inc(o_done.sem, 1)
            run(dve, front, back)

        @block.tensor
        def _(pe):
            loaded.wait(pe, 0, 96)
            reset.wait(pe, 0, 1)

            def front(m, e, slot):
                kq = kq_[e]

                def weights(b):
                    src = wk if b < HEADS else wq if b < 2 * HEADS else wv
                    return src[:, (b % HEADS) * P:(b % HEADS) * P + P]

                if slot == 0:
                    xh_ready.wait(pe, m, 1)
                    pt_ready.wait(pe, m - 1, QUADS)
                if slot < PAIRS_:
                    for b in (2 * slot, 2 * slot + 1):
                        if b >= 2:
                            conv_done.wait(pe, m, b - 1)
                        pe.matmul(pj[b % 2][:, 0:2 * W_EXT], weights(b), flat(xh[:, :, :]), start=True, stop=True).then_inc(pj_full.sem, 1)
                if slot == V_T:
                    silu_done.wait(pe, m, BLOCKS)
                    squared.wait(pe, m, QUADS)
                    for i in range(2):
                        for hq in range(2):
                            mm = pe.transpose(mx[1][:, 256 * i + P * hq:256 * i + P * hq + P], vT[:, i, hq, :], k["ident"][:, :])
                    mm.then_inc(v_full.sem, 1)
                for u, q in enumerate(ORDER):
                    i, hq = q // 2, q % 2
                    if slot == K_T + u:
                        silu_done.wait(pe, m, 4 * hq + 4)
                        if u == 0:
                            nv_ready.wait(pe, m - 1, 2)
                        else:
                            squared.wait(pe, m, u)
                        for h in range(4):
                            mm = pe.transpose(mx[1][:, P * h:P * h + P], kq[:, i, 4 * hq + h, 0, :], k["ident"][:, :])
                        mm.then_inc(kt_full.sem, 1)
                    if slot == Q_T + u:
                        silu_done.wait(pe, m, HEADS + 4 * hq + 4)
                        if u == 0:
                            d_ready.wait(pe, m - 1, QUADS)
                        else:
                            squared.wait(pe, m, QUADS + u)
                        for h in range(4):
                            mm = pe.transpose(mx[0][:, P * h:P * h + P], kq[:, i, 4 * hq + h, 1, :], k["ident"][:, :])
                        mm.then_inc(qt_full.sem, 1)
                for q in range(QUADS):
                    i, hq = q // 2, q % 2
                    if slot == E_ + q:
                        gm_ready.wait(pe, m, q + 1)
                        if q:
                            d_ready.wait(pe, m, q)
                        else:
                            squared.wait(pe, m, 2 * QUADS)
                        pe.matmul(mx[0][:, :], k["after"][:, :], flat(gm[q % 2][:, :, :]), start=True, stop=True).then_inc(e_full.sem, 1)
                    if slot == E_ + 1 + q:
                        if q:
                            pt_ready.wait(pe, m, q)
                        else:
                            conv_done.wait(pe, m, BLOCKS)
                        for h in range(4):
                            mm = pe.matmul(pj[h // 2][:, 256 * (h % 2):256 * (h % 2) + 256], kq[:, i, 4 * hq + h, 0, :],
                                           kq[:, i, 4 * hq + h, :, :].rearrange("p m t -> p (m t)"), start=True, stop=True)
                        mm.then_inc(kq_full.sem, 1)

            def back(n, e, slot):
                kq, kt, CT, PT, XT = kq_[e], kt_[e], CT_[e], PT_[e], XT_[e]
                l = (slot - 1) // 3
                for q in range(QUADS):
                    i, hq = q // 2, q % 2
                    if slot == 0:
                        x1_ready.wait(pe, n, q + 1)
                        o_done.wait(pe, n - 1, q + 1)
                        s_done.wait(pe, n - 1, q + 1)
                        for h in range(4):
                            mm = pe.transpose(lv[q][:, P * h:P * h + P], XT[q][:, h, :], k["ident"][:, :])
                        mm.then_inc(x_full.sem, 1)
                    elif slot < STATE and slot % 3 == 1:
                        x_ready.wait(pe, n, q + 1)
                        if l:
                            xt_ready.wait(pe, n, QUADS * (l - 1) + q + 1)
                        for h in range(4):
                            mm = pe.matmul(lv[q][0:rows(l), 64 * h:64 * h + 64], CT[q][:, h, P - rows(l):P], halves(X[q][:, :, :], LEVELS[l], 0)[:, h], start=True, stop=True)
                        mm.then_inc(w_full.sem, 1)
                    elif slot < STATE and slot % 3 == 2:
                        w_ready.wait(pe, n, QUADS * l + q + 1)
                        for h in range(4):
                            mm = pe.matmul(lv[q][:, 256 + 64 * h:256 + 64 * h + 64], XT[q][0:rows(l), h, :], W[q][0:rows(l), h, :], start=True, stop=True)
                        mm.then_inc(dx_full.sem, 1)
                    elif slot < STATE:
                        dx_added.wait(pe, n, QUADS * l + q + 1)
                        pe.sem_inc(pe_alone.sem, 1)
                        for h in range(4):
                            part = rows(l + 1) if l + 1 < NL_ else P
                            mm = pe.transpose(lv[q][0:part, P * h:P * h + P], X[q][:, h, P - part:P], k["ident"][:, :])
                        mm.then_inc(t_full.sem, 1)
                    elif slot == STATE + q // 2:
                        xt_ready.wait(pe, n, QUADS * (NL_ - 1) + q + 1)
                        for part in range(2):
                            for h in range(4):
                                mm = pe.matmul(lv[q][:, P * part + VD * h:P * part + VD * h + VD], kq[:, i, 4 * hq + h, part, :], S[:, q, VD * h:VD * h + VD], start=True, stop=True)
                        mm.then_inc(s_full.sem, 1)
                    elif slot == STATE + 2 + q // 2:
                        r_ready.wait(pe, n, q + 1)
                        for h in range(4):
                            mm = pe.matmul(lv[q][:, VD * h:VD * h + VD], XT[q][:, h, :], r[q][:, h, :], start=True, stop=True)
                        mm.then_inc(z_full.sem, 1)
                    elif slot == STATE + 4 + q // 2:
                        wd_ready.wait(pe, n, q + 1)
                        pt_masked.wait(pe, n, q + 1)
                        for h in range(4):
                            pe.matmul(lv[q][:, P + VD * h:P + VD * h + VD], PT[q][:, h, :], z[q][:, h, :], start=True, stop=True)
                            mm = pe.matmul(lv[q][:, 2 * P + VD * h:2 * P + VD * h + VD], kt[q][:, h, :], wd[q][:, h, :], start=True, stop=True)
                        mm.then_inc(pw_full.sem, 1)
            run(pe, front, back)


def delta_output(nc, k, x_sb, w, xT, o_dram):
    with ExitStack() as ctx:
        def sb(n, *shape, dt=F32):
            return ctx.enter_context(nc.sbuf_tensor("b2_" + n, list(shape), dt))

        def psum(n, width):
            return ctx.enter_context(nc.psum_tensor("b2_" + n, [P, width], F32))

        def signal(n, per=1):
            return Signal(nc.alloc_semaphore("b2_" + n), per)

        G, V = 4, HEADS * VD
        PASSES = TILES // G
        wg, wo, nw = sb("wg", P, V), sb("wo", P, 2, C), sb("nw", P, VD)
        o, sq_, xs, gate = sb("o", P, G, V), sb("sq", P, G, V), sb("xs", P, G * P), sb("gate", P, G * V)
        ms = sb("ms", P, G * HEADS)
        oT = sb("oT", P, G, 2, P)
        gp, tp, xp = psum("gp", 1024), psum("tp", 1024), psum("xp", 512)
        loaded, o_in, xs_ready, g_full, gated, squared, ms_step, rooted, o_step, oT_full, oT_read, p_full, x_done = (
            signal(n, p) for n, p in (("loaded", 1), ("o_in", 16), ("xs_ready", 1), ("g_full", 1), ("gated", 1), ("squared", 1), ("ms_step", 3),
                                      ("rooted", 1), ("o_step", 3), ("oT_full", 1), ("oT_read", 1), ("p_full", 1), ("x_done", 4)))
        for s in (oT_full, g_full, gated, oT_read, x_done):
            s.with_credit()
        o_rows = o_dram.rearrange("(g t p) v -> g p t v", p=P, t=G)
        block = ctx.enter_context(nc.Block())

        @block.sync
        def _(sp):
            sp.dma_start(wg[:, :], w["Wg"]).then_inc(loaded.sem, 16)
            sp.dma_start(wo[:, :, :], w["Wo"].rearrange("(h v) c -> v h c", v=P)).then_inc(loaded.sem, 16)
            sp.dma_start(nw[:, :], w["o_norm_w"].partition_broadcast(P)).then_inc(loaded.sem, 16)
            with sp.Fori(0, PASSES) as n:
                oT_full.wait(sp, n, 0)
                sp.dma_start(o[:, :, :], o_rows[bass.ds(n, 1)].rearrange("g p t v -> p (g t) v")).then_inc(o_in.sem, 16)

        @block.gpsimd
        def _(pool):
            with pool.Fori(0, PASSES) as n:
                o_in.wait(pool, n, 16)
                pool.tensor_tensor(sq_[:, :, :], o[:, :, :], o[:, :, :], ALU.mult).then_inc(squared.sem, 1)

        @block.scalar
        def _(act):
            gated.open(act)
            oT_read.open(act)
            with act.Fori(0, BATCHES) as b, act.Fori(0, 2) as half:
                n = b * 2 + half
                g_full.wait(act, n, 0)
                act.activation(xs[:, :], xT[:, bass.ds(b, 1), bass.ds(half * (G * P) + (TAPS - 1), G * P)].rearrange("p b t -> p (b t)"), ACT.Copy).then_inc(xs_ready.sem, 1)
                g_full.wait(act, n, 1)
                act.activation(gate[:, :], gp[:, :], ACT.Silu).then_inc(gated.sem, 1)
                ms_step.wait(act, n, 2)
                act.activation(ms[:, :], ms[:, :], ACT.Sqrt).then_inc(rooted.sem, 1)
                oT_full.wait(act, n, 1)
                act.activation(oT[:, :, :, :].rearrange("p a b c -> p (a b c)"), tp[:, :], ACT.Copy).then_inc(oT_read.sem, 1)

        @block.vector
        def _(dve):
            loaded.wait(dve, 0, 48)
            x_done.open(dve)
            with dve.Fori(0, PASSES) as n:
                heads = o[:, :, :].rearrange("p t (h d) -> p (t h) d", d=VD)
                squared.wait(dve, n, 1)
                dve.tensor_reduce(ms[:, :], sq_[:, :, :].rearrange("p t (h d) -> p (t h) d", d=VD), AX.X, ALU.add).then_inc(ms_step.sem, 1)
                ms_step.wait(dve, n, 1)
                dve.tensor_scalar(ms[:, :], ms[:, :], 1.0 / VD, EPS_RMS, ALU.mult, ALU.add).then_inc(ms_step.sem, 1)
                rooted.wait(dve, n, 1)
                dve.reciprocal(ms[:, :], ms[:, :]).then_inc(ms_step.sem, 1)
                ms_step.wait(dve, n, 3)
                dve.tensor_tensor(heads, heads, wide(ms[:, :], 2, [P, G * HEADS, VD]), ALU.mult).then_inc(o_step.sem, 1)
                o_step.wait(dve, n, 1)
                dve.tensor_tensor(heads, heads, wide(nw[:, :], 1, [P, G * HEADS, VD]), ALU.mult).then_inc(o_step.sem, 1)
                o_step.wait(dve, n, 2)
                gated.wait(dve, n, 1)
                flat_o = o[:, :, :].rearrange("p t v -> p (t v)")
                dve.tensor_tensor(flat_o, flat_o, gate[:, :], ALU.mult).then_inc(o_step.sem, 1)
                p_full.wait(dve, n, 1)
                for j in range(G):
                    x = x_sb[:, bass.ds(n * (G * C) + j * C, C)]
                    dve.tensor_tensor(x, x, xp[:, C * j:C * j + C], ALU.add).then_inc(x_done.sem, 1)
                x_done.wait(dve, n, 4)

        @block.tensor
        def _(pe):
            loaded.wait(pe, 0, 48)
            oT_full.open(pe)
            g_full.open(pe)
            with pe.Fori(0, PASSES) as n:
                xs_ready.wait(pe, n, 1)
                gated.wait(pe, n, 0)
                for j in range(G):
                    mm = pe.matmul(gp[:, V * j:V * j + V], xs[:, P * j:P * j + P], wg[:, :], start=True, stop=True)
                mm.then_inc(g_full.sem, 1)
                o_step.wait(pe, n, 3)
                oT_read.wait(pe, n, 0)
                for j in range(G):
                    for hq in range(2):
                        mm = pe.transpose(tp[:, P * (2 * j + hq):P * (2 * j + hq) + P], o[:, j, P * hq:P * hq + P], k["ident"][:, :])
                mm.then_inc(oT_full.sem, 1)
                oT_read.wait(pe, n, 1)
                x_done.wait(pe, n, 0)
                for j in range(G):
                    for hq in range(2):
                        mm = pe.matmul(xp[:, C * j:C * j + C], oT[:, j, hq, :], wo[:, hq, :], start=(hq == 0), stop=(hq == 1))
                mm.then_inc(p_full.sem, 1)


B_WEIGHTS = ["Wq", "Wk", "Wv", "Wa", "Wb", "Wg", "Wo", "A_log", "dt_bias", "conv_q", "conv_k", "conv_v", "o_norm_w"]
INPUTS = ["L0_attn_a_x", "L0_attn_a_W_attn", "L0_attn_a_W_proj", *("L0_attn_b_" + n for n in B_WEIGHTS),
          "L0_ffn_Wr", "L0_ffn_Wg", "L0_ffn_Wu", "L0_ffn_Wd"]


def hybrid_layer(nc, dram, out):
    with ExitStack() as ctx:
        k = make_constants(nc, ctx)
        x_sb = ctx.enter_context(nc.sbuf_tensor("x_sb", [P, TILES * C], F32))
        x_in, x_out = ctx.enter_context(nc.semaphore("x_in")), ctx.enter_context(nc.semaphore("x_out"))
        xn_dram = nc.dram_tensor("xn_rows", (TOKENS, C), F32).ap()
        y_dram = nc.dram_tensor("y_rows", (TOP_K * TOKENS + SLOT_TILES * P, C), F32).ap()
        o_dram = nc.dram_tensor("o_rows", (TOKENS, HEADS * VD), F32).ap()
        tiles = x_sb[:, :].rearrange("p (n c) -> p n c", c=C)
        with nc.Block() as block:
            @block.sync
            def _(sp):
                sp.dma_start(tiles, dram["L0_attn_a_x"].rearrange("b (n p) c -> p (b n) c", p=P)).then_inc(x_in, 16)
                sp.wait_ge(x_in, 16)
        ffn = [dram["L0_ffn_" + n] for n in ("Wr", "Wg", "Wu", "Wd")]
        with nc.cleanup_on_exit():
            nystrom_attention(nc, k, x_sb, dram["L0_attn_a_W_attn"], dram["L0_attn_a_W_proj"])
        with nc.cleanup_on_exit():
            mixture_of_experts(nc, k, x_sb, *ffn, xn_dram, y_dram, "m1_")
        with nc.cleanup_on_exit():
            delta_attention(nc, k, x_sb, {n: dram["L0_attn_b_" + n] for n in B_WEIGHTS}, o_dram)
        with nc.cleanup_on_exit():
            mixture_of_experts(nc, k, x_sb, *ffn, xn_dram, y_dram, "m2_")
        with nc.Block() as block:
            @block.sync
            def _(sp):
                sp.dma_start(out.rearrange("b (n p) c -> p (b n) c", p=P), tiles).then_inc(x_out, 16)
                sp.wait_ge(x_out, 16)


def kernel(**inputs):
    import numpy as np
    import concourse.bacc as bacc
    from concourse.bass_utils import run_bass_kernel_spmd

    nc = bacc.Bacc("TRN2", target_bir_lowering=False, num_devices=1)
    arrays, dram = {}, {}
    for name in INPUTS:
        arrays[name] = np.ascontiguousarray(inputs[name])
        dram[name] = nc.dram_tensor(name, arrays[name].shape, mybir.dt.from_np(arrays[name].dtype), kind="ExternalInput").ap()
    out = nc.dram_tensor("out", (BATCHES, T, C), F32, kind="ExternalOutput").ap()
    hybrid_layer(nc, dram, out)
    return run_bass_kernel_spmd(nc, [arrays], core_ids=[0]).results[0]["out"]
```

```python
import concourse.bass as bass
from concourse import mybir
from contextlib import ExitStack

F32 = mybir.dt.float32
U32 = mybir.dt.uint32
I32 = mybir.dt.int32
ALU = mybir.AluOpType
ACT = mybir.ActivationFunctionType
AX = mybir.AxisListType

P = 128
C = 128
TILES = 32
BATCHES = 4
TPB = TILES // BATCHES
T = TPB * P
EPS_LN = 1e-5


class Signal:

    def __init__(self, sem, per=1):
        self.sem, self.per, self.credit = sem, per, 0

    def with_credit(self, credit=1):
        self.credit = credit
        return self

    def open(self, eng):
        eng.sem_inc(self.sem, self.credit)

    def wait(self, eng, passes, k):
        at = passes * self.per + k
        if not isinstance(at, int):
            assert self.credit or k > 0, self.sem
        if not isinstance(at, int) or at > 0:
            eng.wait_ge(self.sem, at + self.credit)


def wide(ap, axis, shape):
    return ap.unsqueeze(axis).to_broadcast(shape)


def make_constants(nc, ctx):
    def sb(name, shape):
        return ctx.enter_context(nc.sbuf_tensor(name, shape, F32))

    k = {
        "ident": sb("ident", [P, P]),
        "ones": sb("ones", [P, P]),
        "half_ones": sb("half_ones", [P, P]),
        "head_rows": sb("head_rows", [P, 16]),
        "upto": sb("upto", [P, P]),
        "after": sb("after", [P, P]),
        "before": sb("before", [P, P]),
    }
    filled = ctx.enter_context(nc.semaphore("const_filled"))
    shaped = ctx.enter_context(nc.semaphore("const_shaped"))
    with nc.Block() as block:
        @block.gpsimd
        def _(pool):
            for name in ("ones", "half_ones", "head_rows", "upto", "after", "before"):
                pool.memset(k[name][:, :], 1.0).then_inc(filled, 1)
            pool.memset(k["ident"][:, :], 0.0).then_inc(filled, 1)
            pool.wait_ge(filled, 7)

            def select(name, ap, op, fill, base, pattern, step):
                pool.affine_select(out=ap, in_=ap, compare_op=op, fill=fill, base=base,
                                   pattern=pattern, channel_multiplier=step).then_inc(shaped, 1)
            select("ident", k["ident"][:, :], ALU.not_equal, 1.0, 0, [[-1, P]], 1)
            select("upto", k["upto"][:, :], ALU.is_ge, 0.0, 0, [[1, P]], -1)
            select("after", k["after"][:, :], ALU.is_gt, 0.0, 0, [[-1, P]], 1)
            select("before", k["before"][:, :], ALU.is_gt, 0.0, 0, [[1, P]], -1)
            select("half", k["half_ones"][:, 0:64], ALU.is_gt, 0.0, 64, [[0, 64]], -1)
            select("half", k["half_ones"][:, 64:128], ALU.is_ge, 0.0, -64, [[0, 64]], 1)
            select("head", k["head_rows"][:, :], ALU.is_ge, 0.0, 0, [[-8, 16]], 1)
            pool.wait_ge(shaped, 7)
            select("head", k["head_rows"][:, :], ALU.is_ge, 0.0, 7, [[8, 16]], -1)
            pool.wait_ge(shaped, 8)
    return k


def nystrom_attention(nc, k, x_sb, w_attn, w_proj):
    PAIRS, NL, HS, ITERS = 8, 64, 8, 6
    with ExitStack() as ctx:
        def sb(name, *shape):
            return ctx.enter_context(nc.sbuf_tensor("a_" + name, list(shape), F32))

        def psum(name, *shape):
            return ctx.enter_context(nc.psum_tensor("a_" + name, list(shape), F32))

        def signal(name, per=1):
            return Signal(nc.alloc_semaphore("a_" + name), per)

        wa, wp = sb("wa", P, 3 * C), sb("wp", P, C)
        stats, moments, rstd = sb("stats", P, TPB, 6), sb("moments", P, TPB, 2), sb("rstd", P, TPB)
        xn, xT = sb("xn", P, TPB, C), sb("xT", P, T)
        qT, kT, v = sb("qT", P, T), sb("kT", P, T), sb("v", P, TPB, C)
        q_land, k_land = sb("q_land", P, NL), sb("k_land", P, NL)
        q_diag, k_diag = sb("q_diag", P, 16, NL), sb("k_diag", P, 16, NL)
        mid_max, mid_sum, denom = sb("mid_max", P, PAIRS), sb("mid_sum", P, PAIRS), sb("denom", P, PAIRS)
        mid_x, K = sb("mid_x", P, PAIRS, NL), sb("K", P, PAIRS, NL)
        K_diag, KT_diag = sb("K_diag", P, PAIRS, P), sb("KT_diag", P, PAIRS, P)
        Y = [sb(f"Y{n}", P, PAIRS, 2, NL) for n in range(2)]
        M_diag, M2_diag = sb("M_diag", P, PAIRS, P), sb("M2_diag", P, PAIRS, P)
        MY, R, S, S1 = (sb(n, P, PAIRS, 2, NL) for n in ("MY", "R", "S", "S1"))
        far_max, far_sum = sb("far_max", P, PAIRS), sb("far_sum", P, PAIRS)
        far, farT = [sb(f"far{n}", P, T) for n in range(2)], [sb(f"farT{n}", P, TPB, P) for n in range(2)]
        W, ZW = sb("W", P, PAIRS, HS), sb("ZW", P, PAIRS, HS)
        near_max = sb("near_max", P, 16)
        near, nearT = [sb(f"near{n}", P, 16, NL) for n in range(2)], [sb(f"nearT{n}", P, PAIRS, P) for n in range(2)]
        U_diag = sb("U_diag", P, PAIRS, 18)
        y_rs, y, yT = sb("y_rs", P, PAIRS, 2), sb("y", P, PAIRS, 2, HS), sb("yT", P, C)

        sc = [psum(f"sc{n}", P, 1024) for n in range(2)]
        tp, nw, sm = psum("tp", P, 512), psum("nw", P, 1024), psum("sm", P, 512)

        alone, pool_alone = signal("alone"), signal("pool_alone")
        loaded, zeroed = signal("loaded"), signal("zeroed")
        bn_done, aggr_done, rstd_ready, xn_ready = signal("bn_done", 8), signal("aggr_done", 8), signal("rstd_ready"), signal("xn_ready", 8)
        land_sum, land_ready, diag_ready = signal("land_sum", 2), signal("land_ready", 2), signal("diag_ready", 2)
        var_ready, root_ready = signal("var_ready"), signal("root_ready")
        mid_max_ready, mid_sub, mid_exp, mid_sum_ready = (signal(n) for n in ("mid_max_ready", "mid_sub", "mid_exp", "mid_sum_ready"))
        mid_recip, K_ready, K_diag_ready = signal("mid_recip"), signal("K_ready"), signal("K_diag_ready")
        denom_ready, M0_ready, Z0_ready = signal("denom_ready", 2), signal("M0_ready"), signal("Z0_ready")
        Y_ready, M_diag_ready, my_ready, M2_diag_ready = signal("Y_ready", 2 + ITERS), signal("M_diag_ready", 2 * ITERS), signal("my_ready", ITERS), signal("M2_diag_ready", 2 * ITERS)
        R_ready, S1_ready, S_ready = signal("R_ready", ITERS), signal("S1_ready", ITERS), signal("S_ready", ITERS)
        far_bias, far_exp, far_recip, W0_ready = signal("far_bias", 8), signal("far_exp", 8), signal("far_recip"), signal("W0_ready", 2)
        ZW_ready = signal("ZW_ready")
        U_ready = signal("U_ready", 2)
        near_max_ready, near_sub, near_exp = signal("near_max_ready", 8), signal("near_sub", 8), signal("near_exp", 8)
        y_recip, y_ready, yT_ready, x_done = signal("y_recip", 8), signal("y_ready", 8), signal("yT_ready", 8), signal("x_done", 8)
        tp_read, qkv_read = signal("tp_read", 36), signal("qkv_read", 3)
        tp_full, sc_full = signal("tp_full", 36), signal("sc_full", 20)
        mid_full, colsum_full, my_full, m2r_full = signal("mid_full"), signal("colsum_full"), signal("my_full", ITERS), signal("m2r_full", ITERS)
        nv_full, zw_full, u_full = signal("nv_full", 8), signal("zw_full"), signal("u_full")
        y_full, yT_full, o_full = signal("y_full", 8), signal("yT_full", 8), signal("o_full", 8)
        TP_KT, TP_FAR, TP_NEAR = 2, 4, 20
        SC_M0, SC_NEAR = 4, 12
        HALVES = (slice(0, 64), slice(64, 128))

        def sc_far(s):
            return 4 + s if s else 3

        def tile(b, j):
            return bass.ds(b * (TPB * C) + j * C, C)

        def flat(ap):
            return ap.rearrange("p a b -> p (a b)")

        def flat4(ap):
            return ap.rearrange("p a m b -> p (a m b)")

        def live(s):
            return slice(1 if s == ITERS - 1 else 0, 2)

        def loop(eng, batch):
            with eng.Fori(0, BATCHES - 1) as b:
                batch(b, True)
            batch(BATCHES - 1, False)

        block = ctx.enter_context(nc.Block())

        @block.sync
        def _(sp):
            sp.dma_start(wa[:, :], w_attn).then_inc(loaded.sem, 16)
            sp.dma_start(wp[:, :], w_proj).then_inc(loaded.sem, 16)

        @block.gpsimd
        def _(pool):
            for t in (M2_diag, U_diag):
                pool.memset(t[:, :, :], 0.0).then_inc(zeroed.sem, 1)
            pool.wait_ge(zeroed.sem, 2)
            pool.memset(U_diag[0:64, :, 16:17], 1.0).then_inc(zeroed.sem, 1)
            pool.memset(U_diag[64:128, :, 17:18], 1.0).then_inc(zeroed.sem, 1)
            pool.wait_ge(zeroed.sem, 4)
            halves = wide(wide(k["half_ones"][:, ::NL], 1, [P, PAIRS, 2]), 3, [P, PAIRS, 2, NL])

            def by_half(t):
                return t[:, :, :].rearrange("p a (h l) -> p a h l", h=2)

            def wait(signal, b, steps):
                signal.wait(pool, b, steps)
                pool.sem_inc(pool_alone.sem, 1)

            with pool.Fori(0, BATCHES) as b:
                wait(K_ready, b, 1)
                pool.tensor_tensor(by_half(K_diag), wide(K[:, :, :], 2, [P, PAIRS, 2, NL]), halves, ALU.mult).then_inc(K_diag_ready.sem, 1)
                pool.tensor_tensor(Y[0][:, :, 1, :], wide(k["ident"][:, 0:NL], 1, [P, PAIRS, NL]), wide(k["ident"][:, NL:], 1, [P, PAIRS, NL]),
                                   ALU.add).then_inc(Z0_ready.sem, 1)
                Z0_ready.wait(pool, b, 1)
                for s in range(ITERS):
                    wait(Y_ready, b, 2 + s)
                    if s:
                        wait(S_ready, b, s)
                    pool.tensor_scalar(S1[:, :, :, :], Y[s % 2][:, :, :, :], 3.25, None, ALU.mult).then_inc(S1_ready.sem, 1)

        @block.scalar
        def _(act):
            act.wait_ge(zeroed.sem, 4)

            def from_tp(b, n, out):
                tp_full.wait(act, b, n + 1)
                act.activation(out, tp[:, :], ACT.Copy).then_inc(tp_read.sem, 1)

            def root(b):
                var_ready.wait(act, b, 1)
                act.activation(rstd[:, :], rstd[:, :], ACT.Sqrt).then_inc(root_ready.sem, 1)

            def tokens_out(b, g):
                from_tp(b, g, xT[:, 512 * g:512 * g + 512])

            def qkv_out(b, n):
                sc_full.wait(act, b, n + 1)
                act.activation((qT[:, :], kT[:, :], flat(v[:, :, :]))[n], sc[n % 2][:, :], ACT.Copy).then_inc(qkv_read.sem, 1)

            def batch(b, more):
                mid_sub.wait(act, b, 1)
                act.activation(mid_x[:, :, :], mid_x[:, :, :], ACT.Exp).then_inc(mid_exp.sem, 1)

                def far_exponential(s):
                    far_bias.wait(act, b, s + 1)
                    if s >= 2:
                        tp_full.wait(act, b, TP_FAR + 2 * (s - 1))
                    act.activation(far[s % 2][:, :], sc[s % 2][:, :], ACT.Exp, bias=far_max[:, s:s + 1],
                                   accum_out=far_sum[:, s:s + 1]).then_inc(far_exp.sem, 1)

                far_exponential(0)
                for g in range(2):
                    from_tp(b, TP_KT + g, flat(KT_diag[:, 4 * g:4 * g + 4, :]))

                def far_out(s, g):
                    if s >= 2:
                        nv_full.wait(act, b, s - 1)
                    from_tp(b, TP_FAR + 2 * s + g, flat(farT[s % 2][:, 4 * g:4 * g + 4, :]))

                for s in range(PAIRS):
                    far_out(s, 0)
                    if s < ITERS:
                        my_full.wait(act, b, s + 1)
                        if s:
                            S_ready.wait(act, b, s)
                        act.activation(flat4(MY[:, :, :, :]), nw[:, :], ACT.Copy).then_inc(my_ready.sem, 1)
                        my_ready.wait(act, b, s + 1)
                        for r in HALVES:
                            act.activation(M2_diag[r, :, r], MY[r, :, 0, :], ACT.Copy).then_inc(M2_diag_ready.sem, 1)
                    far_out(s, 1)
                    if s + 1 < PAIRS:
                        far_exponential(s + 1)
                    if s < ITERS:
                        Y_ready.wait(act, b, 3 + s)
                        for r in HALVES:
                            act.activation(M_diag[r, :, r], Y[(s + 1) % 2][r, :, 1 if s == ITERS - 1 else 0, :], ACT.Copy).then_inc(M_diag_ready.sem, 1)

                def near_exponential(s):
                    near_sub.wait(act, b, s + 1)
                    act.activation(near[s % 2][:, :, :], near[s % 2][:, :, :], ACT.Exp).then_inc(near_exp.sem, 1)

                def near_out(s, g):
                    if s >= 2:
                        y_full.wait(act, b, s - 1)
                    from_tp(b, TP_NEAR + 2 * s + g, flat(nearT[s % 2][:, 4 * g:4 * g + 4, :]))

                if more:
                    root(b + 1)
                near_exponential(0)
                for s in range(TPB + 2):
                    if more and s == TPB:
                        for g in range(2):
                            tokens_out(b + 1, g)
                    if s < TPB:
                        near_out(s, 0)
                        if s + 1 < TPB:
                            near_exponential(s + 1)
                        near_out(s, 1)
                    if s >= 2:
                        t = s - 2
                        yT_full.wait(act, b, t + 1)
                        if t:
                            o_full.wait(act, b, t)
                        act.activation(yT[:, :], sm[:, 0:C], ACT.Copy).then_inc(yT_ready.sem, 1)
                if more:
                    for n in range(3):
                        qkv_out(b + 1, n)

            root(0)
            for g in range(2):
                tokens_out(0, g)
            for n in range(3):
                qkv_out(0, n)
            loop(act, batch)

        @block.vector
        def _(dve):
            dve.wait_ge(zeroed.sem, 4)

            def norm_start(b):
                xn_ready.wait(dve, b - 1, TPB)
                dve.sem_inc(alone.sem, 1)
                for j in range(TPB):
                    dve.bn_stats(stats[:, j, :], x_sb[:, tile(b, j)]).then_inc(bn_done.sem, 1)
                bn_done.wait(dve, b, 8)
                dve.sem_inc(alone.sem, 1)
                for j in range(TPB):
                    dve.bn_aggr(moments[:, j, :], stats[:, j, :]).then_inc(aggr_done.sem, 1)
                aggr_done.wait(dve, b, 8)
                dve.tensor_scalar(rstd[:, :], moments[:, :, 1], EPS_LN, None, ALU.add).then_inc(var_ready.sem, 1)

            def norm_end(b):
                root_ready.wait(dve, b, 1)
                dve.reciprocal(rstd[:, :], rstd[:, :]).then_inc(rstd_ready.sem, 1)
                rstd_ready.wait(dve, b, 1)
                tp_full.wait(dve, b - 1, 2)
                dve.sem_inc(alone.sem, 1)
                for j in range(TPB):
                    dve.tensor_scalar(xn[:, j, :], x_sb[:, tile(b, j)], moments[:, j, 0:1], rstd[:, j:j + 1],
                                      ALU.subtract, ALU.mult).then_inc(xn_ready.sem, 1)

            def landmarks(b):
                for n, (src, land) in enumerate(((qT, q_land), (kT, k_land))):
                    qkv_read.wait(dve, b, n + 1)
                    dve.tensor_reduce(land[:, :], src[:, :].rearrange("p (l t) -> p l t", l=NL), AX.X, ALU.add).then_inc(land_sum.sem, 1)
                land_sum.wait(dve, b, 2)
                for land in (q_land, k_land):
                    dve.tensor_scalar(land[:, :], land[:, :], NL / T, None, ALU.mult).then_inc(land_ready.sem, 1)
                land_ready.wait(dve, b, 2)
                for land, diag in ((q_land, q_diag), (k_land, k_diag)):
                    dve.tensor_tensor(diag[:, :, :], wide(land[:, :], 1, [P, 16, NL]), wide(k["head_rows"][:, :], 2, [P, 16, NL]),
                                      ALU.mult).then_inc(diag_ready.sem, 1)

            def batch(b, more):
                mid = nw[:, 0:512].rearrange("p (a b) -> p a b", b=NL)
                mid_full.wait(dve, b, 1)
                dve.tensor_reduce(mid_max[:, :], mid, AX.X, ALU.max).then_inc(mid_max_ready.sem, 1)
                mid_max_ready.wait(dve, b, 1)
                dve.tensor_tensor(mid_x[:, :, :], mid, wide(mid_max[:, :], 2, [P, PAIRS, NL]), ALU.subtract).then_inc(mid_sub.sem, 1)
                mid_exp.wait(dve, b, 1)
                dve.tensor_reduce(mid_sum[:, :], mid_x[:, :, :], AX.X, ALU.add).then_inc(mid_sum_ready.sem, 1)
                mid_sum_ready.wait(dve, b, 1)
                dve.reciprocal(mid_sum[:, :], mid_sum[:, :]).then_inc(mid_recip.sem, 1)
                mid_recip.wait(dve, b, 1)
                dve.tensor_tensor(K[:, :, :], mid_x[:, :, :], wide(mid_sum[:, :], 2, [P, PAIRS, NL]), ALU.mult).then_inc(K_ready.sem, 1)
                def far_maximum(s):
                    sc_full.wait(dve, b, sc_far(s) + 1)
                    dve.tensor_reduce(far_max[:, s:s + 1], sc[s % 2][:, :], AX.X, ALU.max, negate=True).then_inc(far_bias.sem, 1)

                far_maximum(0)
                colsum_full.wait(dve, b, 1)
                dve.tensor_reduce(denom[:, :], sm[:, :].rearrange("p (a b) -> p a b", b=NL), AX.X, ALU.max).then_inc(denom_ready.sem, 1)
                denom_ready.wait(dve, b, 1)
                dve.reciprocal(denom[:, :], denom[:, :]).then_inc(denom_ready.sem, 1)
                denom_ready.wait(dve, b, 2)
                sc_full.wait(dve, b, SC_M0 + 1)
                dve.tensor_tensor(M_diag[:, :, :], sc[1][:, :].rearrange("p (a b) -> p a b", b=P),
                                  wide(denom[:, :], 2, [P, PAIRS, P]), ALU.mult).then_inc(M0_ready.sem, 1)
                M0_ready.wait(dve, b, 1)
                for r in HALVES:
                    dve.tensor_copy(Y[0][r, :, 0, :], M_diag[r, :, r]).then_inc(Y_ready.sem, 1)

                for s in range(PAIRS):
                    if s + 1 < PAIRS:
                        far_maximum(s + 1)
                    if more and s == ITERS:
                        norm_start(b + 1)
                    if s < ITERS:
                        now, new, part = Y[s % 2], Y[(s + 1) % 2], live(s)
                        my_ready.wait(dve, b, s + 1)
                        Y_ready.wait(dve, b, 2 + s)
                        if s == 0:
                            Z0_ready.wait(dve, b, 1)
                        dve.scalar_tensor_tensor(R[:, :, part, :], now[:, :, part, :], 7.0, MY[:, :, part, :], ALU.mult, ALU.subtract).then_inc(R_ready.sem, 1)
                        S1_ready.wait(dve, b, s + 1)
                        dve.scalar_tensor_tensor(S[:, :, part, :], MY[:, :, part, :], -3.75, S1[:, :, part, :], ALU.mult, ALU.add).then_inc(S_ready.sem, 1)
                        S_ready.wait(dve, b, s + 1)
                        m2r_full.wait(dve, b, s + 1)
                        got = nw[:, :].rearrange("p (a m b) -> p a m b", m=2, b=NL)
                        dve.scalar_tensor_tensor(new[:, :, part, :], got[:, :, part, :], 0.25, S[:, :, part, :], ALU.mult, ALU.add).then_inc(Y_ready.sem, 1)
                far_exp.wait(dve, b, 8)
                dve.reciprocal(far_sum[:, :], far_sum[:, :]).then_inc(far_recip.sem, 1)
                far_recip.wait(dve, b, 1)
                nv_full.wait(dve, b, 8)
                nv = sm[:, 0:128].rearrange("p (a b) -> p a b", b=2 * HS)
                for h, r in enumerate(HALVES):
                    dve.tensor_tensor(W[r, :, :], nv[r, :, HS * h:HS * h + HS], wide(far_sum[r, :], 2, [64, PAIRS, HS]),
                                      ALU.mult).then_inc(W0_ready.sem, 1)
                W0_ready.wait(dve, b, 2)

                def near_softmax(s):
                    scores = sc[(SC_NEAR + s) % 2][:, :].rearrange("p (a b) -> p a b", b=NL)
                    sc_full.wait(dve, b, SC_NEAR + s + 1)
                    if s:
                        near_sub.wait(dve, b, s)
                    dve.tensor_reduce(near_max[:, :], scores, AX.X, ALU.max).then_inc(near_max_ready.sem, 1)
                    near_max_ready.wait(dve, b, s + 1)
                    if s >= 2:
                        tp_full.wait(dve, b, TP_NEAR + 2 * (s - 1))
                    dve.tensor_tensor(near[s % 2][:, :, :], scores, wide(near_max[:, :], 2, [P, 16, NL]), ALU.subtract).then_inc(near_sub.sem, 1)

                near_softmax(0)
                zw_full.wait(dve, b, 1)
                dve.tensor_copy(flat(ZW[:, :, :]), sm[:, 128:192]).then_inc(ZW_ready.sem, 1)
                u_full.wait(dve, b, 1)
                for h, r in enumerate(HALVES):
                    dve.tensor_tensor(U_diag[r, :, HS * h:HS * h + HS], sm[r, 256:320].rearrange("p (a b) -> p a b", b=HS),
                                      wide(denom[r, :], 2, [64, PAIRS, HS]), ALU.mult).then_inc(U_ready.sem, 1)

                def output(s):
                    got = nw[:, 0:144].rearrange("p (a b) -> p a b", b=18)
                    y_full.wait(dve, b, s + 1)
                    if s:
                        y_ready.wait(dve, b, s)
                    dve.reciprocal(y_rs[:, :, :], got[:, :, 16:18]).then_inc(y_recip.sem, 1)
                    y_recip.wait(dve, b, s + 1)
                    if s:
                        yT_full.wait(dve, b, s)
                    dve.tensor_tensor(y[:, :, :, :], got[:, :, 0:16].rearrange("p a (h d) -> p a h d", h=2),
                                      wide(y_rs[:, :, :], 3, [P, PAIRS, 2, HS]), ALU.mult).then_inc(y_ready.sem, 1)

                def residual(s):
                    o_full.wait(dve, b, s + 1)
                    dve.tensor_tensor(x_sb[:, tile(b, s)], x_sb[:, tile(b, s)], nw[:, 512:512 + C],
                                      ALU.add).then_inc(x_done.sem, 1)

                for s in range(TPB + 3):
                    if s + 1 < TPB:
                        near_softmax(s + 1)
                    if 1 <= s <= TPB:
                        output(s - 1)
                    if s >= 3:
                        residual(s - 3)
                    if more and s == 3:
                        norm_end(b + 1)
                if more:
                    landmarks(b + 1)
                x_done.wait(dve, b, TPB)

            norm_start(0)
            norm_end(0)
            landmarks(0)
            loop(dve, batch)

        @block.tensor
        def _(pe):
            pe.wait_ge(loaded.sem, 32)

            def transpose4(b, n, ins):
                if n:
                    tp_read.wait(pe, b, n)
                else:
                    tp_read.wait(pe, b - 1, TP_NEAR + 2 * TPB)
                for g, ap in enumerate(ins):
                    mm = pe.transpose(tp[:, P * g:P * g + P], ap, k["ident"][:, :])
                mm.then_inc(tp_full.sem, 1)

            def tokens(b, g):
                xn_ready.wait(pe, b, 4 * g + 4)
                transpose4(b, g, [xn[:, j, :] for j in range(4 * g, 4 * g + 4)])

            def qkv(b, n):
                if n < 2:
                    near_sub.wait(pe, b - 1, TPB - 1 + n)
                    if n == 0:
                        tp_read.wait(pe, b, 2)
                    for g in range(2):
                        mm = pe.matmul(sc[n][:, 512 * g:512 * g + 512], wa[:, C * n:C * n + C], xT[:, 512 * g:512 * g + 512], start=True, stop=True)
                else:
                    qkv_read.wait(pe, b, 1)
                    for j in range(TPB):
                        mm = pe.matmul(sc[0][:, C * j:C * j + C], xT[:, P * j:P * j + P], wa[:, 2 * C:3 * C], start=True, stop=True)
                mm.then_inc(sc_full.sem, 1)

            def batch(b, more):
                diag_ready.wait(pe, b, 2)
                for s in range(PAIRS):
                    mm = pe.matmul(nw[:, NL * s:NL * s + NL], flat(q_diag[:, 2 * s:2 * s + 2, :]), k_land[:, :], start=True, stop=True)
                mm.then_inc(mid_full.sem, 1)
                def far_scores(s):
                    if s == 0:
                        qkv_read.wait(pe, b, 3)
                    elif s == 1:
                        M0_ready.wait(pe, b, 1)
                    else:
                        far_exp.wait(pe, b, s - 1)
                    for g in range(2):
                        mm = pe.matmul(sc[s % 2][:, 512 * g:512 * g + 512], flat(q_diag[:, 2 * s:2 * s + 2, :]),
                                       kT[:, 512 * g:512 * g + 512], start=True, stop=True)
                    mm.then_inc(sc_full.sem, 1)

                far_scores(0)
                K_ready.wait(pe, b, 1)
                pe.matmul(sm[:, :], k["half_ones"][:, :], flat(K[:, :, :]), start=True, stop=True).then_inc(colsum_full.sem, 1)
                K_diag_ready.wait(pe, b, 1)
                for g in range(2):
                    transpose4(b, TP_KT + g, [K_diag[:, s, :] for s in range(4 * g, 4 * g + 4)])
                tp_read.wait(pe, b, TP_KT + 2)
                qkv_read.wait(pe, b, 2)
                for s in range(PAIRS):
                    mm = pe.matmul(sc[1][:, P * s:P * s + P], KT_diag[:, s, :], KT_diag[:, s, :], start=True, stop=True)
                mm.then_inc(sc_full.sem, 1)

                def far_times_v(s):
                    tp_read.wait(pe, b, TP_FAR + 2 * s + 2)
                    if s == 0:
                        denom_ready.wait(pe, b, 1)
                    for j in range(TPB):
                        mm = pe.matmul(sm[:, 16 * s:16 * s + 16], farT[s % 2][:, j, :], v[:, j, 16 * s:16 * s + 16],
                                       start=(j == 0), stop=(j == TPB - 1))
                    mm.then_inc(nv_full.sem, 1)

                def far_transposes(s, g):
                    if g == 0:
                        far_exp.wait(pe, b, s + 1)
                    transpose4(b, TP_FAR + 2 * s + g, [far[s % 2][:, P * j:P * j + P] for j in range(4 * g, 4 * g + 4)])

                for s in range(PAIRS):
                    if s + 1 < PAIRS:
                        far_scores(s + 1)
                    far_transposes(s, 0)
                    if s < ITERS:
                        Y_ready.wait(pe, b, 2 + s)
                        if s:
                            M_diag_ready.wait(pe, b, 2 * s)
                        else:
                            Z0_ready.wait(pe, b, 1)
                        for a in range(PAIRS):
                            mm = pe.matmul(nw[:, P * a:P * a + P], M_diag[:, a, :], flat(Y[s % 2][:, a, :, :]), start=True, stop=True)
                        mm.then_inc(my_full.sem, 1)
                    far_transposes(s, 1)
                    if s:
                        far_times_v(s - 1)
                    if s < ITERS:
                        R_ready.wait(pe, b, s + 1)
                        M2_diag_ready.wait(pe, b, 2 * s + 2)
                        part = live(s)
                        for a in range(PAIRS):
                            mm = pe.matmul(nw[:, P * a + NL * part.start:P * a + P], M2_diag[:, a, :], flat(R[:, a, part, :]), start=True, stop=True)
                        mm.then_inc(m2r_full.sem, 1)
                far_times_v(PAIRS - 1)

                def near_scores(s):
                    n = SC_NEAR + s
                    if s < 2:
                        far_exp.wait(pe, b, 7 + s)
                    else:
                        near_sub.wait(pe, b, s - 1)
                    for g in range(2):
                        mm = pe.matmul(sc[n % 2][:, 512 * g:512 * g + 512], qT[:, P * s:P * s + P], flat(k_diag[:, 8 * g:8 * g + 8, :]),
                                       start=True, stop=True)
                    mm.then_inc(sc_full.sem, 1)

                near_scores(0)
                near_scores(1)
                W0_ready.wait(pe, b, 2)
                M_diag_ready.wait(pe, b, 2 * ITERS)
                for a in range(PAIRS):
                    mm = pe.matmul(sm[:, 128 + HS * a:128 + HS * a + HS], M_diag[:, a, :], W[:, a, :], start=True, stop=True)
                mm.then_inc(zw_full.sem, 1)
                ZW_ready.wait(pe, b, 1)
                for a in range(PAIRS):
                    mm = pe.matmul(sm[:, 256 + HS * a:256 + HS * a + HS], K_diag[:, a, :], ZW[:, a, :], start=True, stop=True)
                mm.then_inc(u_full.sem, 1)

                def near_transposes(s, g):
                    if g == 0:
                        near_exp.wait(pe, b, s + 1)
                    transpose4(b, TP_NEAR + 2 * s + g, [flat(near[s % 2][:, 2 * a:2 * a + 2, :]) for a in range(4 * g, 4 * g + 4)])

                for s in range(TPB + 3):
                    if more and s == TPB:
                        tokens(b + 1, 0)
                    if s < TPB:
                        near_transposes(s, 0)
                        if s + 2 < TPB:
                            near_scores(s + 2)
                        near_transposes(s, 1)
                    if 1 <= s <= TPB:
                        t = s - 1
                        tp_read.wait(pe, b, TP_NEAR + 2 * t + 2)
                        if t:
                            y_ready.wait(pe, b, t)
                        else:
                            U_ready.wait(pe, b, 2)
                        for a in range(PAIRS):
                            mm = pe.matmul(nw[:, 18 * a:18 * a + 18], nearT[t % 2][:, a, :], U_diag[:, a, :], start=True, stop=True)
                        mm.then_inc(y_full.sem, 1)
                    if more and s >= TPB:
                        if s == TPB:
                            tokens(b + 1, 1)
                        else:
                            qkv(b + 1, s - TPB - 1)
                    if 2 <= s <= TPB + 1:
                        t = s - 2
                        y_ready.wait(pe, b, t + 1)
                        if t:
                            yT_ready.wait(pe, b, t)
                        pe.transpose(sm[:, 0:C], y[:, :, :, :].rearrange("p a h d -> p (a h d)"), k["ident"][:, :]).then_inc(yT_full.sem, 1)
                    if s >= 3:
                        t = s - 3
                        yT_ready.wait(pe, b, t + 1)
                        if t:
                            x_done.wait(pe, b, t)
                        pe.matmul(nw[:, 512:512 + C], yT[:, :], wp[:, :], start=True, stop=True).then_inc(o_full.sem, 1)
                if more:
                    qkv(b + 1, 2)

            for g in range(2):
                tokens(0, g)
            for n in range(3):
                qkv(0, n)
            loop(pe, batch)


BF16 = mybir.dt.bfloat16

TOKENS = TILES * P
EXPERTS, TOP_K, HIDDEN = 8, 2, 512
DEPTH_SCALE = 1.0 / 12 ** 0.5
SLOT_TILES = TOP_K * TILES + EXPERTS
PARTS = HIDDEN // P


def mixture_of_experts(nc, k, x_sb, wr_dram, wg_dram, wu_dram, wd_dram, xn_dram, y_dram, name):
    with ExitStack() as ctx:
        def sb(n, *shape, dt=F32):
            return ctx.enter_context(nc.sbuf_tensor(name + n, list(shape), dt))

        def psum(cx, n, *shape):
            return cx.enter_context(nc.psum_tensor(name + n, list(shape), F32))

        def signal(n, per=1):
            return Signal(nc.alloc_semaphore(name + n), per)

        wr = sb("wr", P, EXPERTS)
        wg, wu, wd = sb("wg", P, EXPERTS * HIDDEN), sb("wu", P, EXPERTS * HIDDEN), sb("wd", P, EXPERTS * HIDDEN)
        top, best = sb("top", P, TILES, 8), sb("best", P, TILES, 8, dt=U32)
        weight = sb("weight", P, TOP_K, TILES)
        token_row, out_row = sb("token_row", P, SLOT_TILES, dt=U32), sb("out_row", P, SLOT_TILES, dt=U32)
        expert_at = sb("expert_at", 1, SLOT_TILES, dt=I32)
        loaded = signal("loaded")
        route(nc, k, x_sb, wr_dram, wg_dram, wu_dram, wd_dram, xn_dram, wr, wg, wu, wd, top, best, loaded, name)
        place(nc, k, top, best, weight, token_row, out_row, expert_at, name)
        run_experts(nc, k, wg, wu, wd, token_row, out_row, expert_at, xn_dram, y_dram, loaded, name)
        combine(nc, x_sb, weight, y_dram, name)


def route(nc, k, x_sb, wr_dram, wg_dram, wu_dram, wd_dram, xn_dram, wr, wg, wu, wd, top, best, loaded, name):
    with ExitStack() as ctx:
        def sb(n, *shape, dt=F32):
            return ctx.enter_context(nc.sbuf_tensor(name + n, list(shape), dt))

        def signal(n, per=1):
            return Signal(nc.alloc_semaphore(name + n), per)

        G = 8
        stats, moments, rstd = sb("stats", P, G, 6), sb("moments", P, G, 2), sb("rstd", P, G)
        xn, xT = [sb(f"xn{n}", P, G, C) for n in range(2)], sb("xT", P, G, P)
        lg, m8, i8 = sb("lg", P, G, 8), sb("m8", P, G, 8), sb("i8", P, G, 8, dt=U32)
        tp = [ctx.enter_context(nc.psum_tensor(f"{name}tp{n}", [P, 512], F32)) for n in range(2)]
        lp = ctx.enter_context(nc.psum_tensor(f"{name}lp", [P, 512], F32))
        wr_loaded = signal("wr_loaded")
        bn_done, aggr_done, var_ready, root_ready, rstd_ready, xn_ready = (
            signal(n, p) for n, p in (("bn", 8), ("aggr", 8), ("var", 1), ("root", 1), ("rstd", 1), ("xn_ready", 8)))
        tp_full, tp_read, lg_full, lg_ready = signal("tp_full", 2), signal("tp_read", 2), signal("lg_full"), signal("lg_ready")
        m8_ready, i8_ready, kept = signal("m8", 8), signal("i8_", 8), signal("kept", 2)
        stored = [signal(f"stored{n}") for n in range(2)]
        xn_rows = xn_dram.rearrange("(n p) c -> p n c", p=P)
        block = ctx.enter_context(nc.Block())

        @block.sync
        def _(sp):
            sp.dma_start(wr[:, :], wr_dram).then_inc(wr_loaded.sem, 16)
            for g in range(TILES // G):
                sp.wait_ge(xn_ready.sem, 8 * g + 8)
                sp.dma_start(xn_rows[:, G * g:G * g + G, :], xn[g % 2][:, :, :]).then_inc(stored[g % 2].sem, 16)
            for n in range(2):
                sp.wait_ge(stored[n].sem, 8 * (TILES // G))

        @block.vector
        def _(dve):
            def rest(g):
                lg_ready.wait(dve, g, 1)
                if g:
                    kept.wait(dve, g, 0)
                for j in range(G):
                    dve.max(m8[:, j, :], lg[:, j, :]).then_inc(m8_ready.sem, 1)
                m8_ready.wait(dve, g, 8)
                for j in range(G):
                    dve.max_index(i8[:, j, :], m8[:, j, :], lg[:, j, :]).then_inc(i8_ready.sem, 1)
                i8_ready.wait(dve, g, 8)
                dve.tensor_copy(top[:, G * g:G * g + G, :], m8[:, :, :]).then_inc(kept.sem, 1)
                dve.tensor_copy(best[:, G * g:G * g + G, :], i8[:, :, :]).then_inc(kept.sem, 1)

            for g in range(TILES // G):
                if g:
                    xn_ready.wait(dve, g, 0)
                for j in range(G):
                    dve.bn_stats(stats[:, j, :], x_sb[:, (G * g + j) * C:(G * g + j + 1) * C]).then_inc(bn_done.sem, 1)
                bn_done.wait(dve, g, 8)
                for j in range(G):
                    dve.bn_aggr(moments[:, j, :], stats[:, j, :]).then_inc(aggr_done.sem, 1)
                aggr_done.wait(dve, g, 8)
                dve.tensor_scalar(rstd[:, :], moments[:, :, 1], EPS_LN, None, ALU.add).then_inc(var_ready.sem, 1)
                root_ready.wait(dve, g, 1)
                dve.reciprocal(rstd[:, :], rstd[:, :]).then_inc(rstd_ready.sem, 1)
                rstd_ready.wait(dve, g, 1)
                if g >= 2:
                    tp_full.wait(dve, g - 1, 0)
                    dve.wait_ge(stored[g % 2].sem, 16 * (g // 2))
                for j in range(G):
                    dve.tensor_scalar(xn[g % 2][:, j, :], x_sb[:, (G * g + j) * C:(G * g + j + 1) * C], moments[:, j, 0:1],
                                      rstd[:, j:j + 1], ALU.subtract, ALU.mult).then_inc(xn_ready.sem, 1)
                if g:
                    rest(g - 1)
            rest(TILES // G - 1)
            kept.wait(dve, TILES // G, 0)

        @block.scalar
        def _(act):
            for w, dram in ((wg, wg_dram), (wu, wu_dram)):
                act.dma_start(w[:, :].rearrange("c (e h) -> c e h", e=EXPERTS), dram.rearrange("e c h -> c e h")).then_inc(loaded.sem, 16)
            act.dma_start(wd[:, :].rearrange("h (e j c) -> h e j c", e=EXPERTS, j=PARTS),
                          wd_dram.rearrange("e (j h) c -> h e j c", h=P)).then_inc(loaded.sem, 16)
            for g in range(TILES // G):
                var_ready.wait(act, g, 1)
                act.activation(rstd[:, :], rstd[:, :], ACT.Sqrt).then_inc(root_ready.sem, 1)
                if g:
                    lg_full.wait(act, g, 0)
                for h in range(2):
                    tp_full.wait(act, g, h + 1)
                    act.activation(xT[:, 4 * h:4 * h + 4, :].rearrange("p a b -> p (a b)"), tp[h][:, :], ACT.Copy).then_inc(tp_read.sem, 1)
                lg_full.wait(act, g, 1)
                if g:
                    i8_ready.wait(act, g, 0)
                act.activation(lg[:, :, :].rearrange("p a b -> p (a b)"), lp[:, 0:64], ACT.Copy).then_inc(lg_ready.sem, 1)

        @block.tensor
        def _(pe):
            wr_loaded.wait(pe, 0, 16)
            for g in range(TILES // G):
                for h in range(2):
                    xn_ready.wait(pe, g, 4 * h + 4)
                    if g:
                        tp_read.wait(pe, g - 1, h + 1)
                    for j in range(4):
                        mm = pe.transpose(tp[h][:, P * j:P * j + P], xn[g % 2][:, 4 * h + j, :], k["ident"][:, :])
                    mm.then_inc(tp_full.sem, 1)
                tp_read.wait(pe, g, 2)
                if g:
                    lg_ready.wait(pe, g, 0)
                for j in range(G):
                    mm = pe.matmul(lp[:, 8 * j:8 * j + 8], xT[:, j, :], wr[:, :], start=True, stop=True)
                mm.then_inc(lg_full.sem, 1)


def place(nc, k, top, best, weight, token_row, out_row, expert_at, name):
    with ExitStack() as ctx:
        def sb(n, *shape, dt=F32):
            return ctx.enter_context(nc.sbuf_tensor(name + n, list(shape), dt))

        def signal(n, per=1):
            return Signal(nc.alloc_semaphore(name + n), per)

        ei, ef, idx, oh = sb("ei", P, 8, dt=I32), sb("ef", P, 8), sb("idx", P, 2, TILES), sb("oh", P, 2, 8, TILES)
        tok, tok_f = sb("tok", P, TILES, dt=I32), sb("tok_f", P, TILES)
        col, col_f = sb("col", P, P, dt=I32), sb("col_f", P, P)
        spare, spare_f = sb("spare", P, SLOT_TILES, dt=I32), sb("spare_f", P, SLOT_TILES)
        both, cum, reset = sb("both", P, 8, TILES), sb("cum", P, 8, TILES), sb("reset", P, 8, TILES)
        total, cnt, need, end = sb("total", P, 8), sb("cnt", P, 8), sb("need", P, 8), sb("end", P, 8)
        need_i = sb("need_i", P, 8, dt=I32)
        off = sb("off", P, 8)
        pick, slot = sb("pick", P, 8, TILES), sb("slot", P, 2, TILES)
        slot_i, a_i, p_i = (sb(n, P, 2 * TILES, dt=I32) for n in ("slot_i", "a_i", "p_i"))
        a_f, p_f = sb("a_f", P, 2 * TILES), sb("p_f", P, 2 * TILES)
        gap, e1 = sb("gap", P, TILES), sb("e1", P, TILES)
        SOME = 8
        B, hot_a = [sb(f"B{n}", P, SOME, P, dt=BF16) for n in range(2)], [sb(f"hot_a{n}", P, SOME, SLOT_TILES, dt=BF16) for n in range(2)]
        A = [sb(f"A{n}", P, SOME, 2, SLOT_TILES, dt=BF16) for n in range(2)]
        code, code_i, part_i = sb("code", P, 2 * TILES), sb("code_i", P, 2 * TILES, dt=I32), sb("part_i", P, 2 * TILES, dt=I32)
        parts = sb("parts", P, 2, 2 * TILES)
        got, late, empty = sb("got", P, SLOT_TILES), sb("late", P, SLOT_TILES), sb("empty", P, SLOT_TILES)
        row = sb("row", P, SLOT_TILES)
        passed = sb("passed", 1, SLOT_TILES, 8)
        at_f = sb("at_f", 1, SLOT_TILES)
        cp = ctx.enter_context(nc.psum_tensor(f"{name}cp", [P, 512], F32))
        ip = ctx.enter_context(nc.psum_tensor(f"{name}ip", [P, 512], F32))
        counted, iotas, gap_ready, e1_ready = signal("counted"), signal("iotas"), signal("gap_ready"), signal("e1_ready")
        ones_ready = signal("ones_ready")
        total_ready, hot_ready, place_ready, tile_ready, inverted = (signal(n) for n in ("total_ready", "hot_ready", "place_ready", "tile_ready", "inverted"))
        step = signal("step")
        block = ctx.enter_context(nc.Block())

        @block.gpsimd
        def _(pool):
            pool.iota(ei[:, :], [[1, 8]], base=0, channel_multiplier=0).then_inc(iotas.sem, 1)
            pool.iota(tok[:, :], [[P, TILES]], base=1, channel_multiplier=1).then_inc(iotas.sem, 1)
            pool.iota(col[:, :], [[1, P]], base=0, channel_multiplier=0).then_inc(iotas.sem, 1)
            pool.iota(spare[:, :], [[P, SLOT_TILES]], base=TOP_K * TOKENS, channel_multiplier=1).then_inc(iotas.sem, 1)
            for g in range(2 * TILES // SOME):
                hot_ready.wait(pool, 0, g + 1)
                pool.tensor_tensor(A[g % 2][:, :, 1, :], hot_a[g % 2][:, :, :], wide(parts[:, 1, SOME * g:SOME * g + SOME], 2, [P, SOME, SLOT_TILES]),
                                   ALU.mult).then_inc(ones_ready.sem, 1)

        @block.scalar
        def _(act):
            gap_ready.wait(act, 0, 1)
            act.activation(e1[:, :], gap[:, :], ACT.Exp).then_inc(e1_ready.sem, 1)

        @block.tensor
        def _(pe):
            total_ready.wait(pe, 0, 1)
            pe.matmul(cp[:, 0:8], k["before"][:, :], total[:, :], start=True, stop=True)
            pe.matmul(cp[:, 8:16], k["ones"][:, :], total[:, :], start=True, stop=True).then_inc(counted.sem, 1)
            for g in range(2 * TILES // SOME):
                tile_ready.wait(pe, 0, g + 1)
                ones_ready.wait(pe, 0, g + 1)
                place_ready.wait(pe, 0, g + 1)
                for j in range(SOME):
                    mm = pe.matmul(ip[:, 0:2 * SLOT_TILES], B[g % 2][:, j, :], A[g % 2][:, j, :, :].rearrange("p a b -> p (a b)"),
                                   start=(g == 0 and j == 0), stop=(g == 2 * TILES // SOME - 1 and j == SOME - 1))
                mm.then_inc(inverted.sem, 1)

        @block.vector
        def _(dve):
            steps = [0]

            def then(ins):
                steps[0] += 1
                ins.then_inc(step.sem, 1)
                dve.wait_ge(step.sem, steps[0])

            iotas.wait(dve, 0, 4)
            for i, f in ((ei, ef), (tok, tok_f), (col, col_f), (spare, spare_f)):
                then(dve.tensor_copy(f[:, :], i[:, :]))
            dve.tensor_tensor(gap[:, :], top[:, :, 1], top[:, :, 0], ALU.subtract).then_inc(gap_ready.sem, 1)
            then(dve.tensor_copy(idx[:, :, :].rearrange("p a b -> p b a"), best[:, :, 0:2]))
            for n in range(2):
                then(dve.tensor_tensor(oh[:, n, :, :], wide(ef[:, :], 2, [P, 8, TILES]), wide(idx[:, n, :], 1, [P, 8, TILES]), ALU.is_equal))
            then(dve.tensor_tensor(both[:, :, :], oh[:, 0, :, :], oh[:, 1, :, :], ALU.add))
            then(dve.memset(reset[:, :, :], 1.0))
            then(dve.memset(reset[:, :, 0:1], 0.0))
            then(dve.tensor_tensor_scan(cum[:, :, :].rearrange("p a b -> p (a b)"), reset[:, :, :].rearrange("p a b -> p (a b)"),
                                        both[:, :, :].rearrange("p a b -> p (a b)"), 0.0, ALU.mult, ALU.add))
            dve.tensor_copy(total[:, :], cum[:, :, TILES - 1]).then_inc(total_ready.sem, 1)
            e1_ready.wait(dve, 0, 1)
            then(dve.tensor_scalar(gap[:, :], e1[:, :], 1.0, None, ALU.add))
            then(dve.reciprocal(weight[:, 0, :], gap[:, :]))
            then(dve.tensor_tensor(weight[:, 1, :], e1[:, :], weight[:, 0, :], ALU.mult))
            counted.wait(dve, 0, 1)
            then(dve.tensor_copy(off[:, :], cp[:, 0:8]))
            then(dve.tensor_scalar(need_i[:, :], cp[:, 8:16], float(P - 1), None, ALU.add))
            then(dve.tensor_scalar(need_i[:, :], need_i[:, :], 7, None, ALU.logical_shift_right))
            then(dve.tensor_copy(need[:, :], need_i[:, :]))
            then(dve.tensor_tensor_scan(end[:, :], k["ones"][:, 0:8], need[:, :], 0.0, ALU.mult, ALU.add))
            then(dve.tensor_tensor(cnt[:, :], end[:, :], need[:, :], ALU.subtract))
            then(dve.scalar_tensor_tensor(off[:, :], cnt[:, :], float(P), off[:, :], ALU.mult, ALU.add))
            then(dve.tensor_tensor(cum[:, :, :], cum[:, :, :], both[:, :, :], ALU.subtract))
            then(dve.tensor_tensor(cum[:, :, :], cum[:, :, :], wide(off[:, :], 2, [P, 8, TILES]), ALU.add))
            for n in range(2):
                then(dve.tensor_tensor(pick[:, :, :], cum[:, :, :], oh[:, n, :, :], ALU.mult))
                then(dve.tensor_reduce(slot[:, n, :], pick[:, :, :].rearrange("p e t -> p t e"), AX.X, ALU.add))
            then(dve.tensor_copy(slot_i[:, :], slot[:, :, :].rearrange("p a b -> p (a b)")))
            then(dve.tensor_scalar(a_i[:, :], slot_i[:, :], 7, None, ALU.logical_shift_right))
            then(dve.tensor_scalar(p_i[:, :], slot_i[:, :], P - 1, None, ALU.bitwise_and))
            then(dve.tensor_copy(a_f[:, :], a_i[:, :]))
            then(dve.tensor_copy(p_f[:, :], p_i[:, :]))
            then(dve.tensor_copy(code[:, 0:TILES], tok_f[:, :]))
            then(dve.tensor_scalar(code[:, TILES:2 * TILES], tok_f[:, :], float(TOKENS), None, ALU.add))
            then(dve.tensor_copy(code_i[:, :], code[:, :]))
            then(dve.tensor_scalar(part_i[:, :], code_i[:, :], 7, None, ALU.logical_shift_right))
            then(dve.tensor_copy(parts[:, 0, :], part_i[:, :]))
            then(dve.tensor_scalar(part_i[:, :], code_i[:, :], P - 1, None, ALU.bitwise_and))
            then(dve.tensor_copy(parts[:, 1, :], part_i[:, :]))
            for g in range(2 * TILES // SOME):
                some = slice(SOME * g, SOME * g + SOME)
                inverted.wait(dve, 0, g - 1)
                dve.tensor_tensor(hot_a[g % 2][:, :, :], wide(col_f[:, 0:SLOT_TILES], 1, [P, SOME, SLOT_TILES]), wide(a_f[:, some], 2, [P, SOME, SLOT_TILES]),
                                  ALU.is_equal).then_inc(hot_ready.sem, 1)
                dve.tensor_tensor(B[g % 2][:, :, :], wide(col_f[:, :], 1, [P, SOME, P]), wide(p_f[:, some], 2, [P, SOME, P]),
                                  ALU.is_equal).then_inc(place_ready.sem, 1)
                hot_ready.wait(dve, 0, g + 1)
                dve.tensor_tensor(A[g % 2][:, :, 0, :], hot_a[g % 2][:, :, :], wide(parts[:, 0, some], 2, [P, SOME, SLOT_TILES]),
                                  ALU.mult).then_inc(tile_ready.sem, 1)
            then(dve.tensor_tensor(passed[:, :, :], wide(col_f[0:1, 0:SLOT_TILES], 2, [1, SLOT_TILES, 8]), wide(end[0:1, :], 1, [1, SLOT_TILES, 8]), ALU.is_ge))
            then(dve.tensor_reduce(at_f[:, :], passed[:, :, :], AX.X, ALU.add))
            then(dve.tensor_scalar(at_f[:, :], at_f[:, :], float(EXPERTS - 1), float(HIDDEN), ALU.min, ALU.mult))
            then(dve.tensor_copy(expert_at[:, :], at_f[:, :]))
            inverted.wait(dve, 0, 2 * TILES // SOME)
            then(dve.tensor_copy(late[:, :], ip[:, 0:SLOT_TILES]))
            then(dve.scalar_tensor_tensor(got[:, :], late[:, :], float(P), ip[:, SLOT_TILES:2 * SLOT_TILES], ALU.mult, ALU.add))
            then(dve.tensor_scalar(empty[:, :], got[:, :], 0.0, None, ALU.is_equal))
            then(dve.scalar_tensor_tensor(late[:, :], spare_f[:, :], 1.0, empty[:, :], ALU.add, ALU.mult))
            then(dve.scalar_tensor_tensor(row[:, :], got[:, :], -1.0, late[:, :], ALU.add, ALU.add))
            then(dve.tensor_copy(out_row[:, :], row[:, :]))
            then(dve.tensor_scalar(late[:, :], got[:, :], float(TOKENS), float(-TOKENS), ALU.is_gt, ALU.mult))
            then(dve.tensor_tensor(row[:, :], got[:, :], late[:, :], ALU.add))
            then(dve.tensor_scalar(row[:, :], row[:, :], 1.0, -1.0, ALU.max, ALU.add))
            then(dve.tensor_copy(token_row[:, :], row[:, :]))


def run_experts(nc, k, wg, wu, wd, token_row, out_row, expert_at, xn_dram, y_dram, loaded, name):
    with ExitStack() as ctx:
        def sb(n, *shape, dt=F32):
            return ctx.enter_context(nc.sbuf_tensor(name + n, list(shape), dt))

        def psum(n):
            return ctx.enter_context(nc.psum_tensor(name + n, [P, 512], F32))

        def signal(n, per=1):
            return Signal(nc.alloc_semaphore(name + n), per)

        XB = 4
        xg, row_x, row_y = [sb(f"xg{n}", P, C) for n in range(XB)], [sb(f"row_x{n}", P, 1, dt=U32) for n in range(XB)], [sb(f"row_y{n}", P, 1, dt=U32) for n in range(XB)]
        xgT, act_g, h, out = ([sb(f"{m}{n}", P, w) for n in range(2)] for m, w in (("xgT", P), ("sg", 512), ("h", 512), ("yo", C)))
        wg_now, wu_now = ([sb(f"{m}{n}", P, HIDDEN) for n in range(2)] for m in ("wg_now", "wu_now"))
        gp, up = [psum(f"gp{n}") for n in range(2)], [psum(f"up{n}") for n in range(2)]
        xp, dp = psum("xp"), [psum(f"dp{n}") for n in range(2)]
        rows_x, rows_y, gathered = signal("rows_x"), signal("rows_y"), [signal(f"gathered{n}") for n in range(XB)]
        x_full, x_read, gu_full, g_done, h_done = (signal(n) for n in ("x_full", "x_read", "gu_full", "g_done", "h_done"))
        wg_ready, wu_ready, d_full, d_read = (signal(n) for n in ("wg_ready", "wu_ready", "d_full", "d_read"))
        scattered = [signal(f"scattered{n}") for n in range(2)]
        alone = signal("e_alone")
        N = SLOT_TILES

        def column(ap, a):
            return ap[:, bass.ds(a, 1)] if not isinstance(a, int) else ap[:, a:a + 1]

        block = ctx.enter_context(nc.Block())

        @block.gpsimd
        def _(pool):
            def gather(a, u, at):
                if at is None or at >= XB:
                    x_full_wait(pool, a - XB + 1)
                pool.tensor_copy(row_x[u][:, :], column(token_row, a)).then_inc(rows_x.sem, 1)
                pool.wait_ge(rows_x.sem, a + 1)
                pool.sem_inc(alone.sem, 1)
                pool.indirect_dma_start(xg[u][:, :], None, xn_dram, bass.IndirectOffsetOnAxis(row_x[u][:, 0:1], 0)).then_inc(gathered[u].sem, 16)

            def x_full_wait(eng, v):
                eng.wait_ge(x_full.sem, v)
                eng.sem_inc(alone.sem, 1)

            def scatter(a, u, w):
                d_read_wait(a + 1)
                pool.tensor_copy(row_y[u][:, :], column(out_row, a)).then_inc(rows_y.sem, 1)
                pool.wait_ge(rows_y.sem, a + 1)
                pool.sem_inc(alone.sem, 1)
                pool.indirect_dma_start(y_dram, bass.IndirectOffsetOnAxis(row_y[u][:, 0:1], 0), out[w][:, :], None).then_inc(scattered[w].sem, 16)

            def d_read_wait(v):
                pool.wait_ge(d_read.sem, v)
                pool.sem_inc(alone.sem, 1)

            for a in range(3):
                gather(a, a, a)

            def step(s, u, at):
                if at is None or at + 3 < N:
                    gather(s + 3, (u + 3) % 4, None if at is None else at + 3)
                if at is None or at >= 2:
                    scatter(s - 2, (u - 2) % 4, u % 2)

            for s in range(4):
                step(s, s, s)
            with pool.Fori(0, N // 4 - 2) as r:
                for u in range(4):
                    step(r * 4 + (4 + u), u, None)
            for s in range(N - 4, N + 2):
                step(s, s % 4, s)
            for w in range(2):
                pool.wait_ge(scattered[w].sem, 16 * (N // 2))

        @block.tensor
        def _(pe):
            loaded.wait(pe, 0, 48)

            def transpose_x(a, u, at):
                if at is None or at >= 1:
                    pe.wait_ge(x_read.sem, a)
                wait_gathered(pe, a, u)
                pe.transpose(xp[:, 0:P], xg[u][:, :], k["ident"][:, :]).then_inc(x_full.sem, 1)

            def wait_gathered(eng, a, u):
                eng.wait_ge(gathered[u].sem, (a - u + 4) * 4)

            def step(s, u, at):
                if at is None or at >= 1:
                    e_down = pe.value_load(column(expert_at, s - 1), min_val=0, max_val=(EXPERTS - 1) * HIDDEN)
                if at is None or at + 1 < N:
                    transpose_x(s + 1, (u + 1) % 4, None if at is None else at + 1)
                if at is None or at < N:
                    pe.wait_ge(x_read.sem, s + 1)
                    pe.wait_ge(wg_ready.sem, s + 1)
                    pe.wait_ge(wu_ready.sem, s + 1)
                    if at is None or at >= 2:
                        pe.wait_ge(h_done.sem, s - 1)
                    for bank, weights in ((gp, wg_now), (up, wu_now)):
                        for j in range(PARTS):
                            mm = pe.matmul(bank[u % 2][:, P * j:P * j + P], weights[u % 2][:, P * j:P * j + P], xgT[u % 2][:, :], start=True, stop=True)
                    mm.then_inc(gu_full.sem, 1)
                if at is None or at >= 1:
                    v = (u - 1) % 2
                    pe.wait_ge(h_done.sem, s)
                    if at is None or at >= 3:
                        pe.wait_ge(d_read.sem, s - 2)
                    for j in range(PARTS):
                        mm = pe.matmul(dp[v][:, 0:C], h[v][:, P * j:P * j + P], wd[:, bass.ds(e_down + j * C, C)],
                                       start=(j == 0), stop=(j == PARTS - 1))
                    mm.then_inc(d_full.sem, 1)

            transpose_x(0, 0, 0)
            for s in range(4):
                step(s, s, s)
            with pe.Fori(0, N // 4 - 2) as r:
                for u in range(4):
                    step(r * 4 + (4 + u), u, None)
            for s in range(N - 4, N + 1):
                step(s, s % 4, s)

        @block.scalar
        def _(act):
            loaded.wait(act, 0, 48)

            def copy_weights(a, u, at):
                e = act.value_load(column(expert_at, a), min_val=0, max_val=(EXPERTS - 1) * HIDDEN)
                if at is None or at >= 2:
                    act.wait_ge(gu_full.sem, a - 1)
                for now, w, ready in ((wg_now, wg, wg_ready), (wu_now, wu, wu_ready)):
                    act.activation(now[u % 2][:, :], w[:, bass.ds(e, HIDDEN)], ACT.Copy).then_inc(ready.sem, 1)

            def read_x(a, u, at):
                act.wait_ge(x_full.sem, a + 1)
                if at is None or at >= 2:
                    act.wait_ge(gu_full.sem, a - 1)
                act.activation(xgT[u % 2][:, :], xp[:, 0:P], ACT.Copy).then_inc(x_read.sem, 1)

            def step(s, u, at):
                if at is None or at + 1 < N:
                    ahead = None if at is None else at + 1
                    copy_weights(s + 1, u + 1, ahead)
                    read_x(s + 1, u + 1, ahead)
                if at is None or at < N:
                    act.wait_ge(gu_full.sem, s + 1)
                    if at is None or at >= 2:
                        act.wait_ge(h_done.sem, s - 1)
                    act.activation(act_g[u % 2][:, :], gp[u % 2][:, :], ACT.Silu).then_inc(g_done.sem, 1)

            copy_weights(0, 0, 0)
            read_x(0, 0, 0)
            for s in range(4):
                step(s, s, s)
            with act.Fori(0, N // 4 - 2) as r:
                for u in range(4):
                    step(r * 4 + (4 + u), u, None)
            for s in range(N - 4, N):
                step(s, s % 4, s)

        @block.vector
        def _(dve):
            def step(s, u, at):
                if at is None or at < N:
                    dve.wait_ge(g_done.sem, s + 1)
                    if at is None or at >= 2:
                        dve.wait_ge(d_full.sem, s - 1)
                    dve.tensor_tensor(h[u % 2][:, :], act_g[u % 2][:, :], up[u % 2][:, :], ALU.mult).then_inc(h_done.sem, 1)
                if at is None or at >= 1:
                    v = (u - 1) % 2
                    dve.wait_ge(d_full.sem, s)
                    if at is None or at >= 3:
                        dve.wait_ge(scattered[v].sem, (s - 1 - v) * 8)
                    dve.tensor_scalar(out[v][:, :], dp[v][:, 0:C], DEPTH_SCALE, None, ALU.mult).then_inc(d_read.sem, 1)

            for s in range(4):
                step(s, s, s)
            with dve.Fori(0, N // 4 - 2) as r:
                for u in range(4):
                    step(r * 4 + (4 + u), u, None)
            for s in range(N - 4, N + 1):
                step(s, s % 4, s)


def combine(nc, x_sb, weight, y_dram, name):
    with ExitStack() as ctx:
        G, RING = 4, 4
        y = [[ctx.enter_context(nc.sbuf_tensor(f"{name}y{n}{m}", [P, G, C], F32)) for m in range(TOP_K)] for n in range(RING)]
        arrived = [[nc.alloc_semaphore(f"{name}arrived{n}{m}") for m in range(TOP_K)] for n in range(RING)]
        added = nc.alloc_semaphore(f"{name}added")
        rows = y_dram[0:TOP_K * TOKENS, :].rearrange("(m n p) c -> m p n c", m=TOP_K, p=P)
        block = ctx.enter_context(nc.Block())

        def load(eng, m):
            for g in range(TILES // G):
                if g >= RING:
                    eng.wait_ge(added, 2 * G * (g - RING + 1))
                eng.dma_start(y[g % RING][m][:, :, :], rows[m, :, G * g:G * g + G, :]).then_inc(arrived[g % RING][m], 16)

        @block.sync
        def _(sp):
            load(sp, 0)

        @block.scalar
        def _(act):
            load(act, 1)

        @block.vector
        def _(dve):
            for g in range(TILES // G):
                for m in range(TOP_K):
                    dve.wait_ge(arrived[g % RING][m], 16 * (g // RING + 1))
                    if m:
                        dve.wait_ge(added, 2 * G * g + G)
                    for j in range(G):
                        t = G * g + j
                        dve.scalar_tensor_tensor(x_sb[:, t * C:t * C + C], y[g % RING][m][:, j, :], weight[:, m, t:t + 1],
                                                 x_sb[:, t * C:t * C + C], ALU.mult, ALU.add).then_inc(added, 1)
            dve.wait_ge(added, 2 * TILES)


HEADS, KD, VD, TAPS = 8, 128, 32, 4
QUADS = 4
BLOCKS = 2 * HEADS + 2
LEVELS = (2, 4, 8, 16, 32, 64)
EPS_NORM, EPS_RMS = 1e-6, 1e-5
G_, BETA, GAMMA, GAMMA_END, DECAY_END = range(5)


def delta_attention(nc, k, x_sb, w, o_dram):
    with ExitStack() as ctx:
        xT = ctx.enter_context(nc.sbuf_tensor("b_xT", [P, BATCHES, TAPS - 1 + T], F32))
        prm = ctx.enter_context(nc.sbuf_tensor("b_prm", [P, TILES, 5, HEADS], F32))
        delta_inputs(nc, k, x_sb, w, xT, prm)
        delta_chunks(nc, k, w, xT, prm, o_dram)
        delta_output(nc, k, x_sb, w, xT, o_dram)


def delta_inputs(nc, k, x_sb, w, xT, prm):
    with ExitStack() as ctx:
        def sb(n, *shape, dt=F32):
            return ctx.enter_context(nc.sbuf_tensor("b0_" + n, list(shape), dt))

        def signal(n, per=1):
            return Signal(nc.alloc_semaphore("b0_" + n), per)

        G = 8
        stats, moments, rstd = sb("stats", P, G, 6), sb("moments", P, G, 2), sb("rstd", P, G)
        xn = sb("xn", P, G, C)
        wab, a_log, dt = sb("wab", P, 2 * HEADS), sb("a_log", P, HEADS), sb("dt", P, HEADS)
        ab = sb("ab", P, TILES, 2 * HEADS)
        z, nz, lz, eb = (sb(n, P, TILES, HEADS) for n in ("z", "nz", "lz", "eb"))
        tp = [ctx.enter_context(nc.psum_tensor(f"b0_tp{n}", [P, 512], F32)) for n in range(2)]
        ap = ctx.enter_context(nc.psum_tensor("b0_ap", [P, 512], F32))
        gp = [ctx.enter_context(nc.psum_tensor(f"b0_gp{n}", [P, 512], F32)) for n in range(3)]
        loaded, zeroed = signal("loaded"), signal("zeroed")
        bn_done, aggr_done, var_ready, root_ready, rstd_ready, xn_ready = (
            signal(n, p) for n, p in (("bn", 8), ("aggr", 8), ("var", 1), ("root", 1), ("rstd", 1), ("xn_ready", 8)))
        tp_full, tp_read, ab_full, ab_read = signal("tp_full", 2), signal("tp_read", 2), signal("ab_full"), signal("ab_read")
        step, nz_ready, exps, a_ready, g_ready, sums_full, decays = (signal(n) for n in ("step", "nz_ready", "exps", "a_ready", "g_ready", "sums_full", "decays"))
        lz_ready = signal("lz_ready")
        block = ctx.enter_context(nc.Block())

        @block.sync
        def _(sp):
            sp.dma_start(wab[:, 0:HEADS], w["Wa"]).then_inc(loaded.sem, 16)
            sp.dma_start(wab[:, HEADS:2 * HEADS], w["Wb"]).then_inc(loaded.sem, 16)
            sp.dma_start(a_log[:, :], w["A_log"].partition_broadcast(P)).then_inc(loaded.sem, 16)
            sp.dma_start(dt[:, :], w["dt_bias"].partition_broadcast(P)).then_inc(loaded.sem, 16)

        @block.gpsimd
        def _(pool):
            pool.memset(xT[:, :, 0:TAPS - 1], 0.0).then_inc(zeroed.sem, 1)

        @block.vector
        def _(dve):
            for g in range(BATCHES):
                if g:
                    xn_ready.wait(dve, g, 0)
                for j in range(G):
                    dve.bn_stats(stats[:, j, :], x_sb[:, (G * g + j) * C:(G * g + j + 1) * C]).then_inc(bn_done.sem, 1)
                bn_done.wait(dve, g, 8)
                for j in range(G):
                    dve.bn_aggr(moments[:, j, :], stats[:, j, :]).then_inc(aggr_done.sem, 1)
                aggr_done.wait(dve, g, 8)
                dve.tensor_scalar(rstd[:, :], moments[:, :, 1], EPS_LN, None, ALU.add).then_inc(var_ready.sem, 1)
                root_ready.wait(dve, g, 1)
                dve.reciprocal(rstd[:, :], rstd[:, :]).then_inc(rstd_ready.sem, 1)
                rstd_ready.wait(dve, g, 1)
                tp_full.wait(dve, g, 0)
                for j in range(G):
                    dve.tensor_scalar(xn[:, j, :], x_sb[:, (G * g + j) * C:(G * g + j + 1) * C], moments[:, j, 0:1],
                                      rstd[:, j:j + 1], ALU.subtract, ALU.mult).then_inc(xn_ready.sem, 1)
            steps = [0]

            def then(ins):
                steps[0] += 1
                ins.then_inc(step.sem, 1)
                dve.wait_ge(step.sem, steps[0])

            loaded.wait(dve, 0, 64)
            ab_read.wait(dve, BATCHES, 0)
            then(dve.tensor_tensor(z[:, :, :], ab[:, :, 0:HEADS], wide(dt[:, :], 1, [P, TILES, HEADS]), ALU.add))
            then(dve.tensor_scalar(nz[:, :, :], z[:, :, :], -1.0, None, ALU.mult))
            dve.tensor_tensor(nz[:, :, :], nz[:, :, :], z[:, :, :], ALU.min).then_inc(nz_ready.sem, 1)
            lz_ready.wait(dve, 0, 1)
            then(dve.tensor_scalar(z[:, :, :], z[:, :, :], 0.0, None, ALU.max))
            then(dve.tensor_tensor(z[:, :, :], z[:, :, :], lz[:, :, :], ALU.add))
            a_ready.wait(dve, 0, 1)
            then(dve.tensor_tensor(z[:, :, :], z[:, :, :], wide(a_log[:, :], 1, [P, TILES, HEADS]), ALU.mult))
            dve.tensor_scalar(prm[:, :, G_, :], z[:, :, :], -1.0, None, ALU.mult).then_inc(g_ready.sem, 1)
            exps.wait(dve, 0, 2)
            then(dve.tensor_scalar(eb[:, :, :], eb[:, :, :], 1.0, None, ALU.add))
            then(dve.reciprocal(eb[:, :, :], eb[:, :, :]))
            then(dve.tensor_scalar(prm[:, :, BETA, :], eb[:, :, :], 2.0, None, ALU.mult))
            decays.wait(dve, 0, 3)
            then(dve.memset(prm[:, :, GAMMA_END:DECAY_END + 1, :].rearrange("p (b c) a h -> p b c a h", c=TPB)[:, :, TPB - 1], 0.0))

        @block.scalar
        def _(act):
            for g in range(BATCHES):
                var_ready.wait(act, g, 1)
                act.activation(rstd[:, :], rstd[:, :], ACT.Sqrt).then_inc(root_ready.sem, 1)
                for h in range(2):
                    tp_full.wait(act, g, h + 1)
                    act.activation(xT[:, g, TAPS - 1 + 512 * h:TAPS - 1 + 512 * h + 512], tp[h][:, :], ACT.Copy).then_inc(tp_read.sem, 1)
                ab_full.wait(act, g, 1)
                act.activation(ab[:, G * g:G * g + G, :].rearrange("p a b -> p (a b)"), ap[:, 0:128], ACT.Copy).then_inc(ab_read.sem, 1)
            loaded.wait(act, 0, 64)
            act.activation(a_log[:, :], a_log[:, :], ACT.Exp).then_inc(a_ready.sem, 1)
            nz_ready.wait(act, 0, 1)
            act.activation(nz[:, :, :], nz[:, :, :], ACT.Exp).then_inc(exps.sem, 1)
            ab_read.wait(act, BATCHES, 0)
            act.activation(eb[:, :, :], ab[:, :, HEADS:2 * HEADS], ACT.Exp, scale=-1.0).then_inc(exps.sem, 1)
            exps.wait(act, 0, 1)
            act.activation(lz[:, :, :], nz[:, :, :], ACT.Ln, bias=1.0).then_inc(lz_ready.sem, 1)
            sums_full.wait(act, 0, 1)
            for n, which in enumerate((GAMMA, GAMMA_END, DECAY_END)):
                act.activation(prm[:, :, which, :], gp[n][:, 0:256].rearrange("p (a b) -> p a b", b=HEADS), ACT.Exp).then_inc(decays.sem, 1)

        @block.tensor
        def _(pe):
            loaded.wait(pe, 0, 64)
            for g in range(BATCHES):
                for h in range(2):
                    xn_ready.wait(pe, g, 4 * h + 4)
                    if g:
                        tp_read.wait(pe, g - 1, h + 1)
                    for j in range(4):
                        mm = pe.transpose(tp[h][:, P * j:P * j + P], xn[:, 4 * h + j, :], k["ident"][:, :])
                    mm.then_inc(tp_full.sem, 1)
                tp_read.wait(pe, g, 2)
                ab_read.wait(pe, g, 0)
                for j in range(G):
                    mm = pe.matmul(ap[:, 16 * j:16 * j + 16], xT[:, g, TAPS - 1 + P * j:TAPS - 1 + P * j + P], wab[:, :], start=True, stop=True)
                mm.then_inc(ab_full.sem, 1)
            g_ready.wait(pe, 0, 1)
            for n, m in enumerate(("upto", "ones", "after")):
                mm = pe.matmul(gp[n][:, 0:256], k[m][:, :], prm[:, :, G_, :], start=True, stop=True)
            mm.then_inc(sums_full.sem, 1)


def delta_chunks(nc, k, w, xT, prm, o_dram):
    with ExitStack() as ctx:
        def sb(n, *shape, dt=F32):
            return ctx.enter_context(nc.sbuf_tensor("b1_" + n, list(shape), dt))

        def psum(n):
            return ctx.enter_context(nc.psum_tensor("b1_" + n, [P, 512], F32))

        def signal(n, per=1):
            return Signal(nc.alloc_semaphore("b1_" + n), per)

        NL_ = len(LEVELS)
        PASSES = TILES // 2
        STATE = 3 * NL_ + 1
        SLOTS = STATE + 6
        PAIRS_, K_T, Q_T, V_T, E_ = BLOCKS // 2, 3, 7, 10, STATE
        ORDER = (0, 2, 1, 3)
        wq, wk, wv = sb("wq", P, HEADS * KD), sb("wk", P, HEADS * KD), sb("wv", P, HEADS * VD)
        taps = sb("taps", P, BLOCKS, TAPS)
        masks = [sb(f"mask{s}", P, 64) for s in LEVELS]
        mask1 = sb("mask1", P, P)
        W_EXT = TAPS - 1 + P
        PRE = 4
        xh, vT = sb("xh", P, 2, W_EXT), sb("vT", P, 2, 2, P)
        cur_ = [sb(f"cur{e}", P, 2, 5, HEADS) for e in range(2)]
        pre = [sb(f"pre{n}", P, 2, P) for n in range(PRE)]
        kq_ = [sb(f"kq{e}", P, 2, HEADS, 2, P) for e in range(2)]
        sq = [sb(f"sq{n}", P, 4, P) for n in range(2)]
        norm_, rnorm_ = ([sb(f"{n}{e}", P, 2, 2, HEADS) for e in range(2)] for n in ("norm", "rnorm"))
        s__ = [sb(f"s_{e}", P, 2, HEADS) for e in range(2)]
        nv_ = [sb(f"nv{e}", P, 2, 2, 4 * VD) for e in range(2)]
        gm = [sb(f"gm{n}", P, 4, P) for n in range(2)]
        kt_, CT_, PT_, XT_ = ([[sb(f"{n}{e}{q}", P, 4, P) for q in range(QUADS)] for e in range(2)] for n in ("kt", "CT", "PT", "XT"))
        D, X = ([sb(f"{n}{q}", P, 4, P) for q in range(QUADS)] for n in ("D", "X"))
        W = [sb(f"W{q}", P, 4, 64) for q in range(QUADS)]
        S = sb("S", P, QUADS, 4 * VD)
        r, z, wd, o1 = ([sb(f"{n}{q}", P, 4, VD) for q in range(QUADS)] for n in ("r", "z", "wd", "o1"))
        ob = sb("ob", P, QUADS, 4 * VD)
        pj, mx, lv = [psum(f"pj{n}") for n in range(2)], [psum(f"mx{n}") for n in range(2)], [psum(f"lv{q}") for q in range(QUADS)]

        loaded, zeroed, masked, reset = signal("loaded"), signal("zeroed"), signal("masked"), signal("reset")
        alone, pe_alone = signal("alone"), signal("pe_alone")
        xh_ready, cur_part, cur_ready = signal("xh_ready"), signal("cur_part"), signal("cur_ready")
        pj_full, tap_done, tap_next, conv_done, silu_done = (
            signal(n, p * BLOCKS) for n, p in (("pj_full", 1), ("tap_done", 1), ("tap_next", 2), ("conv_done", 1), ("silu_done", 1)))
        squared, n2_ready, n_root, n_step = (
            signal(n, p) for n, p in (("squared", 2 * QUADS), ("n2_ready", 2 * QUADS), ("n_root", 1), ("n_step", 4)))
        v_full, nv_ready = signal("v_full"), signal("nv_ready", 2)
        kt_full, kt_ready, qt_full, gm_ready, e_full, d_ready, kq_full, ct_ready, pt_ready, pt_masked, x1_part, x1_ready, x_full, x_ready = (
            signal(n, QUADS) for n in ("kt_full", "kt_ready", "qt_full", "gm_ready", "e_full", "d_ready", "kq_full", "ct_ready", "pt_ready",
                                       "pt_masked", "x1_part", "x1_ready", "x_full", "x_ready"))
        half_ready = signal("half_ready")
        w_full, w_ready, dx_full, dx_added, t_full, xt_ready = (
            signal(n, NL_ * QUADS) for n in ("w_full", "w_ready", "dx_full", "dx_added", "t_full", "xt_ready"))
        s_full, rg_ready, r_ready, qs_ready, z_full, z_ready, wd_ready, sg_ready, pw_full, o_sum, s_done, o_done = (
            signal(n, QUADS) for n in ("s_full", "rg_ready", "r_ready", "qs_ready", "z_full", "z_ready", "wd_ready", "sg_ready", "pw_full",
                                       "o_sum", "s_done", "o_done"))
        stored = signal("stored", 32)

        def flat(ap):
            return ap.rearrange("p a b -> p (a b)")

        def halves(ap, s, which):
            return ap.rearrange("p h (b t s) -> p h b t s", t=2, s=s)[:, :, :, which, :]

        def rows(l):
            return P // 2 if l == NL_ - 1 else P

        def quad(q):
            return q // 2, slice(4 * (q % 2), 4 * (q % 2) + 4)

        def run(eng, front, back):
            def beside(n, e):
                for slot in range(SLOTS):
                    back(n, e, slot)
                    front(n + 1, 1 - e, slot)
            for slot in range(SLOTS):
                front(0, 0, slot)
            beside(0, 0)
            with eng.Fori(0, (PASSES - 2) // 2) as two:
                beside(two * 2 + 1, 1)
                beside(two * 2 + 2, 0)
            for slot in range(SLOTS):
                back(PASSES - 1, 1, slot)

        o_rows = o_dram.rearrange("(b c p) v -> p b c v", p=P, c=TPB)
        block = ctx.enter_context(nc.Block())

        @block.sync
        def _(sp):
            sp.dma_start(wk[:, :], w["Wk"]).then_inc(loaded.sem, 16)
            sp.dma_start(wq[:, :], w["Wq"]).then_inc(loaded.sem, 16)
            sp.dma_start(wv[:, :], w["Wv"]).then_inc(loaded.sem, 16)
            for n, name in ((0, "conv_k"), (HEADS, "conv_q")):
                sp.dma_start(taps[:, n:n + HEADS, :], w[name].rearrange("(h p) t -> p h t", p=P)).then_inc(loaded.sem, 16)
            sp.dma_start(taps[:, 2 * HEADS:, :], w["conv_v"].rearrange("(h p) t -> p h t", p=P)).then_inc(loaded.sem, 16)
            with sp.Fori(0, PASSES // TPB) as pair, sp.Fori(0, TPB) as c:
                o_done.wait(sp, pair * TPB + c, QUADS)
                for i in range(2):
                    sp.dma_start(o_rows[:, bass.ds(pair * 2 + i, 1), bass.ds(c, 1), :].rearrange("p b c v -> p (b c v)"),
                                 flat(ob[:, 2 * i:2 * i + 2, :])).then_inc(stored.sem, 16)
            stored.wait(sp, PASSES, 0)

        @block.gpsimd
        def _(pool):
            for m in masks:
                pool.memset(m[:, :], -1.0).then_inc(zeroed.sem, 1)
            pool.memset(mask1[:, :], 0.0).then_inc(zeroed.sem, 1)
            pool.wait_ge(zeroed.sem, NL_ + 1)
            for l, (s, m) in enumerate(zip(LEVELS, masks)):
                v = m[:, :].rearrange("p (b s) -> p b s", s=s)
                first, apart = (s, 2 * s) if rows(l) == P else (0, s)
                pool.affine_select(out=v, in_=v, compare_op=ALU.is_ge, fill=0.0, base=-first, pattern=[[-apart, 64 // s], [0, s]],
                                   channel_multiplier=1).then_inc(masked.sem, 1)
            v = mask1[:, :].rearrange("p (a t) -> p a t", t=2)[:, :, 1]
            pool.affine_select(out=v, in_=v, compare_op=ALU.not_equal, fill=-1.0, base=0, pattern=[[2, 64]],
                               channel_multiplier=-1).then_inc(masked.sem, 1)
            pool.wait_ge(masked.sem, NL_ + 1)
            for l, (s, m) in enumerate(zip(LEVELS, masks)):
                v = m[:, :].rearrange("p (b s) -> p b s", s=s)
                first, apart = (s, 2 * s) if rows(l) == P else (0, s)
                pool.affine_select(out=v, in_=v, compare_op=ALU.is_ge, fill=0.0, base=first + s - 1, pattern=[[apart, 64 // s], [0, s]],
                                   channel_multiplier=-1).then_inc(masked.sem, 1)

            def front(m, e, slot):
                cur, CT, PT, XT = cur_[e], CT_[e], PT_[e], XT_[e]

                def build(q):
                    i, hs = quad(q)
                    e_full.wait(pool, m - 1 if q < 2 else m, q + 3 if q < 2 else q - 1)
                    pool.tensor_tensor(gm[q % 2][:, :, :], wide(k["upto"][:, :], 1, [P, 4, P]), wide(cur[:, i, G_, hs], 2, [P, 4, P]),
                                       ALU.mult).then_inc(gm_ready.sem, 1)
                if slot == 0:
                    cur_ready.wait(pool, m, 1)
                    build(0)
                    build(1)
                for q in range(QUADS):
                    if slot == E_ + 1 + q:
                        if q + 2 < QUADS:
                            build(q + 2)
                        ct_ready.wait(pool, m, q + 1)
                        z_full.wait(pool, m - 2, QUADS)
                        pool.tensor_tensor(XT[q][:, :, :], CT[q][:, :, :], wide(mask1[:, :], 1, [P, 4, P]), ALU.mult).then_inc(x1_part.sem, 1)
                        x1_part.wait(pool, m, q + 1)
                        pool.tensor_tensor(XT[q][:, :, :], XT[q][:, :, :], wide(k["ident"][:, :], 1, [P, 4, P]), ALU.add).then_inc(x1_ready.sem, 1)
                        pt_ready.wait(pool, m, q + 1)
                        pool.tensor_tensor(PT[q][:, :, :], PT[q][:, :, :], wide(k["upto"][:, :], 1, [P, 4, P]), ALU.mult).then_inc(pt_masked.sem, 1)

            def back(n, e, slot):
                pass
            run(pool, front, back)

        @block.scalar
        def _(act):
            loaded.wait(act, 0, 96)

            def tokens(m):
                pj_full.wait(act, m - 1, BLOCKS)
                act.activation(xh[:, :, :], xT[:, bass.ds((m // TPB) * 2, 2), bass.ds((m % TPB) * P, W_EXT)], ACT.Copy).then_inc(xh_ready.sem, 1)

            def front(m, e, slot):
                kq, norm, kt = kq_[e], norm_[e], kt_[e]

                def silu(b):
                    conv_done.wait(act, m, b + 1)
                    if b == 0:
                        s_full.wait(act, m - 2, QUADS)
                    if b == 2 * HEADS:
                        v_full.wait(act, m - 1, 1)
                    act.activation(kq[:, :, b % HEADS, b // HEADS, :] if b < 2 * HEADS else vT[:, :, b - 2 * HEADS, :],
                                   pre[b % PRE][:, :, :], ACT.Silu).then_inc(silu_done.sem, 1)
                if slot < PAIRS_:
                    for b in (2 * slot, 2 * slot + 1):
                        pj_full.wait(act, m, b + 1)
                        silu_done.wait(act, m - 1 if b < PRE else m, BLOCKS if b < PRE else b - PRE + 1)
                        act.activation(pre[b % PRE][:, :, :], pj[b % 2][:, 0:2 * W_EXT].rearrange("p (i t) -> p i t", i=2)[:, :, 0:P],
                                       ACT.Copy, scale=taps[:, b, 0:1]).then_inc(tap_done.sem, 1)
                if 0 < slot <= PAIRS_:
                    silu(2 * slot - 2)
                    silu(2 * slot - 1)
                def square(u, bank):
                    n2_ready.wait(act, m - 1 if u < 2 else m, 2 * QUADS - 1 + u if u < 2 else u - 1)
                    act.activation(flat(sq[u % 2][:, :, :]), bank[:, :], ACT.Square).then_inc(squared.sem, 1)

                if slot == E_:
                    n2_ready.wait(act, m, 2 * QUADS)
                    act.activation(norm[:, :, :, :], norm[:, :, :, :], ACT.Sqrt).then_inc(n_root.sem, 1)
                for u, q in enumerate(ORDER):
                    if slot == K_T + u:
                        kt_full.wait(act, m, u + 1)
                        pw_full.wait(act, m - 2, QUADS)
                        act.activation(flat(kt[q][:, :, :]), mx[1][:, :], ACT.Copy).then_inc(kt_ready.sem, 1)
                        square(u, mx[1])
                    if slot == Q_T + u:
                        qt_full.wait(act, m, u + 1)
                        square(QUADS + u, mx[0])
                for q in range(QUADS):
                    if slot == E_ + q:
                        e_full.wait(act, m, q + 1)
                        pt_ready.wait(act, m - 1, q + 1)
                        act.activation(flat(D[q][:, :, :]), mx[0][:, :], ACT.Exp).then_inc(d_ready.sem, 1)

            def back(n, e, slot):
                if slot == 0 and not (isinstance(n, int) and n == PASSES - 1):
                    tokens(n + 1)
                for q in range(QUADS):
                    if slot == 0:
                        x_full.wait(act, n, q + 1)
                        act.activation(flat(X[q][:, :, :]), lv[q][:, :], ACT.Copy).then_inc(x_ready.sem, 1)
                    elif slot < STATE and slot % 3 == 0:
                        t_full.wait(act, n, QUADS * (slot // 3 - 1) + q + 1)
                        l = slot // 3
                        part = rows(l) if l < NL_ else P
                        act.activation(flat(XT_[e][q][0:part, :, :]), lv[q][0:part, :], ACT.Copy).then_inc(xt_ready.sem, 1)
            tokens(0)
            run(act, front, back)

        @block.vector
        def _(dve):
            dve.memset(S[:, :, :], 0.0).then_inc(reset.sem, 1)
            reset.wait(dve, 0, 1)
            loaded.wait(dve, 0, 96)
            dve.wait_ge(masked.sem, 2 * NL_ + 1)

            def front(m, e, slot):
                cur, norm, rnorm, s_, nv, CT, PT = cur_[e], norm_[e], rnorm_[e], s__[e], nv_[e], CT_[e], PT_[e]
                if slot == 0:
                    o_done.wait(dve, m - 2, QUADS)
                    s_done.wait(dve, m - 2, QUADS)
                    dve.sem_inc(alone.sem, 1)
                    for i in range(2):
                        dve.tensor_copy(cur[:, i, :, :].rearrange("p a b -> p (a b)"),
                                        prm[:, :, :, :].rearrange("p t a b -> p t (a b)")[:, bass.ds((m // TPB) * (2 * TPB) + m % TPB + i * TPB, 1), :].rearrange("p t a -> p (t a)")).then_inc(
                            cur_part.sem if i == 0 else cur_ready.sem, 1)
                if slot < PAIRS_:
                    for t in range(1, TAPS):
                        for b in (2 * slot, 2 * slot + 1):
                            if t == 1:
                                tap_done.wait(dve, m, b + 1)
                            else:
                                tap_next.wait(dve, m, 4 * slot + 2 * (t - 2) + b % 2 + 1)
                            src = pj[b % 2][:, 0:2 * W_EXT].rearrange("p (i t) -> p i t", i=2)
                            dve.scalar_tensor_tensor(pre[b % PRE][:, :, :], src[:, :, t:t + P], taps[:, b, t:t + 1], pre[b % PRE][:, :, :],
                                                     ALU.mult, ALU.add).then_inc((conv_done if t == TAPS - 1 else tap_next).sem, 1)
                for u, q in enumerate(ORDER * 2):
                    if slot == K_T + 1 + u:
                        i, hs = quad(q)
                        squared.wait(dve, m, u + 1)
                        dve.tensor_reduce(norm[:, u // QUADS, i, hs], sq[u % 2][:, :, :], AX.X, ALU.add).then_inc(n2_ready.sem, 1)
                if slot == E_ + 1:
                    n_root.wait(dve, m, 1)
                    dve.tensor_scalar(norm[:, :, :, :], norm[:, :, :, :], EPS_NORM, None, ALU.max).then_inc(n_step.sem, 1)
                    n_step.wait(dve, m, 1)
                    dve.reciprocal(rnorm[:, :, :, :], norm[:, :, :, :]).then_inc(n_step.sem, 1)
                    v_full.wait(dve, m, 1)
                    for i in range(2):
                        dve.tensor_tensor(nv[:, i, :, :].rearrange("p a (h d) -> p (a h) d", d=VD), mx[1][:, 256 * i:256 * i + 256].rearrange("p (h d) -> p h d", d=VD),
                                          wide(norm[:, 0, i, :], 2, [P, HEADS, VD]), ALU.mult).then_inc(nv_ready.sem, 1)
                    n_step.wait(dve, m, 2)
                    dve.tensor_tensor(s_[:, :, :], rnorm[:, 0, :, :], rnorm[:, 0, :, :], ALU.mult).then_inc(n_step.sem, 1)
                    n_step.wait(dve, m, 3)
                    dve.tensor_tensor(s_[:, :, :], s_[:, :, :], cur[:, :, BETA, :], ALU.mult).then_inc(n_step.sem, 1)
                for q in range(QUADS):
                    i, hs = quad(q)
                    if slot == E_ + 1 + q:
                        n_step.wait(dve, m, 4)
                        d_ready.wait(dve, m, q + 1)
                        kq_full.wait(dve, m, q + 1)
                        both = [pj[g][:, :].rearrange("p (h m t) -> p h m t", h=2, m=2) for g in range(2)]
                        for h in range(4):
                            dve.scalar_tensor_tensor(CT[q][:, h, :], both[h // 2][:, h % 2, 0, :], s_[:, i, hs][:, h:h + 1], D[q][:, h, :],
                                                     ALU.mult, ALU.mult).then_inc((ct_ready if h == 3 else half_ready).sem, 1)
                        for g in range(2):
                            sl = slice(2 * g, 2 * g + 2)
                            dve.tensor_tensor(PT[q][:, sl, :], both[g][:, :, 1, :], D[q][:, sl, :], ALU.mult).then_inc((pt_ready if g else half_ready).sem, 1)

            def back(n, e, slot):
                cur, rnorm, s_, nv = cur_[e], rnorm_[e], s__[e], nv_[e]
                if 0 < slot < STATE and slot % 3 != 0:
                    l = slot // 3
                    s = LEVELS[l]
                    for q in range(QUADS):
                        if slot % 3 == 1:
                            w_full.wait(dve, n, QUADS * l + q + 1)
                            part = rows(l)
                            dve.tensor_tensor(W[q][0:part, :, :], lv[q][0:part, 0:256].rearrange("p (h c) -> p h c", h=4),
                                              wide(masks[l][0:part, :], 1, [part, 4, 64]), ALU.mult).then_inc(w_ready.sem, 1)
                        else:
                            dx_full.wait(dve, n, QUADS * l + q + 1)
                            low = P - rows(l)
                            v = halves(X[q][low:, :, :], s, 0)
                            dve.tensor_tensor(v, v, lv[q][low:, 256:512].rearrange("p (h b s) -> p h b s", h=4, s=s), ALU.add).then_inc(dx_added.sem, 1)
                if slot == STATE:
                    o_done.wait(dve, n - 1, QUADS)
                    s_done.wait(dve, n - 1, QUADS)
                if slot == STATE + 4:
                    stored.wait(dve, n - 1, 32)
                for q in range(QUADS):
                    i, hs = quad(q)

                    def per_token(ap):
                        return wide(ap, 2, [P, 4, VD])

                    def per_head(ap):
                        return ap.rearrange("p (h d) -> p h d", d=VD)

                    if slot == STATE + q // 2:
                        s_full.wait(dve, n, q + 1)
                        dve.tensor_tensor(r[q][:, :, :], per_head(lv[q][:, 0:P]), per_token(cur[:, i, GAMMA, hs]), ALU.mult).then_inc(rg_ready.sem, 1)
                        dve.tensor_tensor(o1[q][:, :, :], per_head(lv[q][:, P:2 * P]), per_token(cur[:, i, GAMMA, hs]), ALU.mult).then_inc(qs_ready.sem, 1)
                        rg_ready.wait(dve, n, q + 1)
                        dve.tensor_tensor(r[q][:, :, :], per_head(nv[:, i, q % 2, :]), r[q][:, :, :], ALU.subtract).then_inc(r_ready.sem, 1)
                    if slot == STATE + 2 + q // 2:
                        z_full.wait(dve, n, q + 1)
                        dve.tensor_tensor(z[q][:, :, :], per_head(lv[q][:, 0:P]), per_token(s_[:, i, hs]), ALU.mult).then_inc(z_ready.sem, 1)
                        dve.tensor_tensor(per_head(S[:, q, :]), per_head(S[:, q, :]), per_token(cur[:, i, GAMMA_END, hs]), ALU.mult).then_inc(sg_ready.sem, 1)
                        z_ready.wait(dve, n, q + 1)
                        dve.tensor_tensor(wd[q][:, :, :], z[q][:, :, :], per_token(cur[:, i, DECAY_END, hs]), ALU.mult).then_inc(wd_ready.sem, 1)
                    if slot == STATE + 4 + q // 2:
                        pw_full.wait(dve, n, q + 1)
                        sg_ready.wait(dve, n, q + 1)
                        qs_ready.wait(dve, n, q + 1)
                        dve.tensor_tensor(o1[q][:, :, :], o1[q][:, :, :], per_head(lv[q][:, P:2 * P]), ALU.add).then_inc(o_sum.sem, 1)
                        dve.tensor_tensor(S[:, q, :], S[:, q, :], lv[q][:, 2 * P:3 * P], ALU.add).then_inc(s_done.sem, 1)
                        o_sum.wait(dve, n, q + 1)
                        dve.tensor_tensor(per_head(ob[:, q, :]), o1[q][:, :, :], per_token(rnorm[:, 1, i, hs]), ALU.mult).then_inc(o_done.sem, 1)
            run(dve, front, back)

        @block.tensor
        def _(pe):
            loaded.wait(pe, 0, 96)
            reset.wait(pe, 0, 1)

            def front(m, e, slot):
                kq = kq_[e]

                def weights(b):
                    src = wk if b < HEADS else wq if b < 2 * HEADS else wv
                    return src[:, (b % HEADS) * P:(b % HEADS) * P + P]

                if slot == 0:
                    xh_ready.wait(pe, m, 1)
                    pt_ready.wait(pe, m - 1, QUADS)
                if slot < PAIRS_:
                    for b in (2 * slot, 2 * slot + 1):
                        if b >= 2:
                            conv_done.wait(pe, m, b - 1)
                        pe.matmul(pj[b % 2][:, 0:2 * W_EXT], weights(b), flat(xh[:, :, :]), start=True, stop=True).then_inc(pj_full.sem, 1)
                if slot == V_T:
                    silu_done.wait(pe, m, BLOCKS)
                    squared.wait(pe, m, QUADS)
                    for i in range(2):
                        for hq in range(2):
                            mm = pe.transpose(mx[1][:, 256 * i + P * hq:256 * i + P * hq + P], vT[:, i, hq, :], k["ident"][:, :])
                    mm.then_inc(v_full.sem, 1)
                for u, q in enumerate(ORDER):
                    i, hq = q // 2, q % 2
                    if slot == K_T + u:
                        silu_done.wait(pe, m, 4 * hq + 4)
                        if u == 0:
                            nv_ready.wait(pe, m - 1, 2)
                        else:
                            squared.wait(pe, m, u)
                        for h in range(4):
                            mm = pe.transpose(mx[1][:, P * h:P * h + P], kq[:, i, 4 * hq + h, 0, :], k["ident"][:, :])
                        mm.then_inc(kt_full.sem, 1)
                    if slot == Q_T + u:
                        silu_done.wait(pe, m, HEADS + 4 * hq + 4)
                        if u == 0:
                            d_ready.wait(pe, m - 1, QUADS)
                        else:
                            squared.wait(pe, m, QUADS + u)
                        for h in range(4):
                            mm = pe.transpose(mx[0][:, P * h:P * h + P], kq[:, i, 4 * hq + h, 1, :], k["ident"][:, :])
                        mm.then_inc(qt_full.sem, 1)
                for q in range(QUADS):
                    i, hq = q // 2, q % 2
                    if slot == E_ + q:
                        gm_ready.wait(pe, m, q + 1)
                        if q:
                            d_ready.wait(pe, m, q)
                        else:
                            squared.wait(pe, m, 2 * QUADS)
                        pe.matmul(mx[0][:, :], k["after"][:, :], flat(gm[q % 2][:, :, :]), start=True, stop=True).then_inc(e_full.sem, 1)
                    if slot == E_ + 1 + q:
                        if q:
                            pt_ready.wait(pe, m, q)
                        else:
                            conv_done.wait(pe, m, BLOCKS)
                        for h in range(4):
                            mm = pe.matmul(pj[h // 2][:, 256 * (h % 2):256 * (h % 2) + 256], kq[:, i, 4 * hq + h, 0, :],
                                           kq[:, i, 4 * hq + h, :, :].rearrange("p m t -> p (m t)"), start=True, stop=True)
                        mm.then_inc(kq_full.sem, 1)

            def back(n, e, slot):
                kq, kt, CT, PT, XT = kq_[e], kt_[e], CT_[e], PT_[e], XT_[e]
                l = (slot - 1) // 3
                for q in range(QUADS):
                    i, hq = q // 2, q % 2
                    if slot == 0:
                        x1_ready.wait(pe, n, q + 1)
                        o_done.wait(pe, n - 1, q + 1)
                        s_done.wait(pe, n - 1, q + 1)
                        for h in range(4):
                            mm = pe.transpose(lv[q][:, P * h:P * h + P], XT[q][:, h, :], k["ident"][:, :])
                        mm.then_inc(x_full.sem, 1)
                    elif slot < STATE and slot % 3 == 1:
                        x_ready.wait(pe, n, q + 1)
                        if l:
                            xt_ready.wait(pe, n, QUADS * (l - 1) + q + 1)
                        for h in range(4):
                            mm = pe.matmul(lv[q][0:rows(l), 64 * h:64 * h + 64], CT[q][:, h, P - rows(l):P], halves(X[q][:, :, :], LEVELS[l], 0)[:, h], start=True, stop=True)
                        mm.then_inc(w_full.sem, 1)
                    elif slot < STATE and slot % 3 == 2:
                        w_ready.wait(pe, n, QUADS * l + q + 1)
                        if l == NL_ - 1:
                            pe.sem_inc(pe_alone.sem, 1)
                        for h in range(4):
                            mm = pe.matmul(lv[q][P - rows(l):P, 256 + 64 * h:256 + 64 * h + 64], XT[q][0:rows(l), h, P - rows(l):P], W[q][0:rows(l), h, :], start=True, stop=True)
                        mm.then_inc(dx_full.sem, 1)
                    elif slot < STATE:
                        dx_added.wait(pe, n, QUADS * l + q + 1)
                        pe.sem_inc(pe_alone.sem, 1)
                        for h in range(4):
                            part = rows(l + 1) if l + 1 < NL_ else P
                            mm = pe.transpose(lv[q][0:part, P * h:P * h + P], X[q][:, h, P - part:P], k["ident"][:, :])
                        mm.then_inc(t_full.sem, 1)
                    elif slot == STATE + q // 2:
                        xt_ready.wait(pe, n, QUADS * (NL_ - 1) + q + 1)
                        for part in range(2):
                            for h in range(4):
                                mm = pe.matmul(lv[q][:, P * part + VD * h:P * part + VD * h + VD], kq[:, i, 4 * hq + h, part, :], S[:, q, VD * h:VD * h + VD], start=True, stop=True)
                        mm.then_inc(s_full.sem, 1)
                    elif slot == STATE + 2 + q // 2:
                        r_ready.wait(pe, n, q + 1)
                        for h in range(4):
                            mm = pe.matmul(lv[q][:, VD * h:VD * h + VD], XT[q][:, h, :], r[q][:, h, :], start=True, stop=True)
                        mm.then_inc(z_full.sem, 1)
                    elif slot == STATE + 4 + q // 2:
                        wd_ready.wait(pe, n, q + 1)
                        pt_masked.wait(pe, n, q + 1)
                        for h in range(4):
                            pe.matmul(lv[q][:, P + VD * h:P + VD * h + VD], PT[q][:, h, :], z[q][:, h, :], start=True, stop=True)
                            mm = pe.matmul(lv[q][:, 2 * P + VD * h:2 * P + VD * h + VD], kt[q][:, h, :], wd[q][:, h, :], start=True, stop=True)
                        mm.then_inc(pw_full.sem, 1)
            run(pe, front, back)


def delta_output(nc, k, x_sb, w, xT, o_dram):
    with ExitStack() as ctx:
        def sb(n, *shape, dt=F32):
            return ctx.enter_context(nc.sbuf_tensor("b2_" + n, list(shape), dt))

        def psum(n, width):
            return ctx.enter_context(nc.psum_tensor("b2_" + n, [P, width], F32))

        def signal(n, per=1):
            return Signal(nc.alloc_semaphore("b2_" + n), per)

        G, V = 4, HEADS * VD
        PASSES = TILES // G
        wg, wo, nw = sb("wg", P, V), sb("wo", P, 2, C), sb("nw", P, 1)
        o, sq_ = sb("o", P, TILES * V), [sb(f"sq{e}", P, G * V) for e in range(2)]
        xs, gate, gated_o = ([sb(f"{n}{e}", P, width) for e in range(2)] for n, width in (("xs", G * P), ("gate", G * V), ("gated_o", G * V)))
        ms = sb("ms", P, TILES * HEADS)
        oT = [sb(f"oT{e}", P, G, 2, P) for e in range(2)]
        gp, tp, xp = [psum(f"gp{e}", 1024) for e in range(2)], psum("tp", 1024), [psum(f"xp{e}", 512) for e in range(2)]
        loaded, o_in = signal("loaded"), [signal(f"o_in{n}") for n in range(PASSES)]
        wo_ready, squared, summed, ms_step, rooted = (signal(n) for n in ("wo_ready", "squared", "summed", "ms_step", "rooted"))
        xs_ready, g_full, gated, scaled, o_ready, oT_full, oT_read, p_full, x_done = (
            signal(n) for n in ("xs_ready", "g_full", "gated", "scaled", "o_ready", "oT_full", "oT_read", "p_full", "x_done"))
        alone = signal("alone")
        o_rows = o_dram.rearrange("(g t p) v -> g p t v", p=P, t=G)
        block = ctx.enter_context(nc.Block())

        def loop(eng, step):
            step(-1, 1, back=False)
            step(0, 0)
            with eng.Fori(0, (PASSES - 2) // 2) as two:
                step(two * 2 + 1, 1)
                step(two * 2 + 2, 0)
            step(PASSES - 1, 1, front=False)

        @block.sync
        def _(sp):
            sp.dma_start(wg[:, :], w["Wg"]).then_inc(loaded.sem, 16)
            sp.dma_start(wo[:, :, :], w["Wo"].rearrange("(h v) c -> v h c", v=P)).then_inc(loaded.sem, 16)
            for h in range(P // VD):
                sp.dma_start(nw[VD * h:VD * h + VD, :], w["o_norm_w"].unsqueeze(1)).then_inc(loaded.sem, 16)
            for n in range(PASSES):
                sp.dma_start(o[:, n * G * V:(n + 1) * G * V].rearrange("p (t v) -> p t v", v=V), o_rows[n]).then_inc(o_in[n].sem, 16)

        @block.scalar
        def _(act):
            for n in range(PASSES):
                o_in[n].wait(act, 0, 16)
                summed.wait(act, 0, n - 1)
                act.activation(sq_[n % 2][:, :], o[:, n * G * V:(n + 1) * G * V], ACT.Square).then_inc(squared.sem, 1)
            ms_step.wait(act, 0, 1)
            act.activation(ms[:, :], ms[:, :], ACT.Sqrt).then_inc(rooted.sem, 1)

            def step(n, e, back=True, front=True):
                f = 1 - e
                if front:
                    g_full.wait(act, n - 1, 1)
                    tokens = xT[:, :, TAPS - 1:].rearrange("p b (s t) -> p b s t", t=G * P)
                    m = n + 1
                    act.activation(xs[f][:, :], tokens[:, bass.ds(m // 2, 1), bass.ds(m % 2, 1), :].rearrange("p b s t -> p (b s t)"), ACT.Copy).then_inc(xs_ready.sem, 1)
                if back:
                    oT_full.wait(act, n, 1)
                    p_full.wait(act, n - 2, 1)
                    act.activation(oT[e][:, :, :, :].rearrange("p a b c -> p (a b c)"), tp[:, :], ACT.Copy).then_inc(oT_read.sem, 1)
                if front:
                    g_full.wait(act, n + 1, 1)
                    o_ready.wait(act, n - 1, 1)
                    act.activation(gate[f][:, :], gp[f][:, :], ACT.Silu).then_inc(gated.sem, 1)
            loop(act, step)

        @block.vector
        def _(dve):
            loaded.wait(dve, 0, 16 * (2 + P // VD))
            dve.tensor_scalar(wo[:, :, :], wo[:, :, :], nw[:, 0:1], None, ALU.mult).then_inc(wo_ready.sem, 1)
            for n in range(PASSES):
                squared.wait(dve, 0, n + 1)
                dve.tensor_reduce(ms[:, n * G * HEADS:(n + 1) * G * HEADS], sq_[n % 2][:, :].rearrange("p (h d) -> p h d", d=VD), AX.X, ALU.add).then_inc(summed.sem, 1)
            summed.wait(dve, 0, PASSES)
            dve.tensor_scalar(ms[:, :], ms[:, :], 1.0 / VD, EPS_RMS, ALU.mult, ALU.add).then_inc(ms_step.sem, 1)
            rooted.wait(dve, 0, 1)
            dve.reciprocal(ms[:, :], ms[:, :]).then_inc(ms_step.sem, 1)
            ms_step.wait(dve, 0, 2)

            def step(n, e, back=True, front=True):
                f = 1 - e
                if front:
                    m = n + 1
                    oT_full.wait(dve, n - 1, 1)
                    dve.sem_inc(alone.sem, 1)
                    dve.tensor_tensor(gated_o[f][:, :].rearrange("p (h d) -> p h d", d=VD), o[:, bass.ds(m * (G * V), G * V)].rearrange("p (h d) -> p h d", d=VD),
                                      wide(ms[:, bass.ds(m * (G * HEADS), G * HEADS)], 2, [P, G * HEADS, VD]), ALU.mult).then_inc(scaled.sem, 1)
                if back:
                    p_full.wait(dve, n, 1)
                    dve.sem_inc(alone.sem, 1)
                    x = x_sb[:, bass.ds(n * (G * C), G * C)]
                    dve.tensor_tensor(x, x, xp[e][:, :], ALU.add).then_inc(x_done.sem, 1)
                if front:
                    gated.wait(dve, n + 1, 1)
                    scaled.wait(dve, n + 1, 1)
                    dve.tensor_tensor(gated_o[f][:, :], gated_o[f][:, :], gate[f][:, :], ALU.mult).then_inc(o_ready.sem, 1)
            loop(dve, step)
            x_done.wait(dve, PASSES, 0)

        @block.tensor
        def _(pe):
            loaded.wait(pe, 0, 16 * (2 + P // VD))
            wo_ready.wait(pe, 0, 1)

            def step(n, e, back=True, front=True):
                f = 1 - e
                if back:
                    o_ready.wait(pe, n, 1)
                    oT_read.wait(pe, n - 1, 1)
                    for j in range(G):
                        for hq in range(2):
                            mm = pe.transpose(tp[:, P * (2 * j + hq):P * (2 * j + hq) + P], gated_o[e][:, V * j + P * hq:V * j + P * hq + P], k["ident"][:, :])
                    mm.then_inc(oT_full.sem, 1)
                if front:
                    xs_ready.wait(pe, n + 1, 1)
                    gated.wait(pe, n - 1, 1)
                    for j in range(G):
                        mm = pe.matmul(gp[f][:, V * j:V * j + V], xs[f][:, P * j:P * j + P], wg[:, :], start=True, stop=True)
                    mm.then_inc(g_full.sem, 1)
                if back:
                    oT_read.wait(pe, n, 1)
                    x_done.wait(pe, n - 2, 1)
                    for j in range(G):
                        for hq in range(2):
                            mm = pe.matmul(xp[e][:, C * j:C * j + C], oT[e][:, j, hq, :], wo[:, hq, :], start=(hq == 0), stop=(hq == 1))
                    mm.then_inc(p_full.sem, 1)
            loop(pe, step)


B_WEIGHTS = ["Wq", "Wk", "Wv", "Wa", "Wb", "Wg", "Wo", "A_log", "dt_bias", "conv_q", "conv_k", "conv_v", "o_norm_w"]
INPUTS = ["L0_attn_a_x", "L0_attn_a_W_attn", "L0_attn_a_W_proj", *("L0_attn_b_" + n for n in B_WEIGHTS),
          "L0_ffn_Wr", "L0_ffn_Wg", "L0_ffn_Wu", "L0_ffn_Wd"]


def hybrid_layer(nc, dram, out):
    with ExitStack() as ctx:
        k = make_constants(nc, ctx)
        x_sb = ctx.enter_context(nc.sbuf_tensor("x_sb", [P, TILES * C], F32))
        x_in, x_out = ctx.enter_context(nc.semaphore("x_in")), ctx.enter_context(nc.semaphore("x_out"))
        xn_dram = nc.dram_tensor("xn_rows", (TOKENS, C), F32).ap()
        y_dram = nc.dram_tensor("y_rows", (TOP_K * TOKENS + SLOT_TILES * P, C), F32).ap()
        o_dram = nc.dram_tensor("o_rows", (TOKENS, HEADS * VD), F32).ap()
        tiles = x_sb[:, :].rearrange("p (n c) -> p n c", c=C)
        with nc.Block() as block:
            @block.sync
            def _(sp):
                sp.dma_start(tiles, dram["L0_attn_a_x"].rearrange("b (n p) c -> p (b n) c", p=P)).then_inc(x_in, 16)
                sp.wait_ge(x_in, 16)
        ffn = [dram["L0_ffn_" + n] for n in ("Wr", "Wg", "Wu", "Wd")]
        with nc.cleanup_on_exit():
            nystrom_attention(nc, k, x_sb, dram["L0_attn_a_W_attn"], dram["L0_attn_a_W_proj"])
        with nc.cleanup_on_exit():
            mixture_of_experts(nc, k, x_sb, *ffn, xn_dram, y_dram, "m1_")
        with nc.cleanup_on_exit():
            delta_attention(nc, k, x_sb, {n: dram["L0_attn_b_" + n] for n in B_WEIGHTS}, o_dram)
        with nc.cleanup_on_exit():
            mixture_of_experts(nc, k, x_sb, *ffn, xn_dram, y_dram, "m2_")
        with nc.Block() as block:
            @block.sync
            def _(sp):
                sp.dma_start(out.rearrange("b (n p) c -> p (b n) c", p=P), tiles).then_inc(x_out, 16)
                sp.wait_ge(x_out, 16)


def kernel(**inputs):
    import numpy as np
    import concourse.bacc as bacc
    from concourse.bass_utils import run_bass_kernel_spmd

    nc = bacc.Bacc("TRN2", target_bir_lowering=False, num_devices=1)
    arrays, dram = {}, {}
    for name in INPUTS:
        arrays[name] = np.ascontiguousarray(inputs[name])
        dram[name] = nc.dram_tensor(name, arrays[name].shape, mybir.dt.from_np(arrays[name].dtype), kind="ExternalInput").ap()
    out = nc.dram_tensor("out", (BATCHES, T, C), F32, kind="ExternalOutput").ap()
    hybrid_layer(nc, dram, out)
    return run_bass_kernel_spmd(nc, [arrays], core_ids=[0]).results[0]["out"]
```

```python
import concourse.bass as bass
from concourse import mybir
from contextlib import ExitStack

F32 = mybir.dt.float32
U32 = mybir.dt.uint32
I32 = mybir.dt.int32
ALU = mybir.AluOpType
ACT = mybir.ActivationFunctionType
AX = mybir.AxisListType

P = 128
C = 128
TILES = 32
BATCHES = 4
TPB = TILES // BATCHES
T = TPB * P
EPS_LN = 1e-5


class Signal:

    def __init__(self, sem, per=1):
        self.sem, self.per = sem, per

    def at(self, passes, k):
        return passes * self.per + k

    def due(self, passes, k):
        value = self.at(passes, k)
        return not isinstance(value, int) or value > 0


def wide(ap, axis, shape):
    return ap.unsqueeze(axis).to_broadcast(shape)


def make_constants(nc, ctx, x_sb=None, x_dram=None):
    def sb(name, shape):
        return ctx.enter_context(nc.sbuf_tensor(name, shape, F32))

    k = {
        "ident": sb("ident", [P, P]),
        "ones": sb("ones", [P, P]),
        "half_ones": sb("half_ones", [P, P]),
        "head_rows": sb("head_rows", [P, 16]),
        "upto": sb("upto", [P, P]),
        "after": sb("after", [P, P]),
        "before": sb("before", [P, P]),
    }
    filled = ctx.enter_context(nc.semaphore("const_filled"))
    shaped = ctx.enter_context(nc.semaphore("const_shaped"))
    x_in = ctx.enter_context(nc.semaphore("x_in"))
    with nc.Block() as block:
        @block.sync
        def _(sp):
            if x_sb is not None:
                sp.dma_start(x_sb, x_dram).then_inc(x_in, 16)
                sp.wait_ge(x_in, 16)

        @block.gpsimd
        def _(pool):
            for name in ("ones", "half_ones", "head_rows", "upto", "after", "before"):
                pool.memset(k[name][:, :], 1.0).then_inc(filled, 1)
            pool.memset(k["ident"][:, :], 0.0).then_inc(filled, 1)
            pool.wait_ge(filled, 7)

            def select(name, ap, op, fill, base, pattern, step):
                pool.affine_select(out=ap, in_=ap, compare_op=op, fill=fill, base=base,
                                   pattern=pattern, channel_multiplier=step).then_inc(shaped, 1)
            select("ident", k["ident"][:, :], ALU.not_equal, 1.0, 0, [[-1, P]], 1)
            select("upto", k["upto"][:, :], ALU.is_ge, 0.0, 0, [[1, P]], -1)
            select("after", k["after"][:, :], ALU.is_gt, 0.0, 0, [[-1, P]], 1)
            select("before", k["before"][:, :], ALU.is_gt, 0.0, 0, [[1, P]], -1)
            select("half", k["half_ones"][:, 0:64], ALU.is_gt, 0.0, 64, [[0, 64]], -1)
            select("half", k["half_ones"][:, 64:128], ALU.is_ge, 0.0, -64, [[0, 64]], 1)
            select("head", k["head_rows"][:, :], ALU.is_ge, 0.0, 0, [[-8, 16]], 1)
            pool.wait_ge(shaped, 7)
            select("head", k["head_rows"][:, :], ALU.is_ge, 0.0, 7, [[8, 16]], -1)
            pool.wait_ge(shaped, 8)
    return k


def nystrom_attention(nc, k, x_sb, w_attn, w_proj):
    PAIRS, NL, HS, ITERS = 8, 64, 8, 6
    with ExitStack() as ctx:
        def sb(name, *shape):
            return ctx.enter_context(nc.sbuf_tensor("a_" + name, list(shape), F32))

        def psum(name, *shape):
            return ctx.enter_context(nc.psum_tensor("a_" + name, list(shape), F32))

        def signal(name, per=1):
            return Signal(nc.alloc_semaphore("a_" + name), per)

        wa, wp = sb("wa", P, 3 * C), sb("wp", P, C)
        stats, moments, rstd = sb("stats", P, TPB, 6), sb("moments", P, TPB, 2), sb("rstd", P, TPB)
        xn, xT = sb("xn", P, TPB, C), sb("xT", P, T)
        qT, kT, v = sb("qT", P, T), sb("kT", P, T), sb("v", P, TPB, C)
        q_land, k_land = sb("q_land", P, NL), sb("k_land", P, NL)
        q_diag, k_diag = sb("q_diag", P, 16, NL), sb("k_diag", P, 16, NL)
        mid_max, mid_sum, denom = sb("mid_max", P, PAIRS), sb("mid_sum", P, PAIRS), sb("denom", P, PAIRS)
        mid_x, K = sb("mid_x", P, PAIRS, NL), sb("K", P, PAIRS, NL)
        K_diag, KT_diag = sb("K_diag", P, PAIRS, P), sb("KT_diag", P, PAIRS, P)
        Y = [sb(f"Y{n}", P, PAIRS, 2, NL) for n in range(2)]
        M_diag, M2_diag = sb("M_diag", P, PAIRS, P), sb("M2_diag", P, PAIRS, P)
        MY, R, S, S1 = (sb(n, P, PAIRS, 2, NL) for n in ("MY", "R", "S", "S1"))
        far_max, far_sum = sb("far_max", P, PAIRS), sb("far_sum", P, PAIRS)
        far, farT = [sb(f"far{n}", P, T) for n in range(2)], [sb(f"farT{n}", P, TPB, P) for n in range(2)]
        W, ZW = sb("W", P, PAIRS, HS), sb("ZW", P, PAIRS, HS)
        near_max = sb("near_max", P, 16)
        near, nearT = [sb(f"near{n}", P, 16, NL) for n in range(2)], [sb(f"nearT{n}", P, PAIRS, P) for n in range(2)]
        U_diag = sb("U_diag", P, PAIRS, 18)
        y_rs, y, yT = sb("y_rs", P, PAIRS, 2), sb("y", P, PAIRS, 2, HS), sb("yT", P, C)

        sc = [psum(f"sc{n}", P, 1024) for n in range(2)]
        tp, nw, sm = psum("tp", P, 512), psum("nw", P, 1024), psum("sm", P, 512)

        alone, pool_alone = signal("alone"), signal("pool_alone")
        loaded, zeroed = signal("loaded"), signal("zeroed")
        bn_done, aggr_done, rstd_ready, xn_ready = signal("bn_done", 8), signal("aggr_done", 8), signal("rstd_ready"), signal("xn_ready", 8)
        land_sum, land_ready, diag_ready = signal("land_sum", 2), signal("land_ready", 2), signal("diag_ready", 2)
        var_ready, root_ready = signal("var_ready"), signal("root_ready")
        mid_max_ready, mid_sub, mid_exp, mid_sum_ready = (signal(n) for n in ("mid_max_ready", "mid_sub", "mid_exp", "mid_sum_ready"))
        mid_recip, K_ready, K_diag_ready = signal("mid_recip"), signal("K_ready"), signal("K_diag_ready")
        denom_ready, M0_ready, Z0_ready = signal("denom_ready", 2), signal("M0_ready"), signal("Z0_ready")
        Y_ready, M_diag_ready, my_ready, M2_diag_ready = signal("Y_ready", 2 + ITERS), signal("M_diag_ready", 2 * ITERS), signal("my_ready", ITERS), signal("M2_diag_ready", 2 * ITERS)
        R_ready, S1_ready, S_ready = signal("R_ready", ITERS), signal("S1_ready", ITERS), signal("S_ready", ITERS)
        far_bias, far_exp, far_recip, W0_ready = signal("far_bias", 8), signal("far_exp", 8), signal("far_recip"), signal("W0_ready", 2)
        ZW_ready = signal("ZW_ready")
        U_ready = signal("U_ready", 2)
        near_max_ready, near_sub, near_exp = signal("near_max_ready", 8), signal("near_sub", 8), signal("near_exp", 8)
        y_recip, y_ready, yT_ready, x_done = signal("y_recip", 8), signal("y_ready", 8), signal("yT_ready", 8), signal("x_done", 8)
        tp_read, qkv_read = signal("tp_read", 36), signal("qkv_read", 3)
        tp_full, sc_full = signal("tp_full", 36), signal("sc_full", 20)
        mid_full, colsum_full, my_full, m2r_full = signal("mid_full"), signal("colsum_full"), signal("my_full", ITERS), signal("m2r_full", ITERS)
        nv_full, zw_full, u_full = signal("nv_full", 8), signal("zw_full"), signal("u_full")
        y_full, yT_full, o_full = signal("y_full", 8), signal("yT_full", 8), signal("o_full", 8)
        TP_KT, TP_FAR, TP_NEAR = 2, 4, 20
        SC_M0, SC_NEAR = 4, 12
        HALVES = (slice(0, 64), slice(64, 128))

        def sc_far(s):
            return 4 + s if s else 3

        def tile(b, j):
            return bass.ds(b * (TPB * C) + j * C, C)

        def flat(ap):
            return ap.rearrange("p a b -> p (a b)")

        def flat4(ap):
            return ap.rearrange("p a m b -> p (a m b)")

        def live(s):
            return slice(1 if s == ITERS - 1 else 0, 2)

        def loop(eng, batch):
            with eng.Fori(0, BATCHES - 1) as b:
                batch(b, True)
            batch(BATCHES - 1, False)

        block = ctx.enter_context(nc.Block())

        @block.sync
        def _(sp):
            sp.dma_start(wa[:, :], w_attn).then_inc(loaded.sem, 16)
            sp.dma_start(wp[:, :], w_proj).then_inc(loaded.sem, 16)

        @block.gpsimd
        def _(pool):
            for t in (M2_diag, U_diag):
                pool.memset(t[:, :, :], 0.0).then_inc(zeroed.sem, 1)
            pool.wait_ge(zeroed.sem, 2)
            pool.memset(U_diag[0:64, :, 16:17], 1.0).then_inc(zeroed.sem, 1)
            pool.memset(U_diag[64:128, :, 17:18], 1.0).then_inc(zeroed.sem, 1)
            pool.wait_ge(zeroed.sem, 4)
            halves = wide(wide(k["half_ones"][:, ::NL], 1, [P, PAIRS, 2]), 3, [P, PAIRS, 2, NL])

            def by_half(t):
                return t[:, :, :].rearrange("p a (h l) -> p a h l", h=2)

            with pool.Fori(0, BATCHES) as b:
                pool.wait_ge(K_ready.sem, K_ready.at(b, 1))
                pool.sem_inc(pool_alone.sem, 1)
                pool.tensor_tensor(by_half(K_diag), wide(K[:, :, :], 2, [P, PAIRS, 2, NL]), halves, ALU.mult).then_inc(K_diag_ready.sem, 1)
                pool.tensor_tensor(Y[0][:, :, 1, :], wide(k["ident"][:, 0:NL], 1, [P, PAIRS, NL]), wide(k["ident"][:, NL:], 1, [P, PAIRS, NL]),
                                   ALU.add).then_inc(Z0_ready.sem, 1)
                pool.wait_ge(Z0_ready.sem, Z0_ready.at(b, 1))
                for s in range(ITERS):
                    pool.wait_ge(Y_ready.sem, Y_ready.at(b, 2 + s))
                    pool.sem_inc(pool_alone.sem, 1)
                    if s:
                        pool.wait_ge(S_ready.sem, S_ready.at(b, s))
                        pool.sem_inc(pool_alone.sem, 1)
                    pool.tensor_scalar(S1[:, :, :, :], Y[s % 2][:, :, :, :], 3.25, None, ALU.mult).then_inc(S1_ready.sem, 1)

        @block.scalar
        def _(act):
            act.wait_ge(zeroed.sem, 4)

            def from_tp(b, n, out):
                act.wait_ge(tp_full.sem, tp_full.at(b, n + 1))
                act.activation(out, tp[:, :], ACT.Copy).then_inc(tp_read.sem, 1)

            def root(b):
                act.wait_ge(var_ready.sem, var_ready.at(b, 1))
                act.activation(rstd[:, :], rstd[:, :], ACT.Sqrt).then_inc(root_ready.sem, 1)

            def tokens_out(b, g):
                from_tp(b, g, xT[:, 512 * g:512 * g + 512])

            def qkv_out(b, n):
                act.wait_ge(sc_full.sem, sc_full.at(b, n + 1))
                act.activation((qT[:, :], kT[:, :], flat(v[:, :, :]))[n], sc[n % 2][:, :], ACT.Copy).then_inc(qkv_read.sem, 1)

            def batch(b, more):
                act.wait_ge(mid_sub.sem, mid_sub.at(b, 1))
                act.activation(mid_x[:, :, :], mid_x[:, :, :], ACT.Exp).then_inc(mid_exp.sem, 1)

                def far_exponential(s):
                    act.wait_ge(far_bias.sem, far_bias.at(b, s + 1))
                    if s >= 2:
                        if tp_full.due(b, TP_FAR + 2 * (s - 1)):
                            act.wait_ge(tp_full.sem, tp_full.at(b, TP_FAR + 2 * (s - 1)))
                    act.activation(far[s % 2][:, :], sc[s % 2][:, :], ACT.Exp, bias=far_max[:, s:s + 1],
                                   accum_out=far_sum[:, s:s + 1]).then_inc(far_exp.sem, 1)

                far_exponential(0)
                for g in range(2):
                    from_tp(b, TP_KT + g, flat(KT_diag[:, 4 * g:4 * g + 4, :]))

                def far_out(s, g):
                    if s >= 2:
                        if nv_full.due(b, s - 1):
                            act.wait_ge(nv_full.sem, nv_full.at(b, s - 1))
                    from_tp(b, TP_FAR + 2 * s + g, flat(farT[s % 2][:, 4 * g:4 * g + 4, :]))

                for s in range(PAIRS):
                    far_out(s, 0)
                    if s < ITERS:
                        act.wait_ge(my_full.sem, my_full.at(b, s + 1))
                        if s:
                            act.wait_ge(S_ready.sem, S_ready.at(b, s))
                        act.activation(flat4(MY[:, :, :, :]), nw[:, :], ACT.Copy).then_inc(my_ready.sem, 1)
                        act.wait_ge(my_ready.sem, my_ready.at(b, s + 1))
                        for r in HALVES:
                            act.activation(M2_diag[r, :, r], MY[r, :, 0, :], ACT.Copy).then_inc(M2_diag_ready.sem, 1)
                    far_out(s, 1)
                    if s + 1 < PAIRS:
                        far_exponential(s + 1)
                    if s < ITERS:
                        act.wait_ge(Y_ready.sem, Y_ready.at(b, 3 + s))
                        for r in HALVES:
                            act.activation(M_diag[r, :, r], Y[(s + 1) % 2][r, :, 1 if s == ITERS - 1 else 0, :], ACT.Copy).then_inc(M_diag_ready.sem, 1)

                def near_exponential(s):
                    act.wait_ge(near_sub.sem, near_sub.at(b, s + 1))
                    act.activation(near[s % 2][:, :, :], near[s % 2][:, :, :], ACT.Exp).then_inc(near_exp.sem, 1)

                def near_out(s, g):
                    if s >= 2:
                        if y_full.due(b, s - 1):
                            act.wait_ge(y_full.sem, y_full.at(b, s - 1))
                    from_tp(b, TP_NEAR + 2 * s + g, flat(nearT[s % 2][:, 4 * g:4 * g + 4, :]))

                if more:
                    root(b + 1)
                near_exponential(0)
                for s in range(TPB + 2):
                    if more and s == TPB:
                        for g in range(2):
                            tokens_out(b + 1, g)
                    if s < TPB:
                        near_out(s, 0)
                        if s + 1 < TPB:
                            near_exponential(s + 1)
                        near_out(s, 1)
                    if s >= 2:
                        t = s - 2
                        act.wait_ge(yT_full.sem, yT_full.at(b, t + 1))
                        if t:
                            act.wait_ge(o_full.sem, o_full.at(b, t))
                        act.activation(yT[:, :], sm[:, 0:C], ACT.Copy).then_inc(yT_ready.sem, 1)
                if more:
                    for n in range(3):
                        qkv_out(b + 1, n)

            root(0)
            for g in range(2):
                tokens_out(0, g)
            for n in range(3):
                qkv_out(0, n)
            loop(act, batch)

        @block.vector
        def _(dve):
            dve.wait_ge(zeroed.sem, 4)

            def norm_start(b):
                if xn_ready.due(b - 1, TPB):
                    dve.wait_ge(xn_ready.sem, xn_ready.at(b - 1, TPB))
                dve.sem_inc(alone.sem, 1)
                for j in range(TPB):
                    dve.bn_stats(stats[:, j, :], x_sb[:, tile(b, j)]).then_inc(bn_done.sem, 1)
                dve.wait_ge(bn_done.sem, bn_done.at(b, 8))
                dve.sem_inc(alone.sem, 1)
                for j in range(TPB):
                    dve.bn_aggr(moments[:, j, :], stats[:, j, :]).then_inc(aggr_done.sem, 1)
                dve.wait_ge(aggr_done.sem, aggr_done.at(b, 8))
                dve.tensor_scalar(rstd[:, :], moments[:, :, 1], EPS_LN, None, ALU.add).then_inc(var_ready.sem, 1)

            def norm_end(b):
                dve.wait_ge(root_ready.sem, root_ready.at(b, 1))
                dve.reciprocal(rstd[:, :], rstd[:, :]).then_inc(rstd_ready.sem, 1)
                dve.wait_ge(rstd_ready.sem, rstd_ready.at(b, 1))
                if tp_full.due(b - 1, 2):
                    dve.wait_ge(tp_full.sem, tp_full.at(b - 1, 2))
                dve.sem_inc(alone.sem, 1)
                for j in range(TPB):
                    dve.tensor_scalar(xn[:, j, :], x_sb[:, tile(b, j)], moments[:, j, 0:1], rstd[:, j:j + 1],
                                      ALU.subtract, ALU.mult).then_inc(xn_ready.sem, 1)

            def landmarks(b):
                for n, (src, land) in enumerate(((qT, q_land), (kT, k_land))):
                    dve.wait_ge(qkv_read.sem, qkv_read.at(b, n + 1))
                    dve.tensor_reduce(land[:, :], src[:, :].rearrange("p (l t) -> p l t", l=NL), AX.X, ALU.add).then_inc(land_sum.sem, 1)
                dve.wait_ge(land_sum.sem, land_sum.at(b, 2))
                for land in (q_land, k_land):
                    dve.tensor_scalar(land[:, :], land[:, :], NL / T, None, ALU.mult).then_inc(land_ready.sem, 1)
                dve.wait_ge(land_ready.sem, land_ready.at(b, 2))
                for land, diag in ((q_land, q_diag), (k_land, k_diag)):
                    dve.tensor_tensor(diag[:, :, :], wide(land[:, :], 1, [P, 16, NL]), wide(k["head_rows"][:, :], 2, [P, 16, NL]),
                                      ALU.mult).then_inc(diag_ready.sem, 1)

            def batch(b, more):
                mid = nw[:, 0:512].rearrange("p (a b) -> p a b", b=NL)
                dve.wait_ge(mid_full.sem, mid_full.at(b, 1))
                dve.tensor_reduce(mid_max[:, :], mid, AX.X, ALU.max).then_inc(mid_max_ready.sem, 1)
                dve.wait_ge(mid_max_ready.sem, mid_max_ready.at(b, 1))
                dve.tensor_tensor(mid_x[:, :, :], mid, wide(mid_max[:, :], 2, [P, PAIRS, NL]), ALU.subtract).then_inc(mid_sub.sem, 1)
                dve.wait_ge(mid_exp.sem, mid_exp.at(b, 1))
                dve.tensor_reduce(mid_sum[:, :], mid_x[:, :, :], AX.X, ALU.add).then_inc(mid_sum_ready.sem, 1)
                dve.wait_ge(mid_sum_ready.sem, mid_sum_ready.at(b, 1))
                dve.reciprocal(mid_sum[:, :], mid_sum[:, :]).then_inc(mid_recip.sem, 1)
                dve.wait_ge(mid_recip.sem, mid_recip.at(b, 1))
                dve.tensor_tensor(K[:, :, :], mid_x[:, :, :], wide(mid_sum[:, :], 2, [P, PAIRS, NL]), ALU.mult).then_inc(K_ready.sem, 1)
                def far_maximum(s):
                    dve.wait_ge(sc_full.sem, sc_full.at(b, sc_far(s) + 1))
                    dve.tensor_reduce(far_max[:, s:s + 1], sc[s % 2][:, :], AX.X, ALU.max, negate=True).then_inc(far_bias.sem, 1)

                far_maximum(0)
                dve.wait_ge(colsum_full.sem, colsum_full.at(b, 1))
                dve.tensor_reduce(denom[:, :], sm[:, :].rearrange("p (a b) -> p a b", b=NL), AX.X, ALU.max).then_inc(denom_ready.sem, 1)
                dve.wait_ge(denom_ready.sem, denom_ready.at(b, 1))
                dve.reciprocal(denom[:, :], denom[:, :]).then_inc(denom_ready.sem, 1)
                dve.wait_ge(denom_ready.sem, denom_ready.at(b, 2))
                dve.wait_ge(sc_full.sem, sc_full.at(b, SC_M0 + 1))
                dve.tensor_tensor(M_diag[:, :, :], sc[1][:, :].rearrange("p (a b) -> p a b", b=P),
                                  wide(denom[:, :], 2, [P, PAIRS, P]), ALU.mult).then_inc(M0_ready.sem, 1)
                dve.wait_ge(M0_ready.sem, M0_ready.at(b, 1))
                for r in HALVES:
                    dve.tensor_copy(Y[0][r, :, 0, :], M_diag[r, :, r]).then_inc(Y_ready.sem, 1)

                for s in range(PAIRS):
                    if s + 1 < PAIRS:
                        far_maximum(s + 1)
                    if more and s == ITERS:
                        norm_start(b + 1)
                    if s < ITERS:
                        now, new, part = Y[s % 2], Y[(s + 1) % 2], live(s)
                        dve.wait_ge(my_ready.sem, my_ready.at(b, s + 1))
                        dve.wait_ge(Y_ready.sem, Y_ready.at(b, 2 + s))
                        if s == 0:
                            dve.wait_ge(Z0_ready.sem, Z0_ready.at(b, 1))
                        dve.scalar_tensor_tensor(R[:, :, part, :], now[:, :, part, :], 7.0, MY[:, :, part, :], ALU.mult, ALU.subtract).then_inc(R_ready.sem, 1)
                        dve.wait_ge(S1_ready.sem, S1_ready.at(b, s + 1))
                        dve.scalar_tensor_tensor(S[:, :, part, :], MY[:, :, part, :], -3.75, S1[:, :, part, :], ALU.mult, ALU.add).then_inc(S_ready.sem, 1)
                        dve.wait_ge(S_ready.sem, S_ready.at(b, s + 1))
                        dve.wait_ge(m2r_full.sem, m2r_full.at(b, s + 1))
                        got = nw[:, :].rearrange("p (a m b) -> p a m b", m=2, b=NL)
                        dve.scalar_tensor_tensor(new[:, :, part, :], got[:, :, part, :], 0.25, S[:, :, part, :], ALU.mult, ALU.add).then_inc(Y_ready.sem, 1)
                dve.wait_ge(far_exp.sem, far_exp.at(b, 8))
                dve.reciprocal(far_sum[:, :], far_sum[:, :]).then_inc(far_recip.sem, 1)
                dve.wait_ge(far_recip.sem, far_recip.at(b, 1))
                dve.wait_ge(nv_full.sem, nv_full.at(b, 8))
                nv = sm[:, 0:128].rearrange("p (a b) -> p a b", b=2 * HS)
                for h, r in enumerate(HALVES):
                    dve.tensor_tensor(W[r, :, :], nv[r, :, HS * h:HS * h + HS], wide(far_sum[r, :], 2, [64, PAIRS, HS]),
                                      ALU.mult).then_inc(W0_ready.sem, 1)
                dve.wait_ge(W0_ready.sem, W0_ready.at(b, 2))

                def near_softmax(s):
                    scores = sc[(SC_NEAR + s) % 2][:, :].rearrange("p (a b) -> p a b", b=NL)
                    dve.wait_ge(sc_full.sem, sc_full.at(b, SC_NEAR + s + 1))
                    if s:
                        dve.wait_ge(near_sub.sem, near_sub.at(b, s))
                    dve.tensor_reduce(near_max[:, :], scores, AX.X, ALU.max).then_inc(near_max_ready.sem, 1)
                    dve.wait_ge(near_max_ready.sem, near_max_ready.at(b, s + 1))
                    if s >= 2:
                        if tp_full.due(b, TP_NEAR + 2 * (s - 1)):
                            dve.wait_ge(tp_full.sem, tp_full.at(b, TP_NEAR + 2 * (s - 1)))
                    dve.tensor_tensor(near[s % 2][:, :, :], scores, wide(near_max[:, :], 2, [P, 16, NL]), ALU.subtract).then_inc(near_sub.sem, 1)

                near_softmax(0)
                dve.wait_ge(zw_full.sem, zw_full.at(b, 1))
                dve.tensor_copy(flat(ZW[:, :, :]), sm[:, 128:192]).then_inc(ZW_ready.sem, 1)
                dve.wait_ge(u_full.sem, u_full.at(b, 1))
                for h, r in enumerate(HALVES):
                    dve.tensor_tensor(U_diag[r, :, HS * h:HS * h + HS], sm[r, 256:320].rearrange("p (a b) -> p a b", b=HS),
                                      wide(denom[r, :], 2, [64, PAIRS, HS]), ALU.mult).then_inc(U_ready.sem, 1)

                def output(s):
                    got = nw[:, 0:144].rearrange("p (a b) -> p a b", b=18)
                    dve.wait_ge(y_full.sem, y_full.at(b, s + 1))
                    if s:
                        dve.wait_ge(y_ready.sem, y_ready.at(b, s))
                    dve.reciprocal(y_rs[:, :, :], got[:, :, 16:18]).then_inc(y_recip.sem, 1)
                    dve.wait_ge(y_recip.sem, y_recip.at(b, s + 1))
                    if s:
                        dve.wait_ge(yT_full.sem, yT_full.at(b, s))
                    dve.tensor_tensor(y[:, :, :, :], got[:, :, 0:16].rearrange("p a (h d) -> p a h d", h=2),
                                      wide(y_rs[:, :, :], 3, [P, PAIRS, 2, HS]), ALU.mult).then_inc(y_ready.sem, 1)

                def residual(s):
                    dve.wait_ge(o_full.sem, o_full.at(b, s + 1))
                    dve.tensor_tensor(x_sb[:, tile(b, s)], x_sb[:, tile(b, s)], nw[:, 512:512 + C],
                                      ALU.add).then_inc(x_done.sem, 1)

                for s in range(TPB + 3):
                    if s + 1 < TPB:
                        near_softmax(s + 1)
                    if 1 <= s <= TPB:
                        output(s - 1)
                    if s >= 3:
                        residual(s - 3)
                    if more and s == 3:
                        norm_end(b + 1)
                if more:
                    landmarks(b + 1)
                dve.wait_ge(x_done.sem, x_done.at(b, TPB))

            norm_start(0)
            norm_end(0)
            landmarks(0)
            loop(dve, batch)

        @block.tensor
        def _(pe):
            pe.wait_ge(loaded.sem, 32)

            def transpose4(b, n, ins):
                if n:
                    pe.wait_ge(tp_read.sem, tp_read.at(b, n))
                else:
                    if tp_read.due(b - 1, TP_NEAR + 2 * TPB):
                        pe.wait_ge(tp_read.sem, tp_read.at(b - 1, TP_NEAR + 2 * TPB))
                for g, ap in enumerate(ins):
                    mm = pe.transpose(tp[:, P * g:P * g + P], ap, k["ident"][:, :])
                mm.then_inc(tp_full.sem, 1)

            def tokens(b, g):
                pe.wait_ge(xn_ready.sem, xn_ready.at(b, 4 * g + 4))
                transpose4(b, g, [xn[:, j, :] for j in range(4 * g, 4 * g + 4)])

            def qkv(b, n):
                if n < 2:
                    if near_sub.due(b - 1, TPB - 1 + n):
                        pe.wait_ge(near_sub.sem, near_sub.at(b - 1, TPB - 1 + n))
                    if n == 0:
                        pe.wait_ge(tp_read.sem, tp_read.at(b, 2))
                    for g in range(2):
                        mm = pe.matmul(sc[n][:, 512 * g:512 * g + 512], wa[:, C * n:C * n + C], xT[:, 512 * g:512 * g + 512], start=True, stop=True)
                else:
                    pe.wait_ge(qkv_read.sem, qkv_read.at(b, 1))
                    for j in range(TPB):
                        mm = pe.matmul(sc[0][:, C * j:C * j + C], xT[:, P * j:P * j + P], wa[:, 2 * C:3 * C], start=True, stop=True)
                mm.then_inc(sc_full.sem, 1)

            def batch(b, more):
                pe.wait_ge(diag_ready.sem, diag_ready.at(b, 2))
                for s in range(PAIRS):
                    mm = pe.matmul(nw[:, NL * s:NL * s + NL], flat(q_diag[:, 2 * s:2 * s + 2, :]), k_land[:, :], start=True, stop=True)
                mm.then_inc(mid_full.sem, 1)
                def far_scores(s):
                    if s == 0:
                        pe.wait_ge(qkv_read.sem, qkv_read.at(b, 3))
                    elif s == 1:
                        pe.wait_ge(M0_ready.sem, M0_ready.at(b, 1))
                    else:
                        if far_exp.due(b, s - 1):
                            pe.wait_ge(far_exp.sem, far_exp.at(b, s - 1))
                    for g in range(2):
                        mm = pe.matmul(sc[s % 2][:, 512 * g:512 * g + 512], flat(q_diag[:, 2 * s:2 * s + 2, :]),
                                       kT[:, 512 * g:512 * g + 512], start=True, stop=True)
                    mm.then_inc(sc_full.sem, 1)

                far_scores(0)
                pe.wait_ge(K_ready.sem, K_ready.at(b, 1))
                pe.matmul(sm[:, :], k["half_ones"][:, :], flat(K[:, :, :]), start=True, stop=True).then_inc(colsum_full.sem, 1)
                pe.wait_ge(K_diag_ready.sem, K_diag_ready.at(b, 1))
                for g in range(2):
                    transpose4(b, TP_KT + g, [K_diag[:, s, :] for s in range(4 * g, 4 * g + 4)])
                pe.wait_ge(tp_read.sem, tp_read.at(b, TP_KT + 2))
                pe.wait_ge(qkv_read.sem, qkv_read.at(b, 2))
                for s in range(PAIRS):
                    mm = pe.matmul(sc[1][:, P * s:P * s + P], KT_diag[:, s, :], KT_diag[:, s, :], start=True, stop=True)
                mm.then_inc(sc_full.sem, 1)

                def far_times_v(s):
                    pe.wait_ge(tp_read.sem, tp_read.at(b, TP_FAR + 2 * s + 2))
                    if s == 0:
                        pe.wait_ge(denom_ready.sem, denom_ready.at(b, 1))
                    for j in range(TPB):
                        mm = pe.matmul(sm[:, 16 * s:16 * s + 16], farT[s % 2][:, j, :], v[:, j, 16 * s:16 * s + 16],
                                       start=(j == 0), stop=(j == TPB - 1))
                    mm.then_inc(nv_full.sem, 1)

                def far_transposes(s, g):
                    if g == 0:
                        pe.wait_ge(far_exp.sem, far_exp.at(b, s + 1))
                    transpose4(b, TP_FAR + 2 * s + g, [far[s % 2][:, P * j:P * j + P] for j in range(4 * g, 4 * g + 4)])

                for s in range(PAIRS):
                    if s + 1 < PAIRS:
                        far_scores(s + 1)
                    far_transposes(s, 0)
                    if s < ITERS:
                        pe.wait_ge(Y_ready.sem, Y_ready.at(b, 2 + s))
                        if s:
                            pe.wait_ge(M_diag_ready.sem, M_diag_ready.at(b, 2 * s))
                        else:
                            pe.wait_ge(Z0_ready.sem, Z0_ready.at(b, 1))
                        for a in range(PAIRS):
                            mm = pe.matmul(nw[:, P * a:P * a + P], M_diag[:, a, :], flat(Y[s % 2][:, a, :, :]), start=True, stop=True)
                        mm.then_inc(my_full.sem, 1)
                    far_transposes(s, 1)
                    if s:
                        far_times_v(s - 1)
                    if s < ITERS:
                        pe.wait_ge(R_ready.sem, R_ready.at(b, s + 1))
                        pe.wait_ge(M2_diag_ready.sem, M2_diag_ready.at(b, 2 * s + 2))
                        part = live(s)
                        for a in range(PAIRS):
                            mm = pe.matmul(nw[:, P * a + NL * part.start:P * a + P], M2_diag[:, a, :], flat(R[:, a, part, :]), start=True, stop=True)
                        mm.then_inc(m2r_full.sem, 1)
                far_times_v(PAIRS - 1)

                def near_scores(s):
                    n = SC_NEAR + s
                    if s < 2:
                        pe.wait_ge(far_exp.sem, far_exp.at(b, 7 + s))
                    else:
                        if near_sub.due(b, s - 1):
                            pe.wait_ge(near_sub.sem, near_sub.at(b, s - 1))
                    for g in range(2):
                        mm = pe.matmul(sc[n % 2][:, 512 * g:512 * g + 512], qT[:, P * s:P * s + P], flat(k_diag[:, 8 * g:8 * g + 8, :]),
                                       start=True, stop=True)
                    mm.then_inc(sc_full.sem, 1)

                near_scores(0)
                near_scores(1)
                pe.wait_ge(W0_ready.sem, W0_ready.at(b, 2))
                pe.wait_ge(M_diag_ready.sem, M_diag_ready.at(b, 2 * ITERS))
                for a in range(PAIRS):
                    mm = pe.matmul(sm[:, 128 + HS * a:128 + HS * a + HS], M_diag[:, a, :], W[:, a, :], start=True, stop=True)
                mm.then_inc(zw_full.sem, 1)
                pe.wait_ge(ZW_ready.sem, ZW_ready.at(b, 1))
                for a in range(PAIRS):
                    mm = pe.matmul(sm[:, 256 + HS * a:256 + HS * a + HS], K_diag[:, a, :], ZW[:, a, :], start=True, stop=True)
                mm.then_inc(u_full.sem, 1)

                def near_transposes(s, g):
                    if g == 0:
                        pe.wait_ge(near_exp.sem, near_exp.at(b, s + 1))
                    transpose4(b, TP_NEAR + 2 * s + g, [flat(near[s % 2][:, 2 * a:2 * a + 2, :]) for a in range(4 * g, 4 * g + 4)])

                for s in range(TPB + 3):
                    if more and s == TPB:
                        tokens(b + 1, 0)
                    if s < TPB:
                        near_transposes(s, 0)
                        if s + 2 < TPB:
                            near_scores(s + 2)
                        near_transposes(s, 1)
                    if 1 <= s <= TPB:
                        t = s - 1
                        pe.wait_ge(tp_read.sem, tp_read.at(b, TP_NEAR + 2 * t + 2))
                        if t:
                            pe.wait_ge(y_ready.sem, y_ready.at(b, t))
                        else:
                            pe.wait_ge(U_ready.sem, U_ready.at(b, 2))
                        for a in range(PAIRS):
                            mm = pe.matmul(nw[:, 18 * a:18 * a + 18], nearT[t % 2][:, a, :], U_diag[:, a, :], start=True, stop=True)
                        mm.then_inc(y_full.sem, 1)
                    if more and s >= TPB:
                        if s == TPB:
                            tokens(b + 1, 1)
                        else:
                            qkv(b + 1, s - TPB - 1)
                    if 2 <= s <= TPB + 1:
                        t = s - 2
                        pe.wait_ge(y_ready.sem, y_ready.at(b, t + 1))
                        if t:
                            pe.wait_ge(yT_ready.sem, yT_ready.at(b, t))
                        pe.transpose(sm[:, 0:C], y[:, :, :, :].rearrange("p a h d -> p (a h d)"), k["ident"][:, :]).then_inc(yT_full.sem, 1)
                    if s >= 3:
                        t = s - 3
                        pe.wait_ge(yT_ready.sem, yT_ready.at(b, t + 1))
                        if t:
                            pe.wait_ge(x_done.sem, x_done.at(b, t))
                        pe.matmul(nw[:, 512:512 + C], yT[:, :], wp[:, :], start=True, stop=True).then_inc(o_full.sem, 1)
                if more:
                    qkv(b + 1, 2)

            for g in range(2):
                tokens(0, g)
            for n in range(3):
                qkv(0, n)
            loop(pe, batch)


BF16 = mybir.dt.bfloat16

TOKENS = TILES * P
EXPERTS, TOP_K, HIDDEN = 8, 2, 512
DEPTH_SCALE = 1.0 / 12 ** 0.5
SLOT_TILES = TOP_K * TILES + EXPERTS
PARTS = HIDDEN // P


def mixture_of_experts(nc, k, x_sb, wr_dram, wg_dram, wu_dram, wd_dram, xn_dram, y_dram, name):
    with ExitStack() as ctx:
        def sb(n, *shape, dt=F32):
            return ctx.enter_context(nc.sbuf_tensor(name + n, list(shape), dt))

        def psum(cx, n, *shape):
            return cx.enter_context(nc.psum_tensor(name + n, list(shape), F32))

        def signal(n, per=1):
            return Signal(nc.alloc_semaphore(name + n), per)

        wr = sb("wr", P, EXPERTS)
        wg, wu, wd = sb("wg", P, EXPERTS * HIDDEN), sb("wu", P, EXPERTS * HIDDEN), sb("wd", P, EXPERTS * HIDDEN)
        top, best = sb("top", P, TILES, 8), sb("best", P, TILES, 8, dt=U32)
        weight = sb("weight", P, TOP_K, TILES)
        token_row, out_row = sb("token_row", P, SLOT_TILES, dt=U32), sb("out_row", P, SLOT_TILES, dt=U32)
        expert_at = sb("expert_at", 1, SLOT_TILES, dt=I32)
        loaded = signal("loaded")
        route(nc, k, x_sb, wr_dram, wg_dram, wu_dram, wd_dram, xn_dram, wr, wg, wu, wd, top, best, loaded, name)
        place(nc, k, top, best, weight, token_row, out_row, expert_at, name)
        run_experts(nc, k, wg, wu, wd, token_row, out_row, expert_at, xn_dram, y_dram, loaded, name)
        combine(nc, x_sb, weight, y_dram, name)


def route(nc, k, x_sb, wr_dram, wg_dram, wu_dram, wd_dram, xn_dram, wr, wg, wu, wd, top, best, loaded, name):
    with ExitStack() as ctx:
        def sb(n, *shape, dt=F32):
            return ctx.enter_context(nc.sbuf_tensor(name + n, list(shape), dt))

        def signal(n, per=1):
            return Signal(nc.alloc_semaphore(name + n), per)

        G, GROUPS = 8, TILES // 8
        stats, moments, rstd = sb("stats", P, TILES, 6), sb("moments", P, TILES, 2), sb("rstd", P, TILES)
        xn, xT = [sb(f"xn{n}", P, G, C) for n in range(GROUPS)], [sb(f"xT{n}", P, G, P) for n in range(2)]
        lg, m8, i8 = sb("lg", P, G, 8), sb("m8", P, G, 8), sb("i8", P, G, 8, dt=U32)
        tp = [ctx.enter_context(nc.psum_tensor(f"{name}tp{n}", [P, 512], F32)) for n in range(4)]
        lp = [ctx.enter_context(nc.psum_tensor(f"{name}lp{n}", [P, 512], F32)) for n in range(2)]
        wr_loaded = signal("wr_loaded")
        bn_done, aggr_done, var_ready, root_ready, rstd_ready, xn_ready = (
            signal(n, p) for n, p in (("bn", TILES), ("aggr", TILES), ("var", 1), ("root", 1), ("rstd", 1), ("xn_ready", 8)))
        tp_full, tp_read, lg_full, lg_ready = signal("tp_full", 2), signal("tp_read", 2), signal("lg_full"), signal("lg_ready")
        m8_ready, i8_ready, kept = signal("m8", 8), signal("i8_", 8), signal("kept", 2)
        stored = signal("stored", 16)
        xn_rows = xn_dram.rearrange("(n p) c -> p n c", p=P)
        block = ctx.enter_context(nc.Block())

        @block.sync
        def _(sp):
            sp.dma_start(wr[:, :], wr_dram).then_inc(wr_loaded.sem, 16)
            for g in range(GROUPS):
                sp.wait_ge(xn_ready.sem, xn_ready.at(g, 8))
                sp.dma_start(xn_rows[:, G * g:G * g + G, :], xn[g][:, :, :]).then_inc(stored.sem, 16)
            if stored.due(GROUPS, 0):
                sp.wait_ge(stored.sem, stored.at(GROUPS, 0))

        @block.vector
        def _(dve):
            def rest(g):
                dve.wait_ge(lg_ready.sem, lg_ready.at(g, 1))
                if kept.due(g, 0):
                    dve.wait_ge(kept.sem, kept.at(g, 0))
                for j in range(G):
                    dve.max(m8[:, j, :], lg[:, j, :]).then_inc(m8_ready.sem, 1)
                dve.wait_ge(m8_ready.sem, m8_ready.at(g, 8))
                for j in range(G):
                    dve.max_index(i8[:, j, :], m8[:, j, :], lg[:, j, :]).then_inc(i8_ready.sem, 1)
                dve.wait_ge(i8_ready.sem, i8_ready.at(g, 8))
                dve.tensor_copy(top[:, G * g:G * g + G, :], m8[:, :, :]).then_inc(kept.sem, 1)
                dve.tensor_copy(best[:, G * g:G * g + G, :], i8[:, :, :]).then_inc(kept.sem, 1)

            for t in range(TILES):
                dve.bn_stats(stats[:, t, :], x_sb[:, t * C:(t + 1) * C]).then_inc(bn_done.sem, 1)
            for t in range(TILES):
                dve.wait_ge(bn_done.sem, bn_done.at(0, t + 1))
                dve.bn_aggr(moments[:, t, :], stats[:, t, :]).then_inc(aggr_done.sem, 1)
            dve.wait_ge(aggr_done.sem, aggr_done.at(0, TILES))
            dve.tensor_scalar(rstd[:, :], moments[:, :, 1], EPS_LN, None, ALU.add).then_inc(var_ready.sem, 1)
            dve.wait_ge(root_ready.sem, root_ready.at(0, 1))
            dve.reciprocal(rstd[:, :], rstd[:, :]).then_inc(rstd_ready.sem, 1)
            dve.wait_ge(rstd_ready.sem, rstd_ready.at(0, 1))
            for g in range(GROUPS):
                for j in range(G):
                    t = G * g + j
                    dve.tensor_scalar(xn[g][:, j, :], x_sb[:, t * C:(t + 1) * C], moments[:, t, 0:1],
                                      rstd[:, t:t + 1], ALU.subtract, ALU.mult).then_inc(xn_ready.sem, 1)
                if g >= 2:
                    rest(g - 2)
            rest(GROUPS - 2)
            rest(GROUPS - 1)
            if kept.due(GROUPS, 0):
                dve.wait_ge(kept.sem, kept.at(GROUPS, 0))

        @block.scalar
        def _(act):
            for w, dram in ((wg, wg_dram), (wu, wu_dram)):
                act.dma_start(w[:, :].rearrange("c (e h) -> c e h", e=EXPERTS), dram.rearrange("e c h -> c e h")).then_inc(loaded.sem, 16)
            act.dma_start(wd[:, :].rearrange("h (e j c) -> h e j c", e=EXPERTS, j=PARTS),
                          wd_dram.rearrange("e (j h) c -> h e j c", h=P)).then_inc(loaded.sem, 16)
            act.wait_ge(var_ready.sem, var_ready.at(0, 1))
            act.activation(rstd[:, :], rstd[:, :], ACT.Sqrt).then_inc(root_ready.sem, 1)

            def logits(g):
                act.wait_ge(lg_full.sem, lg_full.at(g, 1))
                if i8_ready.due(g, 0):
                    act.wait_ge(i8_ready.sem, i8_ready.at(g, 0))
                act.activation(lg[:, :, :].rearrange("p a b -> p (a b)"), lp[g % 2][:, 0:64], ACT.Copy).then_inc(lg_ready.sem, 1)

            for g in range(GROUPS):
                if lg_full.due(g - 1, 0):
                    act.wait_ge(lg_full.sem, lg_full.at(g - 1, 0))
                for h in range(2):
                    act.wait_ge(tp_full.sem, tp_full.at(g, h + 1))
                    act.activation(xT[g % 2][:, 4 * h:4 * h + 4, :].rearrange("p a b -> p (a b)"), tp[2 * (g % 2) + h][:, :], ACT.Copy).then_inc(tp_read.sem, 1)
                if g:
                    logits(g - 1)
            logits(GROUPS - 1)

        @block.tensor
        def _(pe):
            pe.wait_ge(wr_loaded.sem, wr_loaded.at(0, 16))

            def transposes(g):
                for h in range(2):
                    pe.wait_ge(xn_ready.sem, xn_ready.at(g, 4 * h + 4))
                    if tp_read.due(g - 2, h + 1):
                        pe.wait_ge(tp_read.sem, tp_read.at(g - 2, h + 1))
                    for j in range(4):
                        mm = pe.transpose(tp[2 * (g % 2) + h][:, P * j:P * j + P], xn[g][:, 4 * h + j, :], k["ident"][:, :])
                    mm.then_inc(tp_full.sem, 1)

            transposes(0)
            for g in range(GROUPS):
                if g + 1 < GROUPS:
                    transposes(g + 1)
                pe.wait_ge(tp_read.sem, tp_read.at(g, 2))
                if lg_ready.due(g - 1, 0):
                    pe.wait_ge(lg_ready.sem, lg_ready.at(g - 1, 0))
                for j in range(G):
                    mm = pe.matmul(lp[g % 2][:, 8 * j:8 * j + 8], xT[g % 2][:, j, :], wr[:, :], start=True, stop=True)
                mm.then_inc(lg_full.sem, 1)


def place(nc, k, top, best, weight, token_row, out_row, expert_at, name):
    with ExitStack() as ctx:
        def sb(n, *shape, dt=F32):
            return ctx.enter_context(nc.sbuf_tensor(name + n, list(shape), dt))

        def signal(n, per=1):
            return Signal(nc.alloc_semaphore(name + n), per)

        ei, ef, idx, oh = sb("ei", P, 8, dt=I32), sb("ef", P, 8), sb("idx", P, 2, TILES), sb("oh", P, 2, 8, TILES)
        tok, tok_f = sb("tok", P, TILES, dt=I32), sb("tok_f", P, TILES)
        col, col_f = sb("col", P, P, dt=I32), sb("col_f", P, P)
        spare, spare_f = sb("spare", P, SLOT_TILES, dt=I32), sb("spare_f", P, SLOT_TILES)
        both, cum, reset = sb("both", P, 8, TILES), sb("cum", P, 8, TILES), sb("reset", P, 8, TILES)
        total, cnt, need, end = sb("total", P, 8), sb("cnt", P, 8), sb("need", P, 8), sb("end", P, 8)
        need_i = sb("need_i", P, 8, dt=I32)
        off = sb("off", P, 8)
        pick, slot = sb("pick", P, 8, TILES), sb("slot", P, 2, TILES)
        slot_i, a_i, p_i = (sb(n, P, 2 * TILES, dt=I32) for n in ("slot_i", "a_i", "p_i"))
        a_f, p_f = sb("a_f", P, 2 * TILES), sb("p_f", P, 2 * TILES)
        gap, e1 = sb("gap", P, TILES), sb("e1", P, TILES)
        SOME = 8
        B, hot_a = [sb(f"B{n}", P, SOME, P, dt=BF16) for n in range(2)], [sb(f"hot_a{n}", P, SOME, SLOT_TILES, dt=BF16) for n in range(2)]
        A = [sb(f"A{n}", P, SOME, 2, SLOT_TILES, dt=BF16) for n in range(2)]
        code, code_i, part_i = sb("code", P, 2 * TILES), sb("code_i", P, 2 * TILES, dt=I32), sb("part_i", P, 2 * TILES, dt=I32)
        parts = sb("parts", P, 2, 2 * TILES)
        got, late, empty = sb("got", P, SLOT_TILES), sb("late", P, SLOT_TILES), sb("empty", P, SLOT_TILES)
        row = sb("row", P, SLOT_TILES)
        passed = sb("passed", 1, SLOT_TILES, 8)
        at_f = sb("at_f", 1, SLOT_TILES)
        cp = ctx.enter_context(nc.psum_tensor(f"{name}cp", [P, 512], F32))
        ip = ctx.enter_context(nc.psum_tensor(f"{name}ip", [P, 512], F32))
        counted, iotas, gap_ready, e1_ready = signal("counted"), signal("iotas"), signal("gap_ready"), signal("e1_ready")
        ones_ready = signal("ones_ready")
        total_ready, hot_ready, place_ready, tile_ready, inverted = (signal(n) for n in ("total_ready", "hot_ready", "place_ready", "tile_ready", "inverted"))
        step = signal("step")
        block = ctx.enter_context(nc.Block())

        @block.gpsimd
        def _(pool):
            pool.iota(ei[:, :], [[1, 8]], base=0, channel_multiplier=0).then_inc(iotas.sem, 1)
            pool.iota(tok[:, :], [[P, TILES]], base=1, channel_multiplier=1).then_inc(iotas.sem, 1)
            pool.iota(col[:, :], [[1, P]], base=0, channel_multiplier=0).then_inc(iotas.sem, 1)
            pool.iota(spare[:, :], [[P, SLOT_TILES]], base=TOP_K * TOKENS, channel_multiplier=1).then_inc(iotas.sem, 1)
            for g in range(2 * TILES // SOME):
                pool.wait_ge(hot_ready.sem, hot_ready.at(0, g + 1))
                pool.tensor_tensor(A[g % 2][:, :, 1, :], hot_a[g % 2][:, :, :], wide(parts[:, 1, SOME * g:SOME * g + SOME], 2, [P, SOME, SLOT_TILES]),
                                   ALU.mult).then_inc(ones_ready.sem, 1)

        @block.scalar
        def _(act):
            act.wait_ge(gap_ready.sem, gap_ready.at(0, 1))
            act.activation(e1[:, :], gap[:, :], ACT.Exp).then_inc(e1_ready.sem, 1)

        @block.tensor
        def _(pe):
            pe.wait_ge(total_ready.sem, total_ready.at(0, 1))
            pe.matmul(cp[:, 0:8], k["before"][:, :], total[:, :], start=True, stop=True)
            pe.matmul(cp[:, 8:16], k["ones"][:, :], total[:, :], start=True, stop=True).then_inc(counted.sem, 1)
            for g in range(2 * TILES // SOME):
                pe.wait_ge(tile_ready.sem, tile_ready.at(0, g + 1))
                pe.wait_ge(ones_ready.sem, ones_ready.at(0, g + 1))
                pe.wait_ge(place_ready.sem, place_ready.at(0, g + 1))
                for j in range(SOME):
                    mm = pe.matmul(ip[:, 0:2 * SLOT_TILES], B[g % 2][:, j, :], A[g % 2][:, j, :, :].rearrange("p a b -> p (a b)"),
                                   start=(g == 0 and j == 0), stop=(g == 2 * TILES // SOME - 1 and j == SOME - 1))
                mm.then_inc(inverted.sem, 1)

        @block.vector
        def _(dve):
            steps = [0]

            def then(ins):
                steps[0] += 1
                ins.then_inc(step.sem, 1)
                dve.wait_ge(step.sem, steps[0])

            dve.wait_ge(iotas.sem, iotas.at(0, 4))
            for i, f in ((ei, ef), (tok, tok_f), (col, col_f), (spare, spare_f)):
                then(dve.tensor_copy(f[:, :], i[:, :]))
            dve.tensor_tensor(gap[:, :], top[:, :, 1], top[:, :, 0], ALU.subtract).then_inc(gap_ready.sem, 1)
            then(dve.tensor_copy(idx[:, :, :].rearrange("p a b -> p b a"), best[:, :, 0:2]))
            for n in range(2):
                then(dve.tensor_tensor(oh[:, n, :, :], wide(ef[:, :], 2, [P, 8, TILES]), wide(idx[:, n, :], 1, [P, 8, TILES]), ALU.is_equal))
            then(dve.tensor_tensor(both[:, :, :], oh[:, 0, :, :], oh[:, 1, :, :], ALU.add))
            then(dve.memset(reset[:, :, :], 1.0))
            then(dve.memset(reset[:, :, 0:1], 0.0))
            then(dve.tensor_tensor_scan(cum[:, :, :].rearrange("p a b -> p (a b)"), reset[:, :, :].rearrange("p a b -> p (a b)"),
                                        both[:, :, :].rearrange("p a b -> p (a b)"), 0.0, ALU.mult, ALU.add))
            dve.tensor_copy(total[:, :], cum[:, :, TILES - 1]).then_inc(total_ready.sem, 1)
            dve.wait_ge(e1_ready.sem, e1_ready.at(0, 1))
            then(dve.tensor_scalar(gap[:, :], e1[:, :], 1.0, None, ALU.add))
            then(dve.reciprocal(weight[:, 0, :], gap[:, :]))
            then(dve.tensor_tensor(weight[:, 1, :], e1[:, :], weight[:, 0, :], ALU.mult))
            dve.wait_ge(counted.sem, counted.at(0, 1))
            then(dve.tensor_copy(off[:, :], cp[:, 0:8]))
            then(dve.tensor_scalar(need_i[:, :], cp[:, 8:16], float(P - 1), None, ALU.add))
            then(dve.tensor_scalar(need_i[:, :], need_i[:, :], 7, None, ALU.logical_shift_right))
            then(dve.tensor_copy(need[:, :], need_i[:, :]))
            then(dve.tensor_tensor_scan(end[:, :], k["ones"][:, 0:8], need[:, :], 0.0, ALU.mult, ALU.add))
            then(dve.tensor_tensor(cnt[:, :], end[:, :], need[:, :], ALU.subtract))
            then(dve.scalar_tensor_tensor(off[:, :], cnt[:, :], float(P), off[:, :], ALU.mult, ALU.add))
            then(dve.tensor_tensor(cum[:, :, :], cum[:, :, :], both[:, :, :], ALU.subtract))
            then(dve.tensor_tensor(cum[:, :, :], cum[:, :, :], wide(off[:, :], 2, [P, 8, TILES]), ALU.add))
            for n in range(2):
                then(dve.tensor_tensor(pick[:, :, :], cum[:, :, :], oh[:, n, :, :], ALU.mult))
                then(dve.tensor_reduce(slot[:, n, :], pick[:, :, :].rearrange("p e t -> p t e"), AX.X, ALU.add))
            then(dve.tensor_copy(slot_i[:, :], slot[:, :, :].rearrange("p a b -> p (a b)")))
            then(dve.tensor_scalar(a_i[:, :], slot_i[:, :], 7, None, ALU.logical_shift_right))
            then(dve.tensor_scalar(p_i[:, :], slot_i[:, :], P - 1, None, ALU.bitwise_and))
            then(dve.tensor_copy(a_f[:, :], a_i[:, :]))
            then(dve.tensor_copy(p_f[:, :], p_i[:, :]))
            then(dve.tensor_copy(code[:, 0:TILES], tok_f[:, :]))
            then(dve.tensor_scalar(code[:, TILES:2 * TILES], tok_f[:, :], float(TOKENS), None, ALU.add))
            then(dve.tensor_copy(code_i[:, :], code[:, :]))
            then(dve.tensor_scalar(part_i[:, :], code_i[:, :], 7, None, ALU.logical_shift_right))
            then(dve.tensor_copy(parts[:, 0, :], part_i[:, :]))
            then(dve.tensor_scalar(part_i[:, :], code_i[:, :], P - 1, None, ALU.bitwise_and))
            then(dve.tensor_copy(parts[:, 1, :], part_i[:, :]))
            for g in range(2 * TILES // SOME):
                some = slice(SOME * g, SOME * g + SOME)
                if inverted.due(0, g - 1):
                    dve.wait_ge(inverted.sem, inverted.at(0, g - 1))
                dve.tensor_tensor(hot_a[g % 2][:, :, :], wide(col_f[:, 0:SLOT_TILES], 1, [P, SOME, SLOT_TILES]), wide(a_f[:, some], 2, [P, SOME, SLOT_TILES]),
                                  ALU.is_equal).then_inc(hot_ready.sem, 1)
                dve.tensor_tensor(B[g % 2][:, :, :], wide(col_f[:, :], 1, [P, SOME, P]), wide(p_f[:, some], 2, [P, SOME, P]),
                                  ALU.is_equal).then_inc(place_ready.sem, 1)
                dve.wait_ge(hot_ready.sem, hot_ready.at(0, g + 1))
                dve.tensor_tensor(A[g % 2][:, :, 0, :], hot_a[g % 2][:, :, :], wide(parts[:, 0, some], 2, [P, SOME, SLOT_TILES]),
                                  ALU.mult).then_inc(tile_ready.sem, 1)
            then(dve.tensor_tensor(passed[:, :, :], wide(col_f[0:1, 0:SLOT_TILES], 2, [1, SLOT_TILES, 8]), wide(end[0:1, :], 1, [1, SLOT_TILES, 8]), ALU.is_ge))
            then(dve.tensor_reduce(at_f[:, :], passed[:, :, :], AX.X, ALU.add))
            then(dve.tensor_scalar(at_f[:, :], at_f[:, :], float(EXPERTS - 1), float(HIDDEN), ALU.min, ALU.mult))
            then(dve.tensor_copy(expert_at[:, :], at_f[:, :]))
            dve.wait_ge(inverted.sem, inverted.at(0, 2 * TILES // SOME))
            then(dve.tensor_copy(late[:, :], ip[:, 0:SLOT_TILES]))
            then(dve.scalar_tensor_tensor(got[:, :], late[:, :], float(P), ip[:, SLOT_TILES:2 * SLOT_TILES], ALU.mult, ALU.add))
            then(dve.tensor_scalar(empty[:, :], got[:, :], 0.0, None, ALU.is_equal))
            then(dve.scalar_tensor_tensor(late[:, :], spare_f[:, :], 1.0, empty[:, :], ALU.add, ALU.mult))
            then(dve.scalar_tensor_tensor(row[:, :], got[:, :], -1.0, late[:, :], ALU.add, ALU.add))
            then(dve.tensor_copy(out_row[:, :], row[:, :]))
            then(dve.tensor_scalar(late[:, :], got[:, :], float(TOKENS), float(-TOKENS), ALU.is_gt, ALU.mult))
            then(dve.tensor_tensor(row[:, :], got[:, :], late[:, :], ALU.add))
            then(dve.tensor_scalar(row[:, :], row[:, :], 1.0, -1.0, ALU.max, ALU.add))
            then(dve.tensor_copy(token_row[:, :], row[:, :]))


def run_experts(nc, k, wg, wu, wd, token_row, out_row, expert_at, xn_dram, y_dram, loaded, name):
    with ExitStack() as ctx:
        def sb(n, *shape, dt=F32):
            return ctx.enter_context(nc.sbuf_tensor(name + n, list(shape), dt))

        def psum(n):
            return ctx.enter_context(nc.psum_tensor(name + n, [P, 512], F32))

        def signal(n, per=1):
            return Signal(nc.alloc_semaphore(name + n), per)

        XB = 4
        xg, row_x, row_y = [sb(f"xg{n}", P, C) for n in range(XB)], [sb(f"row_x{n}", P, 1, dt=U32) for n in range(XB)], [sb(f"row_y{n}", P, 1, dt=U32) for n in range(XB)]
        xgT, act_g, h, out = ([sb(f"{m}{n}", P, w) for n in range(2)] for m, w in (("xgT", P), ("sg", 512), ("h", 512), ("yo", C)))
        wg_now, wu_now = ([sb(f"{m}{n}", P, HIDDEN) for n in range(2)] for m in ("wg_now", "wu_now"))
        gp, up = [psum(f"gp{n}") for n in range(2)], [psum(f"up{n}") for n in range(2)]
        xp, dp = psum("xp"), [psum(f"dp{n}") for n in range(2)]
        rows_x, rows_y, gathered = signal("rows_x"), signal("rows_y"), [signal(f"gathered{n}") for n in range(XB)]
        x_full, x_read, gu_full, g_done, h_done = (signal(n) for n in ("x_full", "x_read", "gu_full", "g_done", "h_done"))
        wg_ready, wu_ready, d_full, d_read = (signal(n) for n in ("wg_ready", "wu_ready", "d_full", "d_read"))
        scattered = [signal(f"scattered{n}") for n in range(2)]
        alone = signal("e_alone")
        N = SLOT_TILES

        def column(ap, a):
            return ap[:, bass.ds(a, 1)] if not isinstance(a, int) else ap[:, a:a + 1]

        block = ctx.enter_context(nc.Block())

        @block.gpsimd
        def _(pool):
            def gather(a, u, at):
                if at is None or at >= XB:
                    x_full_wait(pool, a - XB + 1)
                pool.tensor_copy(row_x[u][:, :], column(token_row, a)).then_inc(rows_x.sem, 1)
                pool.wait_ge(rows_x.sem, a + 1)
                pool.sem_inc(alone.sem, 1)
                pool.indirect_dma_start(xg[u][:, :], None, xn_dram, bass.IndirectOffsetOnAxis(row_x[u][:, 0:1], 0)).then_inc(gathered[u].sem, 16)

            def x_full_wait(eng, v):
                eng.wait_ge(x_full.sem, v)
                eng.sem_inc(alone.sem, 1)

            def scatter(a, u, w):
                d_read_wait(a + 1)
                pool.tensor_copy(row_y[u][:, :], column(out_row, a)).then_inc(rows_y.sem, 1)
                pool.wait_ge(rows_y.sem, a + 1)
                pool.sem_inc(alone.sem, 1)
                pool.indirect_dma_start(y_dram, bass.IndirectOffsetOnAxis(row_y[u][:, 0:1], 0), out[w][:, :], None).then_inc(scattered[w].sem, 16)

            def d_read_wait(v):
                pool.wait_ge(d_read.sem, v)
                pool.sem_inc(alone.sem, 1)

            for a in range(3):
                gather(a, a, a)

            def step(s, u, at):
                if at is None or at + 3 < N:
                    gather(s + 3, (u + 3) % 4, None if at is None else at + 3)
                if at is None or at >= 2:
                    scatter(s - 2, (u - 2) % 4, u % 2)

            for s in range(4):
                step(s, s, s)
            with pool.Fori(0, N // 4 - 2) as r:
                for u in range(4):
                    step(r * 4 + (4 + u), u, None)
            for s in range(N - 4, N + 2):
                step(s, s % 4, s)
            for w in range(2):
                pool.wait_ge(scattered[w].sem, 16 * (N // 2))

        @block.tensor
        def _(pe):
            pe.wait_ge(loaded.sem, loaded.at(0, 48))

            def transpose_x(a, u, at):
                if at is None or at >= 1:
                    pe.wait_ge(x_read.sem, a)
                wait_gathered(pe, a, u)
                pe.transpose(xp[:, 0:P], xg[u][:, :], k["ident"][:, :]).then_inc(x_full.sem, 1)

            def wait_gathered(eng, a, u):
                eng.wait_ge(gathered[u].sem, (a - u + 4) * 4)

            def step(s, u, at):
                if at is None or at >= 1:
                    e_down = pe.value_load(column(expert_at, s - 1), min_val=0, max_val=(EXPERTS - 1) * HIDDEN)
                if at is None or at + 1 < N:
                    transpose_x(s + 1, (u + 1) % 4, None if at is None else at + 1)
                if at is None or at < N:
                    pe.wait_ge(x_read.sem, s + 1)
                    pe.wait_ge(wg_ready.sem, s + 1)
                    pe.wait_ge(wu_ready.sem, s + 1)
                    if at is None or at >= 2:
                        pe.wait_ge(h_done.sem, s - 1)
                    for bank, weights in ((gp, wg_now), (up, wu_now)):
                        for j in range(PARTS):
                            mm = pe.matmul(bank[u % 2][:, P * j:P * j + P], weights[u % 2][:, P * j:P * j + P], xgT[u % 2][:, :], start=True, stop=True)
                    mm.then_inc(gu_full.sem, 1)
                if at is None or at >= 1:
                    v = (u - 1) % 2
                    pe.wait_ge(h_done.sem, s)
                    if at is None or at >= 3:
                        pe.wait_ge(d_read.sem, s - 2)
                    for j in range(PARTS):
                        mm = pe.matmul(dp[v][:, 0:C], h[v][:, P * j:P * j + P], wd[:, bass.ds(e_down + j * C, C)],
                                       start=(j == 0), stop=(j == PARTS - 1))
                    mm.then_inc(d_full.sem, 1)

            transpose_x(0, 0, 0)
            for s in range(4):
                step(s, s, s)
            with pe.Fori(0, N // 4 - 2) as r:
                for u in range(4):
                    step(r * 4 + (4 + u), u, None)
            for s in range(N - 4, N + 1):
                step(s, s % 4, s)

        @block.scalar
        def _(act):
            act.wait_ge(loaded.sem, loaded.at(0, 48))

            def copy_weights(a, u, at):
                e = act.value_load(column(expert_at, a), min_val=0, max_val=(EXPERTS - 1) * HIDDEN)
                if at is None or at >= 2:
                    act.wait_ge(gu_full.sem, a - 1)
                for now, w, ready in ((wg_now, wg, wg_ready), (wu_now, wu, wu_ready)):
                    act.activation(now[u % 2][:, :], w[:, bass.ds(e, HIDDEN)], ACT.Copy).then_inc(ready.sem, 1)

            def read_x(a, u, at):
                act.wait_ge(x_full.sem, a + 1)
                if at is None or at >= 2:
                    act.wait_ge(gu_full.sem, a - 1)
                act.activation(xgT[u % 2][:, :], xp[:, 0:P], ACT.Copy).then_inc(x_read.sem, 1)

            def step(s, u, at):
                if at is None or at + 1 < N:
                    ahead = None if at is None else at + 1
                    copy_weights(s + 1, u + 1, ahead)
                    read_x(s + 1, u + 1, ahead)
                if at is None or at < N:
                    act.wait_ge(gu_full.sem, s + 1)
                    if at is None or at >= 2:
                        act.wait_ge(h_done.sem, s - 1)
                    act.activation(act_g[u % 2][:, :], gp[u % 2][:, :], ACT.Silu).then_inc(g_done.sem, 1)

            copy_weights(0, 0, 0)
            read_x(0, 0, 0)
            for s in range(4):
                step(s, s, s)
            with act.Fori(0, N // 4 - 2) as r:
                for u in range(4):
                    step(r * 4 + (4 + u), u, None)
            for s in range(N - 4, N):
                step(s, s % 4, s)

        @block.vector
        def _(dve):
            def step(s, u, at):
                if at is None or at < N:
                    dve.wait_ge(g_done.sem, s + 1)
                    if at is None or at >= 2:
                        dve.wait_ge(d_full.sem, s - 1)
                    dve.tensor_tensor(h[u % 2][:, :], act_g[u % 2][:, :], up[u % 2][:, :], ALU.mult).then_inc(h_done.sem, 1)
                if at is None or at >= 1:
                    v = (u - 1) % 2
                    dve.wait_ge(d_full.sem, s)
                    if at is None or at >= 3:
                        dve.wait_ge(scattered[v].sem, (s - 1 - v) * 8)
                    dve.tensor_scalar(out[v][:, :], dp[v][:, 0:C], DEPTH_SCALE, None, ALU.mult).then_inc(d_read.sem, 1)

            for s in range(4):
                step(s, s, s)
            with dve.Fori(0, N // 4 - 2) as r:
                for u in range(4):
                    step(r * 4 + (4 + u), u, None)
            for s in range(N - 4, N + 1):
                step(s, s % 4, s)


def combine(nc, x_sb, weight, y_dram, name):
    with ExitStack() as ctx:
        G, RING = 4, 4
        y = [[ctx.enter_context(nc.sbuf_tensor(f"{name}y{n}{m}", [P, G, C], F32)) for m in range(TOP_K)] for n in range(RING)]
        arrived = [[nc.alloc_semaphore(f"{name}arrived{n}{m}") for m in range(TOP_K)] for n in range(RING)]
        first_added, scaled, added = (Signal(nc.alloc_semaphore(name + n), p) for n, p in (("first_added", G), ("scaled", G), ("added", 1)))
        rows = y_dram[0:TOP_K * TOKENS, :].rearrange("(m n p) c -> m p n c", m=TOP_K, p=P)
        block = ctx.enter_context(nc.Block())

        @block.sync
        def _(sp):
            for g in range(TILES // G):
                if added.due(g - RING, 1):
                    sp.wait_ge(added.sem, added.at(g - RING, 1))
                for m in range(TOP_K):
                    sp.dma_start(y[g % RING][m][:, :, :], rows[m, :, G * g:G * g + G, :]).then_inc(arrived[g % RING][m], 16)

        @block.vector
        def _(dve):
            for g in range(TILES // G):
                dve.wait_ge(arrived[g % RING][0], 16 * (g // RING + 1))
                for j in range(G):
                    t = G * g + j
                    dve.scalar_tensor_tensor(x_sb[:, t * C:t * C + C], y[g % RING][0][:, j, :], weight[:, 0, t:t + 1],
                                             x_sb[:, t * C:t * C + C], ALU.mult, ALU.add).then_inc(first_added.sem, 1)

        @block.scalar
        def _(act):
            for g in range(TILES // G):
                act.wait_ge(arrived[g % RING][1], 16 * (g // RING + 1))
                for j in range(G):
                    t = G * g + j
                    act.activation(y[g % RING][1][:, j, :], y[g % RING][1][:, j, :], ACT.Copy, scale=weight[:, 1, t:t + 1]).then_inc(scaled.sem, 1)

        @block.gpsimd
        def _(pool):
            for g in range(TILES // G):
                pool.wait_ge(first_added.sem, first_added.at(g, G))
                pool.wait_ge(scaled.sem, scaled.at(g, G))
                x = x_sb[:, G * g * C:G * (g + 1) * C]
                pool.tensor_tensor(x, x, y[g % RING][1][:, :, :].rearrange("p t c -> p (t c)"), ALU.add).then_inc(added.sem, 1)
            if added.due(TILES // G, 0):
                pool.wait_ge(added.sem, added.at(TILES // G, 0))


HEADS, KD, VD, TAPS = 8, 128, 32, 4
QUADS = 4
BLOCKS = 2 * HEADS + 2
LEVELS = (2, 4, 8, 16, 32, 64)
EPS_NORM, EPS_RMS = 1e-6, 1e-5
G_, BETA, GAMMA, GAMMA_END, DECAY_END = range(5)


def delta_attention(nc, k, x_sb, w, o_dram):
    with ExitStack() as ctx:
        xT = ctx.enter_context(nc.sbuf_tensor("b_xT", [P, BATCHES, TAPS - 1 + T], F32))
        prm = ctx.enter_context(nc.sbuf_tensor("b_prm", [P, TILES, 5, HEADS], F32))
        c = {name: ctx.enter_context(nc.sbuf_tensor("b_" + name, shape, F32)) for name, shape in (
            ("wq", [P, HEADS * KD]), ("wk", [P, HEADS * KD]), ("wv", [P, HEADS * VD]), ("taps", [P, BLOCKS, TAPS]),
            ("mask1", [P, P]), ("wg", [P, HEADS * VD]), ("wo", [P, 2, C]), ("nw", [P, 1]),
            ("squares", [P, TILES // 2, 2, HEADS]))}
        c["masks"] = [ctx.enter_context(nc.sbuf_tensor(f"b_mask{s}", [P, 64], F32)) for s in LEVELS]
        chunk_loaded, output_loaded, masked = (Signal(nc.alloc_semaphore("b_" + n)) for n in ("chunk_loaded", "output_loaded", "masked"))
        delta_inputs(nc, k, x_sb, w, xT, prm, c, chunk_loaded, output_loaded, masked)
        delta_chunks(nc, k, w, xT, prm, o_dram, c, chunk_loaded, masked)
        delta_output(nc, k, x_sb, w, xT, o_dram, c, output_loaded)


def rows(l):
    return P // 2 if l == len(LEVELS) - 1 else P


def delta_inputs(nc, k, x_sb, w, xT, prm, c, chunk_loaded, output_loaded, masked):
    with ExitStack() as ctx:
        def sb(n, *shape, dt=F32):
            return ctx.enter_context(nc.sbuf_tensor("b0_" + n, list(shape), dt))

        def signal(n, per=1):
            return Signal(nc.alloc_semaphore("b0_" + n), per)

        G = 8
        stats, moments, rstd = sb("stats", P, TILES, 6), sb("moments", P, TILES, 2), sb("rstd", P, TILES)
        xn = [sb(f"xn{n}", P, G, C) for n in range(BATCHES)]
        wab, a_log, dt = sb("wab", P, 2 * HEADS), sb("a_log", P, HEADS), sb("dt", P, HEADS)
        ab = sb("ab", P, TILES, 2 * HEADS)
        z, nz, lz, eb = (sb(n, P, TILES, HEADS) for n in ("z", "nz", "lz", "eb"))
        tp = [ctx.enter_context(nc.psum_tensor(f"b0_tp{n}", [P, 512], F32)) for n in range(2)]
        ap = [ctx.enter_context(nc.psum_tensor(f"b0_ap{n}", [P, 512], F32)) for n in range(2)]
        gp = [ctx.enter_context(nc.psum_tensor(f"b0_gp{n}", [P, 512], F32)) for n in range(3)]
        loaded, zeroed = signal("loaded"), signal("zeroed")
        bn_done, aggr_done, var_ready, root_ready, rstd_ready, xn_ready = (
            signal(n, p) for n, p in (("bn", TILES), ("aggr", TILES), ("var", 1), ("root", 1), ("rstd", 1), ("xn_ready", 8)))
        tp_full, tp_read, ab_full, ab_read = signal("tp_full", 2), signal("tp_read", 2), signal("ab_full"), signal("ab_read")
        step, nz_ready, exps, a_ready, g_ready, sums_full, decays = (signal(n) for n in ("step", "nz_ready", "exps", "a_ready", "g_ready", "sums_full", "decays"))
        lz_ready, mask_set = signal("lz_ready"), signal("mask_set")
        block = ctx.enter_context(nc.Block())

        @block.sync
        def _(sp):
            sp.dma_start(wab[:, 0:HEADS], w["Wa"]).then_inc(loaded.sem, 16)
            sp.dma_start(wab[:, HEADS:2 * HEADS], w["Wb"]).then_inc(loaded.sem, 16)
            sp.dma_start(a_log[:, :], w["A_log"].partition_broadcast(P)).then_inc(loaded.sem, 16)
            sp.dma_start(dt[:, :], w["dt_bias"].partition_broadcast(P)).then_inc(loaded.sem, 16)
            sp.dma_start(c["wk"][:, :], w["Wk"]).then_inc(chunk_loaded.sem, 16)
            sp.dma_start(c["wq"][:, :], w["Wq"]).then_inc(chunk_loaded.sem, 16)
            sp.dma_start(c["wv"][:, :], w["Wv"]).then_inc(chunk_loaded.sem, 16)
            for n, name in ((0, "conv_k"), (HEADS, "conv_q")):
                sp.dma_start(c["taps"][:, n:n + HEADS, :], w[name].rearrange("(h p) t -> p h t", p=P)).then_inc(chunk_loaded.sem, 16)
            sp.dma_start(c["taps"][:, 2 * HEADS:, :], w["conv_v"].rearrange("(h p) t -> p h t", p=P)).then_inc(chunk_loaded.sem, 16)
            sp.dma_start(c["wg"][:, :], w["Wg"]).then_inc(output_loaded.sem, 16)
            sp.dma_start(c["wo"][:, :, :], w["Wo"].rearrange("(h v) c -> v h c", v=P)).then_inc(output_loaded.sem, 16)
            for h in range(P // VD):
                sp.dma_start(c["nw"][VD * h:VD * h + VD, :], w["o_norm_w"].unsqueeze(1)).then_inc(output_loaded.sem, 16)

        @block.gpsimd
        def _(pool):
            pool.memset(xT[:, :, 0:TAPS - 1], 0.0).then_inc(zeroed.sem, 1)
            for m in c["masks"]:
                pool.memset(m[:, :], -1.0).then_inc(mask_set.sem, 1)
            pool.memset(c["mask1"][:, :], 0.0).then_inc(mask_set.sem, 1)
            pool.wait_ge(mask_set.sem, len(LEVELS) + 1)
            for l, (s, m) in enumerate(zip(LEVELS, c["masks"])):
                v = m[:, :].rearrange("p (b s) -> p b s", s=s)
                first, apart = (s, 2 * s) if rows(l) == P else (0, s)
                pool.affine_select(out=v, in_=v, compare_op=ALU.is_ge, fill=0.0, base=-first, pattern=[[-apart, 64 // s], [0, s]],
                                   channel_multiplier=1).then_inc(masked.sem, 1)
            v = c["mask1"][:, :].rearrange("p (a t) -> p a t", t=2)[:, :, 1]
            pool.affine_select(out=v, in_=v, compare_op=ALU.not_equal, fill=-1.0, base=0, pattern=[[2, 64]],
                               channel_multiplier=-1).then_inc(masked.sem, 1)
            pool.wait_ge(masked.sem, len(LEVELS) + 1)
            for l, (s, m) in enumerate(zip(LEVELS, c["masks"])):
                v = m[:, :].rearrange("p (b s) -> p b s", s=s)
                first, apart = (s, 2 * s) if rows(l) == P else (0, s)
                pool.affine_select(out=v, in_=v, compare_op=ALU.is_ge, fill=0.0, base=first + s - 1, pattern=[[apart, 64 // s], [0, s]],
                                   channel_multiplier=-1).then_inc(masked.sem, 1)

        @block.vector
        def _(dve):
            for t in range(TILES):
                dve.bn_stats(stats[:, t, :], x_sb[:, t * C:(t + 1) * C]).then_inc(bn_done.sem, 1)
            for t in range(TILES):
                dve.wait_ge(bn_done.sem, bn_done.at(0, t + 1))
                dve.bn_aggr(moments[:, t, :], stats[:, t, :]).then_inc(aggr_done.sem, 1)
            dve.wait_ge(aggr_done.sem, aggr_done.at(0, TILES))
            dve.tensor_scalar(rstd[:, :], moments[:, :, 1], EPS_LN, None, ALU.add).then_inc(var_ready.sem, 1)
            dve.wait_ge(root_ready.sem, root_ready.at(0, 1))
            dve.reciprocal(rstd[:, :], rstd[:, :]).then_inc(rstd_ready.sem, 1)
            dve.wait_ge(rstd_ready.sem, rstd_ready.at(0, 1))
            for t in range(TILES):
                dve.tensor_scalar(xn[t // G][:, t % G, :], x_sb[:, t * C:(t + 1) * C], moments[:, t, 0:1],
                                  rstd[:, t:t + 1], ALU.subtract, ALU.mult).then_inc(xn_ready.sem, 1)
            steps = [0]

            def then(ins):
                steps[0] += 1
                ins.then_inc(step.sem, 1)
                dve.wait_ge(step.sem, steps[0])

            dve.wait_ge(loaded.sem, loaded.at(0, 64))
            if ab_read.due(BATCHES, 0):
                dve.wait_ge(ab_read.sem, ab_read.at(BATCHES, 0))
            then(dve.tensor_tensor(z[:, :, :], ab[:, :, 0:HEADS], wide(dt[:, :], 1, [P, TILES, HEADS]), ALU.add))
            then(dve.tensor_scalar(nz[:, :, :], z[:, :, :], -1.0, None, ALU.mult))
            dve.tensor_tensor(nz[:, :, :], nz[:, :, :], z[:, :, :], ALU.min).then_inc(nz_ready.sem, 1)
            dve.wait_ge(lz_ready.sem, lz_ready.at(0, 1))
            then(dve.tensor_scalar(z[:, :, :], z[:, :, :], 0.0, None, ALU.max))
            then(dve.tensor_tensor(z[:, :, :], z[:, :, :], lz[:, :, :], ALU.add))
            dve.wait_ge(a_ready.sem, a_ready.at(0, 1))
            then(dve.tensor_tensor(z[:, :, :], z[:, :, :], wide(a_log[:, :], 1, [P, TILES, HEADS]), ALU.mult))
            dve.tensor_scalar(prm[:, :, G_, :], z[:, :, :], -1.0, None, ALU.mult).then_inc(g_ready.sem, 1)
            dve.wait_ge(exps.sem, exps.at(0, 2))
            then(dve.tensor_scalar(eb[:, :, :], eb[:, :, :], 1.0, None, ALU.add))
            then(dve.reciprocal(eb[:, :, :], eb[:, :, :]))
            then(dve.tensor_scalar(prm[:, :, BETA, :], eb[:, :, :], 2.0, None, ALU.mult))
            dve.wait_ge(decays.sem, decays.at(0, 3))
            then(dve.memset(prm[:, :, GAMMA_END:DECAY_END + 1, :].rearrange("p (b c) a h -> p b c a h", c=TPB)[:, :, TPB - 1], 0.0))

        @block.scalar
        def _(act):
            act.wait_ge(var_ready.sem, var_ready.at(0, 1))
            act.activation(rstd[:, :], rstd[:, :], ACT.Sqrt).then_inc(root_ready.sem, 1)

            def decays_out(g):
                act.wait_ge(ab_full.sem, ab_full.at(g, 1))
                act.activation(ab[:, G * g:G * g + G, :].rearrange("p a b -> p (a b)"), ap[g % 2][:, 0:128], ACT.Copy).then_inc(ab_read.sem, 1)

            for g in range(BATCHES):
                for h in range(2):
                    act.wait_ge(tp_full.sem, tp_full.at(g, h + 1))
                    act.activation(xT[:, g, TAPS - 1 + 512 * h:TAPS - 1 + 512 * h + 512], tp[h][:, :], ACT.Copy).then_inc(tp_read.sem, 1)
                if g:
                    decays_out(g - 1)
            decays_out(BATCHES - 1)
            act.wait_ge(loaded.sem, loaded.at(0, 64))
            act.activation(a_log[:, :], a_log[:, :], ACT.Exp).then_inc(a_ready.sem, 1)
            act.wait_ge(nz_ready.sem, nz_ready.at(0, 1))
            act.activation(nz[:, :, :], nz[:, :, :], ACT.Exp).then_inc(exps.sem, 1)
            if ab_read.due(BATCHES, 0):
                act.wait_ge(ab_read.sem, ab_read.at(BATCHES, 0))
            act.activation(eb[:, :, :], ab[:, :, HEADS:2 * HEADS], ACT.Exp, scale=-1.0).then_inc(exps.sem, 1)
            act.wait_ge(exps.sem, exps.at(0, 1))
            act.activation(lz[:, :, :], nz[:, :, :], ACT.Ln, bias=1.0).then_inc(lz_ready.sem, 1)
            act.wait_ge(sums_full.sem, sums_full.at(0, 1))
            for n, which in enumerate((GAMMA, GAMMA_END, DECAY_END)):
                act.activation(prm[:, :, which, :], gp[n][:, 0:256].rearrange("p (a b) -> p a b", b=HEADS), ACT.Exp).then_inc(decays.sem, 1)

        @block.tensor
        def _(pe):
            pe.wait_ge(loaded.sem, loaded.at(0, 64))

            def transposes(g):
                for h in range(2):
                    pe.wait_ge(xn_ready.sem, xn_ready.at(g, 4 * h + 4))
                    if tp_read.due(g - 1, h + 1):
                        pe.wait_ge(tp_read.sem, tp_read.at(g - 1, h + 1))
                    for j in range(4):
                        mm = pe.transpose(tp[h][:, P * j:P * j + P], xn[g][:, 4 * h + j, :], k["ident"][:, :])
                    mm.then_inc(tp_full.sem, 1)

            transposes(0)
            for g in range(BATCHES):
                if g + 1 < BATCHES:
                    transposes(g + 1)
                pe.wait_ge(tp_read.sem, tp_read.at(g, 2))
                if ab_read.due(g - 1, 0):
                    pe.wait_ge(ab_read.sem, ab_read.at(g - 1, 0))
                for j in range(G):
                    mm = pe.matmul(ap[g % 2][:, 16 * j:16 * j + 16], xT[:, g, TAPS - 1 + P * j:TAPS - 1 + P * j + P], wab[:, :], start=True, stop=True)
                mm.then_inc(ab_full.sem, 1)
            pe.wait_ge(g_ready.sem, g_ready.at(0, 1))
            for n, m in enumerate(("upto", "ones", "after")):
                mm = pe.matmul(gp[n][:, 0:256], k[m][:, :], prm[:, :, G_, :], start=True, stop=True)
            mm.then_inc(sums_full.sem, 1)


def delta_chunks(nc, k, w, xT, prm, o_dram, c, chunk_loaded, masked):
    with ExitStack() as ctx:
        def sb(n, *shape, dt=F32):
            return ctx.enter_context(nc.sbuf_tensor("b1_" + n, list(shape), dt))

        def psum(n):
            return ctx.enter_context(nc.psum_tensor("b1_" + n, [P, 512], F32))

        def signal(n, per=1):
            return Signal(nc.alloc_semaphore("b1_" + n), per)

        NL_ = len(LEVELS)
        PASSES = TILES // 2
        STATE = 3 * NL_ + 1
        S_AT, Z_AT, PW_AT = ([STATE + n for n in at] for at in ((0, 1, 2, 3), (4, 4, 5, 5), (6, 7, 8, 9)))
        SLOTS = STATE + 10
        PAIRS_, K_T, Q_T, V_T = BLOCKS // 2, 3, 7, 10
        E_AT, KQ_AT = [STATE + 2 * q for q in range(QUADS)], [STATE + 2 * q + 1 for q in range(QUADS)]
        ORDER = (0, 2, 1, 3)
        wq, wk, wv, taps, masks, mask1, squares = (c[n] for n in ("wq", "wk", "wv", "taps", "masks", "mask1", "squares"))
        W_EXT = TAPS - 1 + P
        PRE = 4
        xh, vT = sb("xh", P, 2, W_EXT), sb("vT", P, 2, 2, P)
        cur_ = [sb(f"cur{e}", P, 2, 5, HEADS) for e in range(2)]
        pre = [sb(f"pre{n}", P, 2, P) for n in range(PRE)]
        kq_ = [sb(f"kq{e}", P, 2, HEADS, 2, P) for e in range(2)]
        sq = [sb(f"sq{n}", P, 4, P) for n in range(2)]
        norm_, rnorm_ = ([sb(f"{n}{e}", P, 2, 2, HEADS) for e in range(2)] for n in ("norm", "rnorm"))
        s__ = [sb(f"s_{e}", P, 2, HEADS) for e in range(2)]
        nv_ = [sb(f"nv{e}", P, 2, 2, 4 * VD) for e in range(2)]
        gm = [sb(f"gm{n}", P, 4, P) for n in range(2)]
        kt_, CT_, PT_, XT_ = ([[sb(f"{n}{e}{q}", P, 4, P) for q in range(QUADS)] for e in range(2)] for n in ("kt", "CT", "PT", "XT"))
        D, X = ([sb(f"{n}{q}", P, 4, P) for q in range(QUADS)] for n in ("D", "X"))
        W = [sb(f"W{q}", P, 4, 64) for q in range(QUADS)]
        S = sb("S", P, QUADS, 4 * VD)
        r, z, wd, o1 = ([sb(f"{n}{q}", P, 4, VD) for q in range(QUADS)] for n in ("r", "z", "wd", "o1"))
        ob, ob_sq = sb("ob", P, QUADS, 4 * VD), sb("ob_sq", P, QUADS, 4 * VD)
        pj, mx, lv = [psum(f"pj{n}") for n in range(2)], [psum(f"mx{n}") for n in range(2)], [psum(f"lv{q}") for q in range(QUADS)]

        reset = signal("reset")
        alone, pe_alone = signal("alone"), signal("pe_alone")
        xh_ready, cur_part, cur_ready = signal("xh_ready"), signal("cur_part"), signal("cur_ready")
        pj_full, tap_done, tap_next, conv_done, silu_done = (
            signal(n, p * BLOCKS) for n, p in (("pj_full", 1), ("tap_done", 1), ("tap_next", 2), ("conv_done", 1), ("silu_done", 1)))
        squared, n2_ready, n_root, n_step = (
            signal(n, p) for n, p in (("squared", 2 * QUADS), ("n2_ready", 2 * QUADS), ("n_root", 1), ("n_step", 4)))
        v_full, nv_ready = signal("v_full"), signal("nv_ready", 2)
        kt_full, kt_ready, qt_full, gm_ready, e_full, d_ready, kq_full, ct_ready, pt_ready, pt_masked, x1_part, x1_ready, x_full, x_ready = (
            signal(n, QUADS) for n in ("kt_full", "kt_ready", "qt_full", "gm_ready", "e_full", "d_ready", "kq_full", "ct_ready", "pt_ready",
                                       "pt_masked", "x1_part", "x1_ready", "x_full", "x_ready"))
        half_ready = signal("half_ready")
        w_full, w_ready, dx_full, dx_added, t_full, xt_ready = (
            signal(n, NL_ * QUADS) for n in ("w_full", "w_ready", "dx_full", "dx_added", "t_full", "xt_ready"))
        s_full, rg_ready, r_ready, qs_ready, z_full, z_ready, wd_ready, sg_ready, pw_full, o_sum, s_done, o_done = (
            signal(n, QUADS) for n in ("s_full", "rg_ready", "r_ready", "qs_ready", "z_full", "z_ready", "wd_ready", "sg_ready", "pw_full",
                                       "o_sum", "s_done", "o_done"))
        stored, o_squared, o_summed = signal("stored", 32), signal("o_squared"), signal("o_summed")

        def flat(ap):
            return ap.rearrange("p a b -> p (a b)")

        def halves(ap, s, which):
            return ap.rearrange("p h (b t s) -> p h b t s", t=2, s=s)[:, :, :, which, :]

        def quad(q):
            return q // 2, slice(4 * (q % 2), 4 * (q % 2) + 4)

        def run(eng, front, back):
            def beside(n, e):
                for slot in range(SLOTS):
                    back(n, e, slot)
                    front(n + 1, 1 - e, slot)
            for slot in range(SLOTS):
                front(0, 0, slot)
            beside(0, 0)
            with eng.Fori(0, (PASSES - 2) // 2) as two:
                beside(two * 2 + 1, 1)
                beside(two * 2 + 2, 0)
            for slot in range(SLOTS):
                back(PASSES - 1, 1, slot)

        o_rows = o_dram.rearrange("(b c p) v -> p b c v", p=P, c=TPB)
        block = ctx.enter_context(nc.Block())

        @block.sync
        def _(sp):
            with sp.Fori(0, PASSES // TPB) as pair, sp.Fori(0, TPB) as chunk:
                sp.wait_ge(o_done.sem, o_done.at(pair * TPB + chunk, QUADS))
                for i in range(2):
                    sp.dma_start(o_rows[:, bass.ds(pair * 2 + i, 1), bass.ds(chunk, 1), :].rearrange("p b c v -> p (b c v)"),
                                 flat(ob[:, 2 * i:2 * i + 2, :])).then_inc(stored.sem, 16)
            if stored.due(PASSES, 0):
                sp.wait_ge(stored.sem, stored.at(PASSES, 0))

        @block.gpsimd
        def _(pool):
            pool.wait_ge(masked.sem, 2 * NL_ + 1)

            def front(m, e, slot):
                cur, CT, PT, XT = cur_[e], CT_[e], PT_[e], XT_[e]

                def build(q):
                    i, hs = quad(q)
                    if e_full.due(m - 1 if q < 2 else m, q + 3 if q < 2 else q - 1):
                        pool.wait_ge(e_full.sem, e_full.at(m - 1 if q < 2 else m, q + 3 if q < 2 else q - 1))
                    pool.tensor_tensor(gm[q % 2][:, :, :], wide(k["upto"][:, :], 1, [P, 4, P]), wide(cur[:, i, G_, hs], 2, [P, 4, P]),
                                       ALU.mult).then_inc(gm_ready.sem, 1)
                if slot == 0:
                    pool.wait_ge(cur_ready.sem, cur_ready.at(m, 1))
                    build(0)
                    build(1)
                for q in range(QUADS):
                    if slot == KQ_AT[q]:
                        if q + 2 < QUADS:
                            build(q + 2)
                        pool.wait_ge(ct_ready.sem, ct_ready.at(m, q + 1))
                        if z_full.due(m - 2, QUADS):
                            pool.wait_ge(z_full.sem, z_full.at(m - 2, QUADS))
                        pool.tensor_tensor(XT[q][:, :, :], CT[q][:, :, :], wide(mask1[:, :], 1, [P, 4, P]), ALU.mult).then_inc(x1_part.sem, 1)
                        pool.wait_ge(x1_part.sem, x1_part.at(m, q + 1))
                        pool.tensor_tensor(XT[q][:, :, :], XT[q][:, :, :], wide(k["ident"][:, :], 1, [P, 4, P]), ALU.add).then_inc(x1_ready.sem, 1)
                        pool.wait_ge(pt_ready.sem, pt_ready.at(m, q + 1))
                        pool.tensor_tensor(PT[q][:, :, :], PT[q][:, :, :], wide(k["upto"][:, :], 1, [P, 4, P]), ALU.mult).then_inc(pt_masked.sem, 1)

            def back(n, e, slot):
                pass
            run(pool, front, back)

        @block.scalar
        def _(act):
            act.wait_ge(chunk_loaded.sem, 96)

            def tokens(m):
                if pj_full.due(m - 1, BLOCKS):
                    act.wait_ge(pj_full.sem, pj_full.at(m - 1, BLOCKS))
                act.activation(xh[:, :, :], xT[:, bass.ds((m // TPB) * 2, 2), bass.ds((m % TPB) * P, W_EXT)], ACT.Copy).then_inc(xh_ready.sem, 1)

            def front(m, e, slot):
                kq, norm, kt = kq_[e], norm_[e], kt_[e]

                def silu(b):
                    act.wait_ge(conv_done.sem, conv_done.at(m, b + 1))
                    if b == 0:
                        if s_full.due(m - 2, QUADS):
                            act.wait_ge(s_full.sem, s_full.at(m - 2, QUADS))
                    if b == 2 * HEADS:
                        if v_full.due(m - 1, 1):
                            act.wait_ge(v_full.sem, v_full.at(m - 1, 1))
                    act.activation(kq[:, :, b % HEADS, b // HEADS, :] if b < 2 * HEADS else vT[:, :, b - 2 * HEADS, :],
                                   pre[b % PRE][:, :, :], ACT.Silu).then_inc(silu_done.sem, 1)
                if slot < PAIRS_:
                    for b in (2 * slot, 2 * slot + 1):
                        act.wait_ge(pj_full.sem, pj_full.at(m, b + 1))
                        if silu_done.due(m - 1 if b < PRE else m, BLOCKS if b < PRE else b - PRE + 1):
                            act.wait_ge(silu_done.sem, silu_done.at(m - 1 if b < PRE else m, BLOCKS if b < PRE else b - PRE + 1))
                        act.activation(pre[b % PRE][:, :, :], pj[b % 2][:, 0:2 * W_EXT].rearrange("p (i t) -> p i t", i=2)[:, :, 0:P],
                                       ACT.Copy, scale=taps[:, b, 0:1]).then_inc(tap_done.sem, 1)
                if 0 < slot <= PAIRS_:
                    silu(2 * slot - 2)
                    silu(2 * slot - 1)
                def square(u, bank):
                    if n2_ready.due(m - 1 if u < 2 else m, 2 * QUADS - 1 + u if u < 2 else u - 1):
                        act.wait_ge(n2_ready.sem, n2_ready.at(m - 1 if u < 2 else m, 2 * QUADS - 1 + u if u < 2 else u - 1))
                    act.activation(flat(sq[u % 2][:, :, :]), bank[:, :], ACT.Square).then_inc(squared.sem, 1)

                if slot == E_AT[0]:
                    act.wait_ge(n2_ready.sem, n2_ready.at(m, 2 * QUADS))
                    act.activation(norm[:, :, :, :], norm[:, :, :, :], ACT.Sqrt).then_inc(n_root.sem, 1)
                for u, q in enumerate(ORDER):
                    if slot == K_T + u:
                        act.wait_ge(kt_full.sem, kt_full.at(m, u + 1))
                        if pw_full.due(m - 2, QUADS):
                            act.wait_ge(pw_full.sem, pw_full.at(m - 2, QUADS))
                        act.activation(flat(kt[q][:, :, :]), mx[1][:, :], ACT.Copy).then_inc(kt_ready.sem, 1)
                        square(u, mx[1])
                    if slot == Q_T + u:
                        act.wait_ge(qt_full.sem, qt_full.at(m, u + 1))
                        square(QUADS + u, mx[0])
                for q in range(QUADS):
                    if slot == E_AT[q]:
                        act.wait_ge(e_full.sem, e_full.at(m, q + 1))
                        if pt_ready.due(m - 1, q + 1):
                            act.wait_ge(pt_ready.sem, pt_ready.at(m - 1, q + 1))
                        act.activation(flat(D[q][:, :, :]), mx[0][:, :], ACT.Exp).then_inc(d_ready.sem, 1)

            def square_output(n):
                act.wait_ge(o_done.sem, o_done.at(n, QUADS))
                if o_summed.due(n - 1, 1):
                    act.wait_ge(o_summed.sem, o_summed.at(n - 1, 1))
                act.activation(flat(ob_sq[:, :, :]), flat(ob[:, :, :]), ACT.Square).then_inc(o_squared.sem, 1)

            def back(n, e, slot):
                if slot == 2 and o_done.due(n - 1, QUADS):
                    square_output(n - 1)
                if slot == 0 and not (isinstance(n, int) and n == PASSES - 1):
                    tokens(n + 1)
                for q in range(QUADS):
                    if slot == 0:
                        act.wait_ge(x_full.sem, x_full.at(n, q + 1))
                        act.activation(flat(X[q][:, :, :]), lv[q][:, :], ACT.Copy).then_inc(x_ready.sem, 1)
                    elif slot < STATE and slot % 3 == 0:
                        if t_full.due(n, QUADS * (slot // 3 - 1) + q + 1):
                            act.wait_ge(t_full.sem, t_full.at(n, QUADS * (slot // 3 - 1) + q + 1))
                        l = slot // 3
                        low = P - rows(l) if l < NL_ else 0
                        act.activation(XT_[e][q][0:P - low, :, low:P], lv[q][0:P - low, :].rearrange("p (h t) -> p h t", h=4)[:, :, low:P],
                                       ACT.Copy).then_inc(xt_ready.sem, 1)
            tokens(0)
            run(act, front, back)
            square_output(PASSES - 1)

        @block.vector
        def _(dve):
            dve.wait_ge(masked.sem, 2 * NL_ + 1)
            dve.memset(S[:, :, :], 0.0).then_inc(reset.sem, 1)
            dve.wait_ge(reset.sem, reset.at(0, 1))
            dve.wait_ge(chunk_loaded.sem, 96)

            def front(m, e, slot):
                cur, norm, rnorm, s_, nv, CT, PT = cur_[e], norm_[e], rnorm_[e], s__[e], nv_[e], CT_[e], PT_[e]
                if slot == 0:
                    if o_done.due(m - 2, QUADS):
                        dve.wait_ge(o_done.sem, o_done.at(m - 2, QUADS))
                    if s_done.due(m - 2, QUADS):
                        dve.wait_ge(s_done.sem, s_done.at(m - 2, QUADS))
                    dve.sem_inc(alone.sem, 1)
                    for i in range(2):
                        dve.tensor_copy(cur[:, i, :, :].rearrange("p a b -> p (a b)"),
                                        prm[:, :, :, :].rearrange("p t a b -> p t (a b)")[:, bass.ds((m // TPB) * (2 * TPB) + m % TPB + i * TPB, 1), :].rearrange("p t a -> p (t a)")).then_inc(
                            cur_part.sem if i == 0 else cur_ready.sem, 1)
                if slot < PAIRS_:
                    for t in range(1, TAPS):
                        for b in (2 * slot, 2 * slot + 1):
                            if t == 1:
                                dve.wait_ge(tap_done.sem, tap_done.at(m, b + 1))
                            else:
                                if tap_next.due(m, 4 * slot + 2 * (t - 2) + b % 2 + 1):
                                    dve.wait_ge(tap_next.sem, tap_next.at(m, 4 * slot + 2 * (t - 2) + b % 2 + 1))
                            src = pj[b % 2][:, 0:2 * W_EXT].rearrange("p (i t) -> p i t", i=2)
                            dve.scalar_tensor_tensor(pre[b % PRE][:, :, :], src[:, :, t:t + P], taps[:, b, t:t + 1], pre[b % PRE][:, :, :],
                                                     ALU.mult, ALU.add).then_inc((conv_done if t == TAPS - 1 else tap_next).sem, 1)
                for u, q in enumerate(ORDER * 2):
                    if slot == K_T + 1 + u:
                        i, hs = quad(q)
                        dve.wait_ge(squared.sem, squared.at(m, u + 1))
                        dve.tensor_reduce(norm[:, u // QUADS, i, hs], sq[u % 2][:, :, :], AX.X, ALU.add).then_inc(n2_ready.sem, 1)
                if slot == KQ_AT[0]:
                    dve.wait_ge(n_root.sem, n_root.at(m, 1))
                    dve.tensor_scalar(norm[:, :, :, :], norm[:, :, :, :], EPS_NORM, None, ALU.max).then_inc(n_step.sem, 1)
                    dve.wait_ge(n_step.sem, n_step.at(m, 1))
                    dve.reciprocal(rnorm[:, :, :, :], norm[:, :, :, :]).then_inc(n_step.sem, 1)
                    dve.wait_ge(v_full.sem, v_full.at(m, 1))
                    for i in range(2):
                        dve.tensor_tensor(nv[:, i, :, :].rearrange("p a (h d) -> p (a h) d", d=VD), mx[1][:, 256 * i:256 * i + 256].rearrange("p (h d) -> p h d", d=VD),
                                          wide(norm[:, 0, i, :], 2, [P, HEADS, VD]), ALU.mult).then_inc(nv_ready.sem, 1)
                    dve.wait_ge(n_step.sem, n_step.at(m, 2))
                    dve.tensor_tensor(s_[:, :, :], rnorm[:, 0, :, :], rnorm[:, 0, :, :], ALU.mult).then_inc(n_step.sem, 1)
                    dve.wait_ge(n_step.sem, n_step.at(m, 3))
                    dve.tensor_tensor(s_[:, :, :], s_[:, :, :], cur[:, :, BETA, :], ALU.mult).then_inc(n_step.sem, 1)
                for q in range(QUADS):
                    i, hs = quad(q)
                    if slot == KQ_AT[q]:
                        dve.wait_ge(n_step.sem, n_step.at(m, 4))
                        dve.wait_ge(d_ready.sem, d_ready.at(m, q + 1))
                        dve.wait_ge(kq_full.sem, kq_full.at(m, q + 1))
                        both = [pj[g][:, :].rearrange("p (h m t) -> p h m t", h=2, m=2) for g in range(2)]
                        for h in range(4):
                            dve.scalar_tensor_tensor(CT[q][:, h, :], both[h // 2][:, h % 2, 0, :], s_[:, i, hs][:, h:h + 1], D[q][:, h, :],
                                                     ALU.mult, ALU.mult).then_inc((ct_ready if h == 3 else half_ready).sem, 1)
                        for g in range(2):
                            sl = slice(2 * g, 2 * g + 2)
                            dve.tensor_tensor(PT[q][:, sl, :], both[g][:, :, 1, :], D[q][:, sl, :], ALU.mult).then_inc((pt_ready if g else half_ready).sem, 1)

            def sum_squares(n):
                dve.wait_ge(o_squared.sem, o_squared.at(n, 1))
                dve.sem_inc(alone.sem, 1)
                dve.tensor_reduce(squares[:, bass.ds(n, 1), :, :].rearrange("p n i h -> p (n i h)"),
                                  flat(ob_sq[:, :, :]).rearrange("p (h d) -> p h d", d=VD), AX.X, ALU.add).then_inc(o_summed.sem, 1)

            def back(n, e, slot):
                if slot == 3 and o_done.due(n - 1, QUADS):
                    sum_squares(n - 1)
                cur, rnorm, s_, nv = cur_[e], rnorm_[e], s__[e], nv_[e]
                if 0 < slot < STATE and slot % 3 != 0:
                    l = slot // 3
                    s = LEVELS[l]
                    for q in range(QUADS):
                        if slot % 3 == 1:
                            dve.wait_ge(w_full.sem, w_full.at(n, QUADS * l + q + 1))
                            part = rows(l)
                            dve.tensor_tensor(W[q][0:part, :, :], lv[q][0:part, 0:256].rearrange("p (h c) -> p h c", h=4),
                                              wide(masks[l][0:part, :], 1, [part, 4, 64]), ALU.mult).then_inc(w_ready.sem, 1)
                        else:
                            dve.wait_ge(dx_full.sem, dx_full.at(n, QUADS * l + q + 1))
                            low = P - rows(l)
                            v = halves(X[q][low:, :, :], s, 0)
                            dve.tensor_tensor(v, v, lv[q][low:, 256:512].rearrange("p (h b s) -> p h b s", h=4, s=s), ALU.add).then_inc(dx_added.sem, 1)
                if slot == STATE:
                    if o_done.due(n - 1, QUADS):
                        dve.wait_ge(o_done.sem, o_done.at(n - 1, QUADS))
                    if s_done.due(n - 1, QUADS):
                        dve.wait_ge(s_done.sem, s_done.at(n - 1, QUADS))
                if slot == PW_AT[0]:
                    if stored.due(n - 1, 32):
                        dve.wait_ge(stored.sem, stored.at(n - 1, 32))
                        dve.wait_ge(o_squared.sem, o_squared.at(n - 1, 1))
                for q in range(QUADS):
                    i, hs = quad(q)

                    def per_token(ap):
                        return wide(ap, 2, [P, 4, VD])

                    def per_head(ap):
                        return ap.rearrange("p (h d) -> p h d", d=VD)

                    if slot == S_AT[q]:
                        dve.wait_ge(s_full.sem, s_full.at(n, q + 1))
                        dve.tensor_tensor(r[q][:, :, :], per_head(lv[q][:, 0:P]), per_token(cur[:, i, GAMMA, hs]), ALU.mult).then_inc(rg_ready.sem, 1)
                        dve.tensor_tensor(o1[q][:, :, :], per_head(lv[q][:, P:2 * P]), per_token(cur[:, i, GAMMA, hs]), ALU.mult).then_inc(qs_ready.sem, 1)
                        dve.wait_ge(rg_ready.sem, rg_ready.at(n, q + 1))
                        dve.tensor_tensor(r[q][:, :, :], per_head(nv[:, i, q % 2, :]), r[q][:, :, :], ALU.subtract).then_inc(r_ready.sem, 1)
                    if slot == Z_AT[q]:
                        dve.wait_ge(z_full.sem, z_full.at(n, q + 1))
                        dve.tensor_tensor(z[q][:, :, :], per_head(lv[q][:, 0:P]), per_token(s_[:, i, hs]), ALU.mult).then_inc(z_ready.sem, 1)
                        dve.tensor_tensor(per_head(S[:, q, :]), per_head(S[:, q, :]), per_token(cur[:, i, GAMMA_END, hs]), ALU.mult).then_inc(sg_ready.sem, 1)
                        dve.wait_ge(z_ready.sem, z_ready.at(n, q + 1))
                        dve.tensor_tensor(wd[q][:, :, :], z[q][:, :, :], per_token(cur[:, i, DECAY_END, hs]), ALU.mult).then_inc(wd_ready.sem, 1)
                    if slot == PW_AT[q]:
                        dve.wait_ge(pw_full.sem, pw_full.at(n, q + 1))
                        dve.wait_ge(sg_ready.sem, sg_ready.at(n, q + 1))
                        dve.wait_ge(qs_ready.sem, qs_ready.at(n, q + 1))
                        dve.tensor_tensor(o1[q][:, :, :], o1[q][:, :, :], per_head(lv[q][:, P:2 * P]), ALU.add).then_inc(o_sum.sem, 1)
                        dve.tensor_tensor(S[:, q, :], S[:, q, :], lv[q][:, 2 * P:3 * P], ALU.add).then_inc(s_done.sem, 1)
                        dve.wait_ge(o_sum.sem, o_sum.at(n, q + 1))
                        dve.tensor_tensor(per_head(ob[:, q, :]), o1[q][:, :, :], per_token(rnorm[:, 1, i, hs]), ALU.mult).then_inc(o_done.sem, 1)
            run(dve, front, back)
            sum_squares(PASSES - 1)

        @block.tensor
        def _(pe):
            pe.wait_ge(chunk_loaded.sem, 96)
            pe.wait_ge(reset.sem, reset.at(0, 1))

            def front(m, e, slot):
                kq = kq_[e]

                def weights(b):
                    src = wk if b < HEADS else wq if b < 2 * HEADS else wv
                    return src[:, (b % HEADS) * P:(b % HEADS) * P + P]

                if slot == 0:
                    pe.wait_ge(xh_ready.sem, xh_ready.at(m, 1))
                    if pt_ready.due(m - 1, QUADS):
                        pe.wait_ge(pt_ready.sem, pt_ready.at(m - 1, QUADS))
                if slot < PAIRS_:
                    for b in (2 * slot, 2 * slot + 1):
                        if b >= 2:
                            if conv_done.due(m, b - 1):
                                pe.wait_ge(conv_done.sem, conv_done.at(m, b - 1))
                        pe.matmul(pj[b % 2][:, 0:2 * W_EXT], weights(b), flat(xh[:, :, :]), start=True, stop=True).then_inc(pj_full.sem, 1)
                if slot == V_T:
                    pe.wait_ge(silu_done.sem, silu_done.at(m, BLOCKS))
                    pe.wait_ge(squared.sem, squared.at(m, QUADS))
                    for i in range(2):
                        for hq in range(2):
                            mm = pe.transpose(mx[1][:, 256 * i + P * hq:256 * i + P * hq + P], vT[:, i, hq, :], k["ident"][:, :])
                    mm.then_inc(v_full.sem, 1)
                for u, q in enumerate(ORDER):
                    i, hq = q // 2, q % 2
                    if slot == K_T + u:
                        pe.wait_ge(silu_done.sem, silu_done.at(m, 4 * hq + 4))
                        if u == 0:
                            if nv_ready.due(m - 1, 2):
                                pe.wait_ge(nv_ready.sem, nv_ready.at(m - 1, 2))
                        else:
                            pe.wait_ge(squared.sem, squared.at(m, u))
                        for h in range(4):
                            mm = pe.transpose(mx[1][:, P * h:P * h + P], kq[:, i, 4 * hq + h, 0, :], k["ident"][:, :])
                        mm.then_inc(kt_full.sem, 1)
                    if slot == Q_T + u:
                        pe.wait_ge(silu_done.sem, silu_done.at(m, HEADS + 4 * hq + 4))
                        if u == 0:
                            if d_ready.due(m - 1, QUADS):
                                pe.wait_ge(d_ready.sem, d_ready.at(m - 1, QUADS))
                        else:
                            pe.wait_ge(squared.sem, squared.at(m, QUADS + u))
                        for h in range(4):
                            mm = pe.transpose(mx[0][:, P * h:P * h + P], kq[:, i, 4 * hq + h, 1, :], k["ident"][:, :])
                        mm.then_inc(qt_full.sem, 1)
                for q in range(QUADS):
                    i, hq = q // 2, q % 2
                    if slot == E_AT[q]:
                        pe.wait_ge(gm_ready.sem, gm_ready.at(m, q + 1))
                        if q:
                            pe.wait_ge(d_ready.sem, d_ready.at(m, q))
                        else:
                            pe.wait_ge(squared.sem, squared.at(m, 2 * QUADS))
                        pe.matmul(mx[0][:, :], k["after"][:, :], flat(gm[q % 2][:, :, :]), start=True, stop=True).then_inc(e_full.sem, 1)
                    if slot == KQ_AT[q]:
                        if q:
                            pe.wait_ge(pt_ready.sem, pt_ready.at(m, q))
                        else:
                            pe.wait_ge(conv_done.sem, conv_done.at(m, BLOCKS))
                        for h in range(4):
                            mm = pe.matmul(pj[h // 2][:, 256 * (h % 2):256 * (h % 2) + 256], kq[:, i, 4 * hq + h, 0, :],
                                           kq[:, i, 4 * hq + h, :, :].rearrange("p m t -> p (m t)"), start=True, stop=True)
                        mm.then_inc(kq_full.sem, 1)

            def back(n, e, slot):
                kq, kt, CT, PT, XT = kq_[e], kt_[e], CT_[e], PT_[e], XT_[e]
                l = (slot - 1) // 3
                for q in range(QUADS):
                    i, hq = q // 2, q % 2
                    if slot == 0:
                        pe.wait_ge(x1_ready.sem, x1_ready.at(n, q + 1))
                        if o_done.due(n - 1, q + 1):
                            pe.wait_ge(o_done.sem, o_done.at(n - 1, q + 1))
                        if s_done.due(n - 1, q + 1):
                            pe.wait_ge(s_done.sem, s_done.at(n - 1, q + 1))
                        for h in range(4):
                            mm = pe.transpose(lv[q][:, P * h:P * h + P], XT[q][:, h, :], k["ident"][:, :])
                        mm.then_inc(x_full.sem, 1)
                    elif slot < STATE and slot % 3 == 1:
                        pe.wait_ge(x_ready.sem, x_ready.at(n, q + 1))
                        if l:
                            if xt_ready.due(n, QUADS * (l - 1) + q + 1):
                                pe.wait_ge(xt_ready.sem, xt_ready.at(n, QUADS * (l - 1) + q + 1))
                        for h in range(4):
                            mm = pe.matmul(lv[q][0:rows(l), 64 * h:64 * h + 64], CT[q][:, h, P - rows(l):P], halves(X[q][:, :, :], LEVELS[l], 0)[:, h], start=True, stop=True)
                        mm.then_inc(w_full.sem, 1)
                    elif slot < STATE and slot % 3 == 2:
                        pe.wait_ge(w_ready.sem, w_ready.at(n, QUADS * l + q + 1))
                        if l == NL_ - 1:
                            pe.sem_inc(pe_alone.sem, 1)
                        for h in range(4):
                            mm = pe.matmul(lv[q][P - rows(l):P, 256 + 64 * h:256 + 64 * h + 64], XT[q][0:rows(l), h, P - rows(l):P], W[q][0:rows(l), h, :], start=True, stop=True)
                        mm.then_inc(dx_full.sem, 1)
                    elif slot < STATE:
                        pe.wait_ge(dx_added.sem, dx_added.at(n, QUADS * l + q + 1))
                        pe.sem_inc(pe_alone.sem, 1)
                        for h in range(4):
                            low = P - rows(l + 1) if l + 1 < NL_ else 0
                            mm = pe.transpose(lv[q][0:P - low, P * h + low:P * h + P], X[q][low:P, h, low:P], k["ident"][low:P, low:P])
                        mm.then_inc(t_full.sem, 1)
                    elif slot == S_AT[q]:
                        if xt_ready.due(n, QUADS * (NL_ - 1) + q + 1):
                            pe.wait_ge(xt_ready.sem, xt_ready.at(n, QUADS * (NL_ - 1) + q + 1))
                        for part in range(2):
                            for h in range(4):
                                mm = pe.matmul(lv[q][:, P * part + VD * h:P * part + VD * h + VD], kq[:, i, 4 * hq + h, part, :], S[:, q, VD * h:VD * h + VD], start=True, stop=True)
                        mm.then_inc(s_full.sem, 1)
                    elif slot == Z_AT[q]:
                        pe.wait_ge(r_ready.sem, r_ready.at(n, q + 1))
                        for h in range(4):
                            mm = pe.matmul(lv[q][:, VD * h:VD * h + VD], XT[q][:, h, :], r[q][:, h, :], start=True, stop=True)
                        mm.then_inc(z_full.sem, 1)
                    elif slot == PW_AT[q]:
                        pe.wait_ge(wd_ready.sem, wd_ready.at(n, q + 1))
                        pe.wait_ge(pt_masked.sem, pt_masked.at(n, q + 1))
                        for h in range(4):
                            pe.matmul(lv[q][:, P + VD * h:P + VD * h + VD], PT[q][:, h, :], z[q][:, h, :], start=True, stop=True)
                            mm = pe.matmul(lv[q][:, 2 * P + VD * h:2 * P + VD * h + VD], kt[q][:, h, :], wd[q][:, h, :], start=True, stop=True)
                        mm.then_inc(pw_full.sem, 1)
            run(pe, front, back)


def delta_output(nc, k, x_sb, w, xT, o_dram, c, output_loaded):
    with ExitStack() as ctx:
        def sb(n, *shape, dt=F32):
            return ctx.enter_context(nc.sbuf_tensor("b2_" + n, list(shape), dt))

        def psum(n, width):
            return ctx.enter_context(nc.psum_tensor("b2_" + n, [P, width], F32))

        def signal(n, per=1):
            return Signal(nc.alloc_semaphore("b2_" + n), per)

        G, V = 4, HEADS * VD
        PASSES = TILES // G
        wg, wo, nw, squares = c["wg"], c["wo"], c["nw"], c["squares"]
        o = [sb(f"o{e}", P, G * V) for e in range(2)]
        xs, gate, gated_o = ([sb(f"{n}{e}", P, width) for e in range(2)] for n, width in (("xs", G * P), ("gate", G * V), ("gated_o", G * V)))
        ms = sb("ms", P, TILES * HEADS)
        oT = [sb(f"oT{e}", P, G, 2, P) for e in range(2)]
        gp, tp, xp = [psum(f"gp{e}", 1024) for e in range(2)], psum("tp", 1024), [psum(f"xp{e}", 512) for e in range(2)]
        o_in = [signal(f"o_in{e}") for e in range(2)]
        wo_ready, ms_step, rooted = (signal(n) for n in ("wo_ready", "ms_step", "rooted"))
        xs_ready, g_full, gated, scaled, o_ready, oT_full, oT_read, p_full, x_done = (
            signal(n) for n in ("xs_ready", "g_full", "gated", "scaled", "o_ready", "oT_full", "oT_read", "p_full", "x_done"))
        alone = signal("alone")
        o_rows = o_dram.rearrange("(g t p) v -> g p t v", p=P, t=G)
        block = ctx.enter_context(nc.Block())

        def loop(eng, step):
            step(-1, 1, back=False)
            step(0, 0)
            with eng.Fori(0, (PASSES - 2) // 2) as two:
                step(two * 2 + 1, 1)
                step(two * 2 + 2, 0)
            step(PASSES - 1, 1, front=False)

        @block.sync
        def _(sp):
            for n in range(PASSES):
                if scaled.due(n - 2, 1):
                    sp.wait_ge(scaled.sem, scaled.at(n - 2, 1))
                sp.dma_start(o[n % 2][:, :].rearrange("p (t v) -> p t v", v=V), o_rows[n]).then_inc(o_in[n % 2].sem, 16)

        @block.scalar
        def _(act):
            act.wait_ge(ms_step.sem, 2)
            act.activation(ms[:, :], ms[:, :], ACT.Sqrt).then_inc(rooted.sem, 1)

            def step(n, e, back=True, front=True):
                f = 1 - e
                if front:
                    if g_full.due(n - 1, 1):
                        act.wait_ge(g_full.sem, g_full.at(n - 1, 1))
                    tokens = xT[:, :, TAPS - 1:].rearrange("p b (s t) -> p b s t", t=G * P)
                    m = n + 1
                    act.activation(xs[f][:, :], tokens[:, bass.ds(m // 2, 1), bass.ds(m % 2, 1), :].rearrange("p b s t -> p (b s t)"), ACT.Copy).then_inc(xs_ready.sem, 1)
                if back:
                    act.wait_ge(oT_full.sem, oT_full.at(n, 1))
                    if p_full.due(n - 2, 1):
                        act.wait_ge(p_full.sem, p_full.at(n - 2, 1))
                    act.activation(oT[e][:, :, :, :].rearrange("p a b c -> p (a b c)"), tp[:, :], ACT.Copy).then_inc(oT_read.sem, 1)
                if front:
                    act.wait_ge(g_full.sem, g_full.at(n + 1, 1))
                    if o_ready.due(n - 1, 1):
                        act.wait_ge(o_ready.sem, o_ready.at(n - 1, 1))
                    act.activation(gate[f][:, :], gp[f][:, :], ACT.Silu).then_inc(gated.sem, 1)
            loop(act, step)

        @block.vector
        def _(dve):
            for pair in range(BATCHES // 2):
                dve.tensor_scalar(ms[:, pair * 2 * TPB * HEADS:(pair + 1) * 2 * TPB * HEADS].rearrange("p (i c h) -> p i c h", i=2, h=HEADS),
                                  squares[:, pair * TPB:(pair + 1) * TPB, :, :].rearrange("p c i h -> p i c h"),
                                  1.0 / VD, EPS_RMS, ALU.mult, ALU.add).then_inc(ms_step.sem, 1)
            dve.wait_ge(output_loaded.sem, 16 * (2 + P // VD))
            dve.tensor_scalar(wo[:, :, :], wo[:, :, :], nw[:, 0:1], None, ALU.mult).then_inc(wo_ready.sem, 1)
            dve.wait_ge(rooted.sem, 1)
            dve.reciprocal(ms[:, :], ms[:, :]).then_inc(ms_step.sem, 1)
            dve.wait_ge(ms_step.sem, 3)

            def step(n, e, back=True, front=True):
                f = 1 - e
                if front:
                    m = n + 1
                    if oT_full.due(n - 1, 1):
                        dve.wait_ge(oT_full.sem, oT_full.at(n - 1, 1))
                    dve.wait_ge(o_in[f].sem, (m - f) * 8 + 16)
                    dve.sem_inc(alone.sem, 1)
                    dve.tensor_tensor(gated_o[f][:, :].rearrange("p (h d) -> p h d", d=VD), o[f][:, :].rearrange("p (h d) -> p h d", d=VD),
                                      wide(ms[:, bass.ds(m * (G * HEADS), G * HEADS)], 2, [P, G * HEADS, VD]), ALU.mult).then_inc(scaled.sem, 1)
                    dve.wait_ge(gated.sem, gated.at(n + 1, 1))
                    dve.wait_ge(scaled.sem, scaled.at(n + 1, 1))
                    dve.tensor_tensor(gated_o[f][:, :], gated_o[f][:, :], gate[f][:, :], ALU.mult).then_inc(o_ready.sem, 1)
                if back:
                    dve.wait_ge(p_full.sem, p_full.at(n, 1))
                    dve.sem_inc(alone.sem, 1)
                    x = x_sb[:, bass.ds(n * (G * C), G * C)]
                    dve.tensor_tensor(x, x, xp[e][:, :], ALU.add).then_inc(x_done.sem, 1)
            loop(dve, step)
            if x_done.due(PASSES, 0):
                dve.wait_ge(x_done.sem, x_done.at(PASSES, 0))

        @block.tensor
        def _(pe):
            pe.wait_ge(output_loaded.sem, 16 * (2 + P // VD))
            pe.wait_ge(wo_ready.sem, wo_ready.at(0, 1))

            def step(n, e, back=True, front=True):
                f = 1 - e
                if front:
                    pe.wait_ge(xs_ready.sem, xs_ready.at(n + 1, 1))
                    if gated.due(n - 1, 1):
                        pe.wait_ge(gated.sem, gated.at(n - 1, 1))
                    for j in range(G):
                        mm = pe.matmul(gp[f][:, V * j:V * j + V], xs[f][:, P * j:P * j + P], wg[:, :], start=True, stop=True)
                    mm.then_inc(g_full.sem, 1)
                if back:
                    pe.wait_ge(o_ready.sem, o_ready.at(n, 1))
                    if oT_read.due(n - 1, 1):
                        pe.wait_ge(oT_read.sem, oT_read.at(n - 1, 1))
                    for j in range(G):
                        for hq in range(2):
                            mm = pe.transpose(tp[:, P * (2 * j + hq):P * (2 * j + hq) + P], gated_o[e][:, V * j + P * hq:V * j + P * hq + P], k["ident"][:, :])
                    mm.then_inc(oT_full.sem, 1)
                    pe.wait_ge(oT_read.sem, oT_read.at(n, 1))
                    if x_done.due(n - 2, 1):
                        pe.wait_ge(x_done.sem, x_done.at(n - 2, 1))
                    for j in range(G):
                        for hq in range(2):
                            mm = pe.matmul(xp[e][:, C * j:C * j + C], oT[e][:, j, hq, :], wo[:, hq, :], start=(hq == 0), stop=(hq == 1))
                    mm.then_inc(p_full.sem, 1)
            loop(pe, step)


B_WEIGHTS = ["Wq", "Wk", "Wv", "Wa", "Wb", "Wg", "Wo", "A_log", "dt_bias", "conv_q", "conv_k", "conv_v", "o_norm_w"]
INPUTS = ["L0_attn_a_x", "L0_attn_a_W_attn", "L0_attn_a_W_proj", *("L0_attn_b_" + n for n in B_WEIGHTS),
          "L0_ffn_Wr", "L0_ffn_Wg", "L0_ffn_Wu", "L0_ffn_Wd"]


def hybrid_layer(nc, dram, out):
    with ExitStack() as ctx:
        x_sb = ctx.enter_context(nc.sbuf_tensor("x_sb", [P, TILES * C], F32))
        x_out = ctx.enter_context(nc.semaphore("x_out"))
        xn_dram = nc.dram_tensor("xn_rows", (TOKENS, C), F32).ap()
        y_dram = nc.dram_tensor("y_rows", (TOP_K * TOKENS + SLOT_TILES * P, C), F32).ap()
        o_dram = nc.dram_tensor("o_rows", (TOKENS, HEADS * VD), F32).ap()
        tiles = x_sb[:, :].rearrange("p (n c) -> p n c", c=C)
        k = make_constants(nc, ctx, tiles, dram["L0_attn_a_x"].rearrange("b (n p) c -> p (b n) c", p=P))
        ffn = [dram["L0_ffn_" + n] for n in ("Wr", "Wg", "Wu", "Wd")]
        with nc.cleanup_on_exit():
            nystrom_attention(nc, k, x_sb, dram["L0_attn_a_W_attn"], dram["L0_attn_a_W_proj"])
        with nc.cleanup_on_exit():
            mixture_of_experts(nc, k, x_sb, *ffn, xn_dram, y_dram, "m1_")
        with nc.cleanup_on_exit():
            delta_attention(nc, k, x_sb, {n: dram["L0_attn_b_" + n] for n in B_WEIGHTS}, o_dram)
        with nc.cleanup_on_exit():
            mixture_of_experts(nc, k, x_sb, *ffn, xn_dram, y_dram, "m2_")
        with nc.Block() as block:
            @block.sync
            def _(sp):
                sp.dma_start(out.rearrange("b (n p) c -> p (b n) c", p=P), tiles).then_inc(x_out, 16)
                sp.wait_ge(x_out, 16)


def kernel(**inputs):
    import numpy as np
    import concourse.bacc as bacc
    from concourse.bass_utils import run_bass_kernel_spmd

    nc = bacc.Bacc("TRN2", target_bir_lowering=False, num_devices=1)
    arrays, dram = {}, {}
    for name in INPUTS:
        arrays[name] = np.ascontiguousarray(inputs[name])
        dram[name] = nc.dram_tensor(name, arrays[name].shape, mybir.dt.from_np(arrays[name].dtype), kind="ExternalInput").ap()
    out = nc.dram_tensor("out", (BATCHES, T, C), F32, kind="ExternalOutput").ap()
    hybrid_layer(nc, dram, out)
    return run_bass_kernel_spmd(nc, [arrays], core_ids=[0]).results[0]["out"]
```
